# Optimizing a Trainium2 kernel written in Bass

```python
import numpy as np
import jax
import jax.numpy as jnp

def _softmax(x, axis=-1):
    return jax.nn.softmax(x, axis=axis)

def _gelu(x):
    return jax.nn.gelu(x, approximate=True)

def _silu(x):
    return jax.nn.silu(x)

def _sigmoid(x):
    return jax.nn.sigmoid(x)

def _layernorm(x, axis=-1, eps=1e-05):
    m = jnp.mean(x, axis=axis, keepdims=True)
    v = jnp.var(x, axis=axis, keepdims=True)
    return (x - m) / jnp.sqrt(v + eps)

def _scatter_add(tgt, idx, src, axis=0):
    return tgt.at[idx].add(src)

def _segment_sum(src, seg, n):
    return jax.ops.segment_sum(src, seg, n)
kernel_name = 'mk_metaformer_d2_conv_nhwc256_r2_1051cb'

def setup_inputs(seed: int=0):
    np.random.seed(seed)
    _w = jnp.asarray

    def _rec_inputs():
        import jax
        import jax.numpy as jnp
        _gk = jax.random.key(seed)
        x = -8.268e-05 + 0.9999 * jax.random.normal(jax.random.fold_in(_gk, 1), (4, 112, 112, 128), jnp.float32)
        return x
    x = _rec_inputs()

    def _L0_conv_setup():
        import jax, jax.numpy as jnp
        import numpy as np
        B, H, W, C = (4, 112, 112, 128)
        WIN = 8
        PRETRAIN = 8
        HEADS = 8
        HD = C // HEADS
        SHIFT = WIN // 2
        CPB_HIDDEN = 256

        def _l2norm(x, eps=1.55e-05):
            return x * jax.lax.rsqrt(jnp.maximum(jnp.sum(x * x, axis=-1, keepdims=True), eps))

        def _rel_coords_table():
            coords = np.arange(1 - WIN, WIN, dtype=np.float32)
            tab = np.stack(np.meshgrid(coords, coords, indexing='ij'), axis=-1)
            tab *= 8.0 / (PRETRAIN - 1.0)
            tab = np.sign(tab) * np.log1p(np.abs(tab)) / np.log(8.0)
            return tab.reshape(-1, 2).astype(np.float32)

        def _rel_index():
            idx = np.stack(np.meshgrid(np.arange(WIN), np.arange(WIN), indexing='ij')).reshape(2, -1)
            rel = idx[:, :, None] - idx[:, None, :] + (WIN - 1)
            return (rel[0] * (2 * WIN - 1) + rel[1]).reshape(-1)

        def _shift_mask():
            s = SHIFT
            row = np.repeat(np.arange(3), [H - WIN, WIN - s, s])
            col = np.repeat(np.arange(3), [W - WIN, WIN - s, s])
            region = row[:, None] * 3 + col[None, :] + 1
            reg = region.reshape(H // WIN, WIN, W // WIN, WIN).transpose(0, 2, 1, 3)
            reg = reg.reshape(-1, WIN * WIN)
            diff = reg[:, :, None] - reg[:, None, :]
            return np.where(diff == 0, 0.0, -100.0).astype(np.float32)[None, :, None]
        _REL_TAB = _rel_coords_table()
        _REL_IDX = _rel_index()
        _SHIFT_MASK = _shift_mask()

        def _forward(x, w_qkv, q_bias, v_bias, scale, cpb_w1, cpb_b1, cpb_w2, w_proj, b_proj):
            nh, nw = (H // WIN, W // WIN)
            nwin = nh * nw
            qkv = jnp.einsum('bhwc,cd->bhwd', x, w_qkv)
            qkv = qkv + jnp.concatenate([q_bias, jnp.zeros_like(q_bias), v_bias])
            qkv = jnp.roll(qkv, (-SHIFT, -SHIFT), axis=(1, 2))
            qkv = qkv.reshape(B, nh, WIN, nw, WIN, 3, HEADS, HD)
            qkv = qkv.transpose(0, 1, 3, 6, 2, 4, 5, 7).reshape(B, nwin, HEADS, WIN * WIN, 3, HD)
            q, k, v = (qkv[..., 0, :], qkv[..., 1, :], qkv[..., 2, :])
            q = _l2norm(q) * jnp.exp(scale)
            k = _l2norm(k)
            attn = jnp.einsum('bnhqd,bnhkd->bnhqk', q, k)
            hbias = jax.nn.relu(jnp.asarray(_REL_TAB) @ cpb_w1 + cpb_b1)
            btab = jax.nn.sigmoid(hbias @ cpb_w2) * 16.0
            bias = btab[jnp.asarray(_REL_IDX)].reshape(WIN * WIN, WIN * WIN, HEADS)
            bias = bias.transpose(2, 0, 1)[None, None]
            attn = attn + bias + jnp.asarray(_SHIFT_MASK)
            attn = jax.nn.softmax(attn, axis=-1)
            out = jnp.einsum('bnhqk,bnhkd->bnhqd', attn, v)
            out = out.reshape(B, nh, nw, HEADS, WIN, WIN, HD)
            out = out.transpose(0, 1, 4, 2, 5, 3, 6).reshape(B, H, W, C)
            out = jnp.roll(out, (SHIFT, SHIFT), axis=(1, 2))
            return jnp.einsum('bhwc,cd->bhwd', out, w_proj) + b_proj
        key = jax.random.key(seed)
        ks = jax.random.split(key, 6)

        def norm(k, shape, scale=0.02):
            return jax.random.normal(k, shape, dtype=jnp.float32) * scale
        return {'x': jax.random.normal(ks[0], (B, H, W, C), dtype=jnp.float32), 'w_qkv': norm(ks[1], (C, 3 * C)), 'q_bias': jnp.zeros((C,), jnp.float32), 'v_bias': jnp.zeros((C,), jnp.float32), 'scale': jnp.full((HEADS, 1, 1), np.log(10.0), jnp.float32), 'cpb_w1': norm(ks[2], (2, CPB_HIDDEN), 0.1), 'cpb_b1': jnp.zeros((CPB_HIDDEN,), jnp.float32), 'cpb_w2': norm(ks[3], (CPB_HIDDEN, HEADS), 0.1), 'w_proj': norm(ks[4], (C, C)), 'b_proj': jnp.zeros((C,), jnp.float32)}
    _L0_conv_all = _L0_conv_setup()
    _L0_conv_in = {k: v for k, v in _L0_conv_all.items() if k in ('w_qkv', 'q_bias', 'v_bias', 'scale', 'cpb_w1', 'cpb_b1', 'cpb_w2', 'w_proj', 'b_proj')}
    del _L0_conv_all

    def _L0_ffn_setup():
        import jax, jax.numpy as jnp
        import numpy as np
        B, S, D = (8, 2048, 128)
        H = 4 * D
        CAPACITY = 0.5
        key = jax.random.key(seed)
        ks = jax.random.split(key, 6)
        x = jax.random.normal(ks[0], (B, S, D), dtype=jnp.float32)
        attention_mask = jnp.zeros((B, 1, 1, S), dtype=jnp.float32)
        wr = jax.random.normal(ks[1], (D, 1), dtype=jnp.float32) * 0.02
        br = jnp.zeros((1,), dtype=jnp.float32)
        w1 = jax.random.normal(ks[2], (D, H), dtype=jnp.float32) * 0.02
        b1 = jnp.zeros((H,), dtype=jnp.float32)
        w2 = jax.random.normal(ks[3], (H, D), dtype=jnp.float32) * 0.02
        b2 = jnp.zeros((D,), dtype=jnp.float32)
        return {'x': x, 'attention_mask': attention_mask, 'wr': wr, 'br': br, 'w1': w1, 'b1': b1, 'w2': w2, 'b2': b2}
    _L0_ffn_all = _L0_ffn_setup()
    _L0_ffn_in = {k: v for k, v in _L0_ffn_all.items() if k in ('attention_mask', 'wr', 'br', 'w1', 'b1', 'w2', 'b2')}
    del _L0_ffn_all

    def _L1_conv_setup():
        import jax, jax.numpy as jnp
        import numpy as np
        from jax import lax
        WBITS = 2
        ABITS = 2
        STRIDES = (1, 1)
        PADDING = 'SAME'

        def _ste_quantize(x, k):
            n = float(2 ** k - 1)
            q = jnp.round(x * n) / n
            return x + lax.stop_gradient(q - x)

        def _quantize_weight(w, k):
            t = jnp.tanh(w)
            t = t / jnp.max(jnp.abs(t)) * 0.5 + 0.5
            return 2.0 * _ste_quantize(t, k) - 1.0

        def _quantize_act(x, k):
            return _ste_quantize(jnp.clip(x, 0.0, 1.0), k)
        key = jax.random.key(seed)
        kx, kw = jax.random.split(key)
        x = jax.random.uniform(kx, (32, 56, 56, 128), dtype=jnp.float32)
        w = jax.random.normal(kw, (3, 3, 128, 128), dtype=jnp.float32) * 0.2
        w = w / jnp.sqrt(1e-07 + jnp.sum(w * w, axis=(0, 1, 2), keepdims=True))
        return {'x': x, 'w': w}
    _L1_conv_all = _L1_conv_setup()
    _L1_conv_in = {k: v for k, v in _L1_conv_all.items() if k in ('w',)}
    del _L1_conv_all

    def _L1_ffn_setup():
        import jax, jax.numpy as jnp
        import numpy as np
        B, N, D = (16, 2048, 128)
        NUM_EXPERTS, TOP_K, HEADS = (4, 2, 4)
        N_EDGES = 524288
        LN_EPS = 1e-05

        def _layernorm(x, g, b):
            mu = x.mean(-1, keepdims=True)
            var = ((x - mu) ** 2).mean(-1, keepdims=True)
            return (x - mu) * jax.lax.rsqrt(var + LN_EPS) * g + b

        def _forward(x, edge_index, W_gat, att_src, att_dst, b_gat, ln_gamma, ln_beta, W1, b1, W2, b2):
            Bc, Nc, Dc = x.shape
            M = Bc * Nc
            x_flat = x.reshape(M, Dc)
            h = (x_flat @ W_gat).reshape(M, HEADS, NUM_EXPERTS)
            loops = jnp.arange(M, dtype=edge_index.dtype)
            src = jnp.concatenate([edge_index[0], loops])
            dst = jnp.concatenate([edge_index[1], loops])
            a_src = (h * att_src).sum(-1)
            a_dst = (h * att_dst).sum(-1)
            e = jax.nn.leaky_relu(a_src[src] + a_dst[dst], negative_slope=0.2)
            e_max = jax.ops.segment_max(e, dst, num_segments=M)
            ee = jnp.exp(e - e_max[dst])
            denom = jax.ops.segment_sum(ee, dst, num_segments=M)
            alpha = ee / (denom[dst] + 1e-16)
            msg = h[src] * alpha[:, :, None]
            agg = jax.ops.segment_sum(msg, dst, num_segments=M).reshape(M, HEADS * NUM_EXPERTS) + b_gat
            scores = _layernorm(agg, ln_gamma, ln_beta).reshape(M, HEADS, NUM_EXPERTS).mean(1)
            scores = scores.reshape(Bc, Nc, NUM_EXPERTS)
            topk_s, topk_i = jax.lax.top_k(scores, TOP_K)
            w = jax.nn.softmax(topk_s, axis=-1)
            out = jnp.zeros_like(x)
            for ei in range(NUM_EXPERTS):
                g = jnp.where(topk_i == ei, w, 0.0).sum(-1)
                hh = jax.nn.gelu(x @ W1[ei] + b1[ei], approximate=False)
                out = out + g[..., None] * (hh @ W2[ei] + b2[ei])
            return out
        key = jax.random.key(seed)
        ks = jax.random.split(key, 8)
        s = 0.05
        return {'x': jax.random.normal(ks[0], (B, N, D), jnp.float32), 'W_gat': jax.random.normal(ks[1], (D, HEADS * NUM_EXPERTS), jnp.float32) * s, 'att_src': jax.random.normal(ks[2], (HEADS, NUM_EXPERTS), jnp.float32) * s, 'att_dst': jax.random.normal(ks[3], (HEADS, NUM_EXPERTS), jnp.float32) * s, 'b_gat': jnp.zeros((HEADS * NUM_EXPERTS,), jnp.float32), 'ln_gamma': jnp.ones((HEADS * NUM_EXPERTS,), jnp.float32), 'ln_beta': jnp.zeros((HEADS * NUM_EXPERTS,), jnp.float32), 'W1': jax.random.normal(ks[4], (NUM_EXPERTS, D, 2 * D), jnp.float32) * s, 'b1': jnp.zeros((NUM_EXPERTS, 2 * D), jnp.float32), 'W2': jax.random.normal(ks[5], (NUM_EXPERTS, 2 * D, D), jnp.float32) * s, 'b2': jnp.zeros((NUM_EXPERTS, D), jnp.float32), 'edge_index': jax.random.randint(ks[6], (2, N_EDGES), 0, B * N, jnp.int32)}
    _L1_ffn_all = _L1_ffn_setup()
    _L1_ffn_in = {k: v for k, v in _L1_ffn_all.items() if k in ('W_gat', 'att_src', 'att_dst', 'b_gat', 'ln_gamma', 'ln_beta', 'W1', 'b1', 'W2', 'b2', 'edge_index')}
    del _L1_ffn_all
    return {'x': x, 'L0_conv_w_qkv': _L0_conv_in['w_qkv'], 'L0_conv_q_bias': _L0_conv_in['q_bias'], 'L0_conv_v_bias': _L0_conv_in['v_bias'], 'L0_conv_scale': _L0_conv_in['scale'], 'L0_conv_cpb_w1': _L0_conv_in['cpb_w1'], 'L0_conv_cpb_b1': _L0_conv_in['cpb_b1'], 'L0_conv_cpb_w2': _L0_conv_in['cpb_w2'], 'L0_conv_w_proj': _L0_conv_in['w_proj'], 'L0_conv_b_proj': _L0_conv_in['b_proj'], 'L0_ffn_attention_mask': _L0_ffn_in['attention_mask'], 'L0_ffn_wr': _L0_ffn_in['wr'], 'L0_ffn_br': _L0_ffn_in['br'], 'L0_ffn_w1': _L0_ffn_in['w1'], 'L0_ffn_b1': _L0_ffn_in['b1'], 'L0_ffn_w2': _L0_ffn_in['w2'], 'L0_ffn_b2': _L0_ffn_in['b2'], 'L1_conv_w': _L1_conv_in['w'], 'L1_ffn_W_gat': _L1_ffn_in['W_gat'], 'L1_ffn_att_src': _L1_ffn_in['att_src'], 'L1_ffn_att_dst': _L1_ffn_in['att_dst'], 'L1_ffn_b_gat': _L1_ffn_in['b_gat'], 'L1_ffn_ln_gamma': _L1_ffn_in['ln_gamma'], 'L1_ffn_ln_beta': _L1_ffn_in['ln_beta'], 'L1_ffn_W1': _L1_ffn_in['W1'], 'L1_ffn_b1': _L1_ffn_in['b1'], 'L1_ffn_W2': _L1_ffn_in['W2'], 'L1_ffn_b2': _L1_ffn_in['b2'], 'L1_ffn_edge_index': _L1_ffn_in['edge_index']}

def reference(x, L0_conv_w_qkv, L0_conv_q_bias, L0_conv_v_bias, L0_conv_scale, L0_conv_cpb_w1, L0_conv_cpb_b1, L0_conv_cpb_w2, L0_conv_w_proj, L0_conv_b_proj, L0_ffn_attention_mask, L0_ffn_wr, L0_ffn_br, L0_ffn_w1, L0_ffn_b1, L0_ffn_w2, L0_ffn_b2, L1_conv_w, L1_ffn_W_gat, L1_ffn_att_src, L1_ffn_att_dst, L1_ffn_b_gat, L1_ffn_ln_gamma, L1_ffn_ln_beta, L1_ffn_W1, L1_ffn_b1, L1_ffn_W2, L1_ffn_b2, L1_ffn_edge_index):
    import jax
    import jax.numpy as jnp

    def _L0_conv_ref(x, w_qkv, q_bias, v_bias, scale, cpb_w1, cpb_b1, cpb_w2, w_proj, b_proj):
        import jax, jax.numpy as jnp
        import numpy as np
        B, H, W, C = (4, 112, 112, 128)
        WIN = 8
        PRETRAIN = 8
        HEADS = 8
        HD = C // HEADS
        SHIFT = WIN // 2
        CPB_HIDDEN = 256

        def _l2norm(x, eps=1.55e-05):
            return x * jax.lax.rsqrt(jnp.maximum(jnp.sum(x * x, axis=-1, keepdims=True), eps))

        def _rel_coords_table():
            coords = np.arange(1 - WIN, WIN, dtype=np.float32)
            tab = np.stack(np.meshgrid(coords, coords, indexing='ij'), axis=-1)
            tab *= 8.0 / (PRETRAIN - 1.0)
            tab = np.sign(tab) * np.log1p(np.abs(tab)) / np.log(8.0)
            return tab.reshape(-1, 2).astype(np.float32)

        def _rel_index():
            idx = np.stack(np.meshgrid(np.arange(WIN), np.arange(WIN), indexing='ij')).reshape(2, -1)
            rel = idx[:, :, None] - idx[:, None, :] + (WIN - 1)
            return (rel[0] * (2 * WIN - 1) + rel[1]).reshape(-1)

        def _shift_mask():
            s = SHIFT
            row = np.repeat(np.arange(3), [H - WIN, WIN - s, s])
            col = np.repeat(np.arange(3), [W - WIN, WIN - s, s])
            region = row[:, None] * 3 + col[None, :] + 1
            reg = region.reshape(H // WIN, WIN, W // WIN, WIN).transpose(0, 2, 1, 3)
            reg = reg.reshape(-1, WIN * WIN)
            diff = reg[:, :, None] - reg[:, None, :]
            return np.where(diff == 0, 0.0, -100.0).astype(np.float32)[None, :, None]
        _REL_TAB = _rel_coords_table()
        _REL_IDX = _rel_index()
        _SHIFT_MASK = _shift_mask()

        def _forward(x, w_qkv, q_bias, v_bias, scale, cpb_w1, cpb_b1, cpb_w2, w_proj, b_proj):
            nh, nw = (H // WIN, W // WIN)
            nwin = nh * nw
            qkv = jnp.einsum('bhwc,cd->bhwd', x, w_qkv)
            qkv = qkv + jnp.concatenate([q_bias, jnp.zeros_like(q_bias), v_bias])
            qkv = jnp.roll(qkv, (-SHIFT, -SHIFT), axis=(1, 2))
            qkv = qkv.reshape(B, nh, WIN, nw, WIN, 3, HEADS, HD)
            qkv = qkv.transpose(0, 1, 3, 6, 2, 4, 5, 7).reshape(B, nwin, HEADS, WIN * WIN, 3, HD)
            q, k, v = (qkv[..., 0, :], qkv[..., 1, :], qkv[..., 2, :])
            q = _l2norm(q) * jnp.exp(scale)
            k = _l2norm(k)
            attn = jnp.einsum('bnhqd,bnhkd->bnhqk', q, k)
            hbias = jax.nn.relu(jnp.asarray(_REL_TAB) @ cpb_w1 + cpb_b1)
            btab = jax.nn.sigmoid(hbias @ cpb_w2) * 16.0
            bias = btab[jnp.asarray(_REL_IDX)].reshape(WIN * WIN, WIN * WIN, HEADS)
            bias = bias.transpose(2, 0, 1)[None, None]
            attn = attn + bias + jnp.asarray(_SHIFT_MASK)
            attn = jax.nn.softmax(attn, axis=-1)
            out = jnp.einsum('bnhqk,bnhkd->bnhqd', attn, v)
            out = out.reshape(B, nh, nw, HEADS, WIN, WIN, HD)
            out = out.transpose(0, 1, 4, 2, 5, 3, 6).reshape(B, H, W, C)
            out = jnp.roll(out, (SHIFT, SHIFT), axis=(1, 2))
            return jnp.einsum('bhwc,cd->bhwd', out, w_proj) + b_proj
        return _forward(x, w_qkv, q_bias, v_bias, scale, cpb_w1, cpb_b1, cpb_w2, w_proj, b_proj)

    def _L0_ffn_ref(x, attention_mask, wr, br, w1, b1, w2, b2):
        import jax, jax.numpy as jnp
        import numpy as np
        B, S, D = (8, 2048, 128)
        H = 4 * D
        CAPACITY = 0.5
        b, s, d = x.shape
        weights = (jnp.einsum('bsd,do->bso', x, wr) + br)[..., 0]
        k = max(1, int(CAPACITY * s))
        kk = k - 1 if k > 1 else 1
        _, idx = jax.lax.top_k(weights, k)
        sel_idx = idx[:, :kk]
        sel = jnp.take_along_axis(x, sel_idx[:, :, None], axis=1)
        h = jax.nn.gelu(jnp.einsum('bkd,dh->bkh', sel, w1) + b1)
        y = jnp.einsum('bkh,hd->bkd', h, w2) + b2
        w_sel = jnp.take_along_axis(weights, sel_idx, axis=1)
        y = y * w_sel[..., None]
        batch_idx = jnp.arange(b)[:, None]
        processed = jnp.zeros_like(x).at[batch_idx, sel_idx].set(y)
        return processed + x

    def _L1_conv_ref(x, w):
        import jax, jax.numpy as jnp
        import numpy as np
        from jax import lax
        WBITS = 2
        ABITS = 2
        STRIDES = (1, 1)
        PADDING = 'SAME'

        def _ste_quantize(x, k):
            n = float(2 ** k - 1)
            q = jnp.round(x * n) / n
            return x + lax.stop_gradient(q - x)

        def _quantize_weight(w, k):
            t = jnp.tanh(w)
            t = t / jnp.max(jnp.abs(t)) * 0.5 + 0.5
            return 2.0 * _ste_quantize(t, k) - 1.0

        def _quantize_act(x, k):
            return _ste_quantize(jnp.clip(x, 0.0, 1.0), k)
        wq = _quantize_weight(w, WBITS)
        xq = _quantize_act(x, ABITS)
        out = lax.conv_general_dilated(xq, wq, window_strides=STRIDES, padding=PADDING, dimension_numbers=('NHWC', 'HWIO', 'NHWC'))
        return out

    def _L1_ffn_ref(x, W_gat, att_src, att_dst, b_gat, ln_gamma, ln_beta, W1, b1, W2, b2, edge_index):
        import jax, jax.numpy as jnp
        import numpy as np
        B, N, D = (16, 2048, 128)
        NUM_EXPERTS, TOP_K, HEADS = (4, 2, 4)
        N_EDGES = 524288
        LN_EPS = 1e-05

        def _layernorm(x, g, b):
            mu = x.mean(-1, keepdims=True)
            var = ((x - mu) ** 2).mean(-1, keepdims=True)
            return (x - mu) * jax.lax.rsqrt(var + LN_EPS) * g + b

        def _forward(x, edge_index, W_gat, att_src, att_dst, b_gat, ln_gamma, ln_beta, W1, b1, W2, b2):
            Bc, Nc, Dc = x.shape
            M = Bc * Nc
            x_flat = x.reshape(M, Dc)
            h = (x_flat @ W_gat).reshape(M, HEADS, NUM_EXPERTS)
            loops = jnp.arange(M, dtype=edge_index.dtype)
            src = jnp.concatenate([edge_index[0], loops])
            dst = jnp.concatenate([edge_index[1], loops])
            a_src = (h * att_src).sum(-1)
            a_dst = (h * att_dst).sum(-1)
            e = jax.nn.leaky_relu(a_src[src] + a_dst[dst], negative_slope=0.2)
            e_max = jax.ops.segment_max(e, dst, num_segments=M)
            ee = jnp.exp(e - e_max[dst])
            denom = jax.ops.segment_sum(ee, dst, num_segments=M)
            alpha = ee / (denom[dst] + 1e-16)
            msg = h[src] * alpha[:, :, None]
            agg = jax.ops.segment_sum(msg, dst, num_segments=M).reshape(M, HEADS * NUM_EXPERTS) + b_gat
            scores = _layernorm(agg, ln_gamma, ln_beta).reshape(M, HEADS, NUM_EXPERTS).mean(1)
            scores = scores.reshape(Bc, Nc, NUM_EXPERTS)
            topk_s, topk_i = jax.lax.top_k(scores, TOP_K)
            w = jax.nn.softmax(topk_s, axis=-1)
            out = jnp.zeros_like(x)
            for ei in range(NUM_EXPERTS):
                g = jnp.where(topk_i == ei, w, 0.0).sum(-1)
                hh = jax.nn.gelu(x @ W1[ei] + b1[ei], approximate=False)
                out = out + g[..., None] * (hh @ W2[ei] + b2[ei])
            return out
        return _forward(x, edge_index, W_gat, att_src, att_dst, b_gat, ln_gamma, ln_beta, W1, b1, W2, b2)

    def _gn(v, G=32, eps=1e-05):
        B_, H_, W_, C_ = v.shape
        g = v.reshape(B_, H_, W_, G, C_ // G)
        m = jnp.mean(g, axis=(1, 2, 4), keepdims=True)
        s = jnp.var(g, axis=(1, 2, 4), keepdims=True)
        return ((g - m) / jnp.sqrt(s + eps)).reshape(v.shape)

    def _ln_c(v, eps=1e-06):
        m = jnp.mean(v, axis=-1, keepdims=True)
        s = jnp.var(v, axis=-1, keepdims=True)
        return (v - m) / jnp.sqrt(s + eps)

    def _ln_t(v, eps=1e-05):
        m = jnp.mean(v, axis=-1, keepdims=True)
        s = jnp.var(v, axis=-1, keepdims=True)
        return (v - m) / jnp.sqrt(s + eps)

    def _to_tokens(v):
        B_, H_, W_, C_ = v.shape
        return v.reshape(B_, H_ * W_, C_)

    def _from_tokens(t, like):
        return t.reshape(like.shape)
    x = x + _L0_conv_ref(_ln_c(x), L0_conv_w_qkv, L0_conv_q_bias, L0_conv_v_bias, L0_conv_scale, L0_conv_cpb_w1, L0_conv_cpb_b1, L0_conv_cpb_w2, L0_conv_w_proj, L0_conv_b_proj)
    t = _to_tokens(x)
    t = t + _L0_ffn_ref(_ln_t(t), L0_ffn_attention_mask, L0_ffn_wr, L0_ffn_br, L0_ffn_w1, L0_ffn_b1, L0_ffn_w2, L0_ffn_b2)
    x = _from_tokens(t, x)
    x = x + _L1_conv_ref(_ln_c(x), L1_conv_w)
    t = _to_tokens(x)
    t = t + _L1_ffn_ref(_ln_t(t), L1_ffn_W_gat, L1_ffn_att_src, L1_ffn_att_dst, L1_ffn_b_gat, L1_ffn_ln_gamma, L1_ffn_ln_beta, L1_ffn_W1, L1_ffn_b1, L1_ffn_W2, L1_ffn_b2, L1_ffn_edge_index)
    x = _from_tokens(t, x)
    return x

_drawn_inputs = setup_inputs


def setup_inputs(seed=0):
    import zlib

    import numpy as np

    out = dict(_drawn_inputs(seed))
    spreads = {'L0_conv_q_bias': (0.0, 0.1),
     'L0_conv_v_bias': (0.0, 0.1),
     'L0_conv_scale': (2.3025851249694824, 0.2),
     'L0_conv_cpb_b1': (0.0, 0.311),
     'L0_conv_b_proj': (0.0, 0.1),
     'L0_ffn_b1': (0.0, 0.434),
     'L0_ffn_b2': (0.0, 0.1),
     'L1_ffn_b_gat': (0.0, 0.337),
     'L1_ffn_ln_gamma': (1.0, 0.6),
     'L1_ffn_ln_beta': (0.0, 0.711),
     'L1_ffn_b1': (0.0, 0.8),
     'L1_ffn_b2': (0.0, 0.66)}
    factors = {'L1_ffn_att_src': 41.343, 'L1_ffn_att_dst': 186.387}
    for name, (base, spread) in spreads.items():
        noise = np.random.default_rng([zlib.crc32(name.encode()), seed]).standard_normal(out[name].shape)
        drawn = base * np.exp(spread * noise) if base else spread * noise
        out[name] = jnp.asarray(drawn.astype(out[name].dtype))
    for name, factor in factors.items():
        out[name] = (out[name] * factor).astype(out[name].dtype)
    return out
```

```python
from contextlib import ExitStack

import numpy as np

import concourse.bass as bass
from concourse import mybir

F32 = mybir.dt.float32
BF16 = mybir.dt.bfloat16
I32 = mybir.dt.int32
ALU = mybir.AluOpType
ACT = mybir.ActivationFunctionType
AX_X = mybir.AxisListType.X

P = 128
B, H, W, C = 4, 112, 112, 128
M = B * H * W
E = 524288
EP = E // P
NPP = M // P
BLK = 64
DST_MID = M / 2 - 0.5


class Steps:

    def __init__(self, sem):
        self.sem, self.n = sem, 0

    def done_by(self, ins, by=1):
        ins.then_inc(self.sem, by)
        self.n += by
        return self.n


def clear(nc, sems):
    with nc.Block() as block:
        @block.gpsimd
        def _(pool):
            for sem in sems:
                pool.sem_clear(sem)


def sort_edges(nc, edges, sgn_dram, ident_dram, src_dram, dst_dram, same_dram, first_dram):
    with ExitStack() as ctx:
        def sb(name, shape, dt):
            return ctx.enter_context(nc.sbuf_tensor(name, shape, dt))

        def sem(name):
            return ctx.enter_context(nc.semaphore(name))

        src = sb("so_src", [P, EP], I32)
        dst = sb("so_dst", [P, EP], I32)
        ka = sb("so_ka", [P, EP], F32)
        kb = sb("so_kb", [P, EP], F32)
        sgn = sb("so_sgn", [P, 8], F32)
        heads = sb("so_heads", [P, EP // BLK], F32)
        ident = sb("so_ident", [P, P], F32)
        banks = [ctx.enter_context(nc.psum_tensor(f"so_ps{i}", [P, 512], F32)) for i in range(8)]
        loaded = sem("so_loaded")
        stepped = Steps(sem("so_stepped"))
        scaled = Steps(sem("so_scaled"))
        turned = Steps(sem("so_turned"))
        moved = Steps(sem("so_moved"))
        stored = sem("so_stored")

        NCH, LOCAL = 8, 12
        PH = 19
        plan = []
        x, y = ka, kb
        for k in range(1, LOCAL + 1):
            plan.append(("stage", x, y, 1 << (k - 1), True)); x, y = y, x
            for b in range(k - 2, -1, -1):
                plan.append(("stage", x, y, 1 << b, False)); x, y = y, x
        for k in range(LOCAL + 1, PH + 1):
            plan.append(("flip", x, y, k)); x, y = y, x
            plan.append(("turn", x, y)); x, y = y, x
            for b in range(k - 1 - LOCAL, -1, -1):
                plan.append(("stage", x, y, 1 << b, False)); x, y = y, x
            plan.append(("turn", x, y)); x, y = y, x
            for b in range(LOCAL - 1, -1, -1):
                plan.append(("stage", x, y, 1 << b, False)); x, y = y, x
        final, other = x, y

        with nc.Block() as block:
            at, s, m, t, f = [], 7, 0, 0, 0
            for item in plan:
                at.append((s, m, t, f))
                if item[0] == "stage":
                    s += 2
                elif item[0] == "flip":
                    f += NCH
                else:
                    t, m, s = t + NCH, m + NCH // 2, s + NCH // 2
            end = s

            @block.sync
            def _(sp):
                sp.dma_start(src[:, :], edges[0].rearrange("(p e) -> p e", p=P)).then_inc(loaded, 16)
                sp.dma_start(dst[:, :], edges[1].rearrange("(p e) -> p e", p=P)).then_inc(loaded, 16)
                sp.dma_start(sgn[:, :], sgn_dram).then_inc(loaded, 16)
                sp.dma_start(ident[:, :], ident_dram).then_inc(loaded, 16)
                sp.wait_ge(stepped.sem, end + 7)
                for dram, tile in ((src_dram, src), (dst_dram, final), (same_dram, other)):
                    sp.dma_start(dram.rearrange("(p e) -> p e", p=P), tile[:, :]).then_inc(stored, 16)
                sp.dma_start(first_dram, heads[:, :]).then_inc(stored, 16)
                sp.wait_ge(stored, 64)

            @block.scalar
            def _(act):
                act.wait_ge(loaded, 64)
                for item, (s, m, t, f) in zip(plan, at):
                    if item[0] == "flip":
                        _, a, b, k = item
                        act.wait_ge(stepped.sem, s)
                        for c in range(NCH):
                            w = slice(512 * c, 512 * c + 512)
                            nc.scalar.activation(b[:, w], a[:, w], ACT.Copy,
                                                 scale=sgn[:, k - LOCAL:k - LOCAL + 1]).then_inc(scaled.sem, 1)
                    elif item[0] == "turn":
                        _, a, b = item
                        for c in range(0, NCH, 2):
                            act.wait_ge(turned.sem, t + c + 1)
                            nc.scalar.activation(b[:, 512 * c:512 * c + 512], banks[c][:, :], ACT.Copy).then_inc(moved.sem, 1)

            @block.tensor
            def _(pe):
                pe.wait_ge(loaded, 64)
                for item, (s, m, t, f) in zip(plan, at):
                    if item[0] != "turn":
                        continue
                    _, a, b = item
                    pe.wait_ge(stepped.sem, s)
                    if m:
                        pe.wait_ge(moved.sem, m)
                    for c in range(NCH):
                        if f and t // NCH % 2 == 0:
                            pe.wait_ge(scaled.sem, f - NCH + c + 1)
                        for q in range(4):
                            w = slice(512 * c + P * q, 512 * c + P * (q + 1))
                            last = nc.tensor.transpose(banks[c][:, P * q:P * (q + 1)], a[:, w], ident[:, :])
                        last.then_inc(turned.sem, 1)

            @block.vector
            def _(v):
                done = stepped
                v.wait_ge(loaded, 64)
                done.done_by(nc.vector.tensor_scalar(ka[:, :], dst[:, :], DST_MID, None, ALU.subtract))
                v.wait_ge(done.sem, 1)
                done.done_by(nc.vector.scalar_tensor_tensor(kb[:, :], ka[:, :], -1.0, ka[:, :], ALU.mult, ALU.max))
                v.wait_ge(done.sem, 2)
                done.done_by(nc.vector.tensor_scalar(dst[:, :], kb[:, :], 127.5, None, ALU.add))
                v.wait_ge(done.sem, 3)
                done.done_by(nc.vector.scalar_tensor_tensor(dst[:, :], dst[:, :], 16, src[:, :],
                                                            ALU.logical_shift_left, ALU.bitwise_or))
                done.done_by(nc.vector.tensor_scalar(kb[:, :], ka[:, :], 0.0, 2.0, ALU.is_ge, ALU.mult))
                v.wait_ge(done.sem, 5)
                done.done_by(nc.vector.scalar_tensor_tensor(kb[:, :], kb[:, :], 1.0, dst[:, :].bitcast(F32),
                                                            ALU.subtract, ALU.mult))
                v.wait_ge(done.sem, 6)
                done.done_by(nc.vector.tensor_scalar(ka[:, :], kb[:, :], sgn[:, 0:1], None, ALU.mult))
                for item, (s, m, t, f) in zip(plan, at):
                    if item[0] == "stage":
                        _, a, b, d, mirror = item
                        v.wait_ge(done.sem, s)
                        if m:
                            v.wait_ge(moved.sem, m)
                        av = a[:, :].rearrange("p (g h s) -> p g h s", h=2, s=d)
                        bv = b[:, :].rearrange("p (g h s) -> p g h s", h=2, s=d)
                        r = slice(None, None, -1) if mirror and d > 1 else slice(None)
                        done.done_by(nc.vector.tensor_tensor(bv[:, :, 0, :], av[:, :, 0, :], av[:, :, 1, r], ALU.min))
                        done.done_by(nc.vector.tensor_tensor(bv[:, :, 1, r], av[:, :, 0, :], av[:, :, 1, r], ALU.max))
                    elif item[0] == "turn":
                        _, a, b = item
                        for c in range(1, NCH, 2):
                            v.wait_ge(turned.sem, t + c + 1)
                            done.done_by(nc.vector.tensor_copy(b[:, 512 * c:512 * c + 512], banks[c][:, :]))
                assert done.n == end
                v.wait_ge(done.sem, end)
                bits = final[:, :].bitcast(I32)
                done.done_by(nc.vector.tensor_scalar(src[:, :], bits, 0xFFFF, None, ALU.bitwise_and))
                done.done_by(nc.vector.tensor_scalar(dst[:, :], bits, 16, 0x7FFF, ALU.logical_shift_right, ALU.bitwise_and))
                done.done_by(nc.vector.tensor_scalar(other[:, :], final[:, :], 0.0, 2.0, ALU.is_ge, ALU.mult))
                v.wait_ge(done.sem, end + 3)
                done.done_by(nc.vector.tensor_scalar(final[:, :], dst[:, :], 127.5, None, ALU.subtract))
                v.wait_ge(done.sem, end + 4)
                done.done_by(nc.vector.scalar_tensor_tensor(final[:, :], other[:, :], 1.0, final[:, :], ALU.subtract, ALU.mult))
                v.wait_ge(done.sem, end + 5)
                done.done_by(nc.vector.tensor_scalar(final[:, :], final[:, :], DST_MID, None, ALU.add))
                v.wait_ge(done.sem, end + 6)
                nc.vector.tensor_copy(heads[:, :], final[:, 0:EP:BLK])
                nc.vector.memset(other[:, 0:1], 0.0)
                done.done_by(nc.vector.tensor_tensor(other[:, 1:EP], final[:, 1:EP], final[:, 0:EP - 1], ALU.is_equal))
        clear(nc, (loaded, stepped.sem, scaled.sem, turned.sem, moved.sem, stored))


def row_signs():
    p = np.arange(P)
    s = [np.where((p >> (k - 12)) & 1, -1.0, 1.0) for k in range(12, 20)]
    cols = [s[0]] + [s[i - 1] * s[i] for i in range(1, 8)]
    return np.stack(cols, 1).astype(np.float32)


WIN, SHIFT, HEADS, HD = 8, 4, 8, 16
PAIRS = M // P
PPS = 7
STRIPS = PAIRS // PPS
SPI = H // WIN
GRP = 4
VW = 2 * HD + 2
QK_EPS = 1.55e-05


def make_bias(nc, d, tables):
    T = (2 * WIN - 1) ** 2
    HID = 256
    with ExitStack() as ctx:
        def sb(name, shape, dt=F32):
            return ctx.enter_context(nc.sbuf_tensor(name, shape, dt))

        w1 = sb("mb_w1", [2, HID])
        rel = sb("mb_rel", [2, T])
        b1 = sb("mb_b1", [P, 2])
        w2 = sb("mb_w2", [P, 2, HEADS])
        hid = sb("mb_hid", [P, 2, T])
        bt = sb("mb_bt", [HEADS, 3, T])
        bias = sb("mb_bias", [P, HEADS, WIN * WIN])
        masks = sb("mb_masks", [P, 4, WIN * WIN])
        full = sb("mb_full", [P, 2, HEADS, WIN * WIN])
        ph = ctx.enter_context(nc.psum_tensor("mb_ph", [P, 2, 512], F32))
        pt = ctx.enter_context(nc.psum_tensor("mb_pt", [HEADS, 512], F32))
        sem = {n: ctx.enter_context(nc.semaphore("mb_" + n)) for n in
               ("loaded", "masks_in", "hidden", "relu", "table", "exp", "sig", "bt_out", "spread", "bias_in", "sum", "full_out")}
        bt_dram = tables["bt"]
        bias_dram = tables["bias"]
        with nc.Block() as block:
            @block.sync
            def _(sp):
                for dst, src in ((w1[:, :], d["cpb_w1"]), (rel[:, :], d["rel_tab"]),
                                 (b1[:, :], d["cpb_b1"]),
                                 (w2[:, :, :], d["cpb_w2"])):
                    sp.dma_start(dst, src).then_inc(sem["loaded"], 16)
                sp.dma_start(masks[:, :, :], d["masks"]).then_inc(sem["masks_in"], 16)
                sp.wait_ge(sem["sig"], 3)
                sp.dma_start(bt_dram, bt[:, 2, :]).then_inc(sem["bt_out"], 16)
                sp.wait_ge(sem["bt_out"], 16)
                with sp.Fori(0, WIN) as qr:
                    with sp.Fori(0, WIN) as qc:
                        at = (7 - qr) * 15 + (7 - qc)
                        src = bass.AP(bt_dram.tensor, at, [[T, HEADS], [15, WIN], [1, WIN]])
                        dst = bass.AP(bias_dram.tensor, (qr * WIN + qc) * 512, [[64, HEADS], [8, WIN], [1, WIN]])
                        sp.dma_start(dst, src).then_inc(sem["spread"], 16)
                sp.wait_ge(sem["spread"], 16 * WIN * WIN)
                for w in range(2):
                    sp.dma_start(bias[64 * w:64 * w + 64, :, :].rearrange("p h k -> p (h k)"),
                                 bias_dram).then_inc(sem["bias_in"], 16)
                for m in range(4):
                    sp.wait_ge(sem["sum"], m + 1)
                    sp.dma_start(tables["bm"][m], full[:, m % 2, :, :].rearrange("p h k -> p (h k)")).then_inc(sem["full_out"], 16)
                sp.wait_ge(sem["full_out"], 64)

            @block.tensor
            def _(pe):
                pe.wait_ge(sem["loaded"], 64)
                for m in range(2):
                    nc.tensor.matmul(ph[:, m, 0:T], w1[:, P * m:P * (m + 1)], rel[:, :], start=True, stop=True).then_inc(sem["hidden"], 1)
                pe.wait_ge(sem["relu"], 2)
                for m in range(2):
                    last = nc.tensor.matmul(pt[:, 0:T], w2[:, m, :], hid[:, m, :], start=m == 0, stop=m == 1)
                last.then_inc(sem["table"], 1)

            @block.scalar
            def _(act):
                for m in range(2):
                    act.wait_ge(sem["hidden"], m + 1)
                    nc.scalar.activation(hid[:, m, :], ph[:, m, 0:T], ACT.Relu, bias=b1[:, m:m + 1]).then_inc(sem["relu"], 1)
                act.wait_ge(sem["table"], 1)
                nc.scalar.activation(bt[:, 0, :], pt[:, 0:T], ACT.Exp, scale=-1.0).then_inc(sem["exp"], 1)

            @block.vector
            def _(v):
                v.wait_ge(sem["exp"], 1)
                nc.vector.tensor_scalar(bt[:, 1, :], bt[:, 0, :], 1.0, None, ALU.add).then_inc(sem["sig"], 1)
                v.wait_ge(sem["sig"], 1)
                nc.vector.reciprocal(bt[:, 0, :], bt[:, 1, :]).then_inc(sem["sig"], 1)
                v.wait_ge(sem["sig"], 2)
                nc.vector.tensor_scalar(bt[:, 2, :], bt[:, 0, :], 16.0, None, ALU.mult).then_inc(sem["sig"], 1)
                v.wait_ge(sem["masks_in"], 16)
                v.wait_ge(sem["bias_in"], 32)
                for m in range(4):
                    if m >= 2:
                        v.wait_ge(sem["full_out"], 16 * m)
                    mk = masks[:, m, :].rearrange("p (o k) -> p o k", o=1).to_broadcast([P, HEADS, WIN * WIN])
                    nc.vector.tensor_tensor(full[:, m % 2, :, :], bias[:, :, :], mk, ALU.add).then_inc(sem["sum"], 1)
        clear(nc, sem.values())


def last_row(eng, strip):
    if isinstance(strip, int):
        return int((strip + 1) % SPI == 0)
    return ((2147 - (strip + 1) * 147 % 2048) >> 11) % 2


def attention(nc, d, tables, x1_dram, score_sb, stats_sb):
    with ExitStack() as ctx:
        def sb(name, shape, dt=F32):
            return ctx.enter_context(nc.sbuf_tensor("at_" + name, shape, dt))

        def ps(name, shape):
            return ctx.enter_context(nc.psum_tensor("at_" + name, shape, F32))

        def sem(name):
            return ctx.enter_context(nc.semaphore("at_" + name))

        ident = sb("ident", [P, P])
        wqkv = sb("wqkv", [P, 3 * C])
        wproj = sb("wproj", [P, C])
        same_head = sb("same_head", [P, P])
        consts = sb("consts", [P, 8])
        bproj = sb("bproj", [1, C])
        wr = sb("wr", [P, C])
        bm = sb("bm", [P, 4, 512])
        kscale = sb("kscale", [P, 3])
        eps = sb("eps", [P, 2])
        nswr = sb("nswr", [P, 2])
        vb_cols = sb("vb_cols", [P, P])
        ones = sb("ones", [P, P])
        beff = sb("beff", [P, C])
        xs = [sb(f"xs{i}", [P, PPS, C]) for i in range(2)]
        xb = [sb(f"xb{i}", [P, PPS, C]) for i in range(2)]
        x1 = [sb(f"x1{i}", [P, PPS, C]) for i in range(2)]
        st = [sb(f"st{i}", [P, PPS, 6]) for i in range(2)]
        mv = [sb(f"mv{i}", [P, PPS, 2]) for i in range(2)]
        lnv = [sb(f"lnv{i}", [P, PPS]) for i in range(2)]
        rstd = [sb(f"rstd{i}", [P, PPS]) for i in range(2)]
        wst = [sb(f"wst{i}", [P, PPS, 6]) for i in range(2)]
        wmv = [sb(f"wmv{i}", [P, PPS, 2]) for i in range(2)]
        wln = [sb(f"wln{i}", [P, PPS]) for i in range(2)]
        wrs = [sb(f"wrs{i}", [P, PPS]) for i in range(2)]
        wdot = [sb(f"wdot{i}", [P, PPS]) for i in range(2)]
        wtmp = [sb(f"wtmp{i}", [P, 2, PPS]) for i in range(2)]
        junk = [sb(f"junk{i}", [P, C]) for i in range(2)]
        xh = [sb(f"xh{i}", [P, C]) for i in range(2)]
        xT = [sb(f"xT{i}", [P, 192]) for i in range(2)]
        qk = [sb(f"qk{i}", [P, 2 * P]) for i in range(2)]
        sq = [sb(f"sq{i}", [P, 2 * P]) for i in range(2)]
        nm = [sb(f"nm{i}", [P, 2 * P]) for i in range(2)]
        nl = [sb(f"nl{i}", [P, 2 * P]) for i in range(2)]
        rs = [sb(f"rs{i}", [P, 2 * P]) for i in range(2)]
        qn = [sb(f"qn{i}", [P, P]) for i in range(2)]
        kn = [sb(f"kn{i}", [P, 2, 2, 64]) for i in range(2)]
        vbd = [sb(f"vbd{i}", [P, 2, GRP, VW]) for i in range(PPS)]
        lg = [sb(f"lg{i}", [P, HEADS, 64]) for i in range(2)]
        lm = [sb(f"lm{i}", [P, HEADS, 64]) for i in range(2)]
        mx = [sb(f"mx{i}", [P, HEADS]) for i in range(2)]
        pr = [sb(f"pr{i}", [P, HEADS * 64]) for i in range(2)]
        pT = [sb(f"pT{i}", [P, GRP, P]) for i in range(2)]
        rc = [sb(f"rc{i}", [P, HEADS]) for i in range(2)]
        on = [sb(f"on{i}", [P, C]) for i in range(2)]
        oT = [sb(f"oT{i}", [P, P]) for i in range(2)]

        p_s = ps("p_s", [P, GRP, 512])
        p_O = p_s[:, 0, P:P + GRP * VW].rearrange("p (g v) -> p g v", g=GRP)
        p_proj = p_s[:, 1, P:P + C]
        p_n = ps("p_n", [P, 512])
        p_qkv = ps("p_qkv", [P, 4, P])
        p_tr = ps("p_tr", [P, 512])
        p_xT, p_oT = p_tr[:, 0:192], p_tr[:, 256:384]
        p_pT = ps("p_pT", [P, GRP, P])

        S = {n: sem(n) for n in (
            "consts_in", "setup", "ks", "beff_p", "x_in0", "x_in1", "x_out0", "x_out1", "xstat", "xrstd", "xb",
            "xh", "xTp", "xT", "qkvp", "qk", "v", "sq", "norm", "nmax", "rs", "qkn", "scores",
            "logit", "prob", "pTp", "pT", "outp", "on", "oTp", "oT", "proj", "x1", "dot", "wstat", "wrstd", "score", "passed", "passed_sp")}
        N = PAIRS
        HALF = 2 * PPS

        def pairs_of(eng, emit):
            for u in range(-3, HALF):
                emit(Step(eng, u, u, 0, True, False))
            with eng.Fori(1, STRIPS // 2 - 1) as i:
                for u in range(HALF):
                    emit(Step(eng, u, i * HALF + u, i * 2, False, False))
            for u in range(HALF + 3):
                emit(Step(eng, u, N - HALF + u, STRIPS - 2, False, True))

        class Step:
            def __init__(self, eng, u, t, s0, first, last):
                self.eng, self.u, self.t, self.s0, self.first, self.last = eng, u, t, s0, first, last

            def has(self, off):
                return not (self.first and self.u + off < 0) and not (self.last and self.u + off >= HALF)

            def wait(self, name, off, per=1, k=None):
                if self.has(off):
                    self.eng.wait_ge(S[name], (self.t + off) * per + (per if k is None else k))

            def slot(self, off):
                return (self.u + off) % 2

            def strip(self, off):
                s = (self.u + off) // PPS
                return self.s0 + s, s % 2, (self.u + off) % PPS

        with nc.Block() as block:
            @block.sync
            def _(sp):
                for dst, src in ((ident[:, :], d["ident"]), (wqkv[:, :], d["w_qkv"]), (wproj[:, :], d["w_proj"]),
                                 (same_head[:, :], d["same_head"]), (consts[:, :], d["consts"]),
                                 (bproj[:, :], d["b_proj"]), (wr[:, :], d["wr"])):
                    sp.dma_start(dst, src).then_inc(S["consts_in"], 16)
                sp.dma_start(bm[:, :, :], tables["bm"].rearrange("m p k -> p m k")).then_inc(S["consts_in"], 16)
                for s in range(2):
                    sp.dma_start(xs[s][:, :, :], d["x_win"][s]).then_inc(S[f"x_in{s}"], 16)

                def emit(p):
                    strip, s, j = p.strip(3)
                    if p.has(3) and j == PPS - 1 and not p.last and p.u + 3 < HALF:
                        p.wait("xh", 3)
                        sp.sem_inc(S["passed_sp"], 1)
                        sp.wait_ge(S["xb"], strip + 1)
                        sp.dma_start(xs[s][:, :, :], d["x_win"][bass.ds(strip + 2, 1)].rearrange("o p u c -> (o p) u c")).then_inc(S[f"x_in{s}"], 16)
                    strip, s, j = p.strip(-3)
                    if p.has(-3) and j == PPS - 1:
                        p.wait("x1", -3)
                        sp.dma_start(x1_dram[bass.ds(strip, 1)].rearrange("o p u c -> (o p) u c"), x1[s][:, :, :]).then_inc(S[f"x_out{s}"], 16)

                pairs_of(sp, emit)
                for s in range(2):
                    sp.wait_ge(S[f"x_out{s}"], 16 * (STRIPS // 2))

            @block.tensor
            def _(pe):
                pe.wait_ge(S["consts_in"], 16 * 8)
                pe.wait_ge(S["setup"], 5)
                nc.tensor.matmul(p_proj, vb_cols[:, :], wproj[:, :], start=True, stop=False)
                nc.tensor.matmul(p_proj, ones[0:1, :], bproj[:, :], start=False, stop=True).then_inc(S["beff_p"], 1)
                pe.wait_ge(S["setup"], 6)

                def emit(p):
                    if p.has(2):
                        r = p.slot(2)
                        p.wait("xT", 2)
                        p.wait("v", 1)
                        for j in range(2):
                            nc.tensor.matmul(p_qkv[:, j, :], wqkv[:, C * j:C * (j + 1)], xT[r][:, 0:P], start=True, stop=True)
                        for j in range(2):
                            mm = nc.tensor.matmul(p_qkv[:, 2 + j, :], xT[r][:, 64 * j:64 * j + P], wqkv[:, 2 * C:3 * C], start=True, stop=True)
                        mm.then_inc(S["qkvp"], 1)
                    if p.has(1):
                        r = p.slot(1)
                        p.wait("qkn", 1)
                        p.wait("logit", 0, 3, 1)
                        p.wait("on", -2, 2)
                        p.wait("x1", -4)
                        for w in range(2):
                            for g in range(GRP):
                                rows = slice(32 * g, 32 * g + 32)
                                mm = nc.tensor.matmul(p_s[64 * w:64 * w + 64, g, 0:P], qn[r][rows, 64 * w:64 * w + 64],
                                                      kn[r][rows, w, :, :], start=True, stop=True)
                        mm.then_inc(S["scores"], 1)
                    if p.has(2):
                        p.wait("sq", 2)
                        p.wait("nmax", 1)
                        nc.tensor.matmul(p_n[:, 0:256], same_head[:, :], sq[p.slot(2)][:, :], start=True, stop=True).then_inc(S["norm"], 1)
                    if p.has(-1):
                        r = p.slot(-1)
                        vb = vbd[(p.u - 1) % PPS]
                        p.wait("pT", -1)
                        p.wait("v", -1)
                        p.wait("logit", 0, 3, 1)
                        p.wait("on", -2, 2)
                        for w in range(2):
                            for g in range(GRP):
                                mm = nc.tensor.matmul(p_O[64 * w:64 * w + 64, g, :], pT[r][:, g, 64 * w:64 * w + 64],
                                                      vb[:, w, g, :], start=True, stop=True)
                        mm.then_inc(S["outp"], 1)
                    if p.has(-2):
                        p.wait("on", -2, 2)
                        p.wait("xT", 2)
                        p.wait("oT", -3)
                        nc.tensor.transpose(p_oT, on[p.slot(-2)][:, :], ident[:, :]).then_inc(S["oTp"], 1)
                    if p.has(3):
                        r = p.slot(3)
                        p.wait("xh", 3)
                        p.wait("xT", 2)
                        p.wait("oT", -3)
                        nc.tensor.transpose(p_xT[:, 0:P], xh[r][:, :], ident[:, :])
                        nc.tensor.transpose(p_xT[:, P:192], xh[r][0:64, :], ident[0:64, 0:64]).then_inc(S["xTp"], 1)
                    if p.has(0):
                        p.wait("prob", 0)
                        p.wait("pT", -1)
                        for g in range(GRP):
                            mm = nc.tensor.transpose(p_pT[:, g, :], pr[p.slot(0)][:, P * g:P * (g + 1)], ident[:, :])
                        mm.then_inc(S["pTp"], 1)
                    if p.has(-3):
                        p.wait("oT", -3)
                        p.wait("logit", 0, 3, 1)
                        p.wait("x1", -4)
                        nc.tensor.matmul(p_proj, oT[p.slot(-3)][:, :], wproj[:, :], start=True, stop=True).then_inc(S["proj"], 1)
                pairs_of(pe, emit)

            @block.gpsimd
            def _(pool):
                def emit(p):
                    if p.has(2):
                        r = p.slot(2)
                        p.wait("qk", 2)
                        p.wait("norm", 0)
                        nc.gpsimd.tensor_tensor(sq[r][:, :], qk[r][:, :], qk[r][:, :], ALU.mult).then_inc(S["sq"], 1)
                pairs_of(pool, emit)

            @block.scalar
            def _(act):
                nc.scalar.preload_act_table_set("natural_log_exp_and_others")
                act.wait_ge(S["consts_in"], 16 * 8)
                nc.scalar.activation(kscale[:, 0:1], consts[:, 1:2], ACT.Exp).then_inc(S["ks"], 1)
                act.wait_ge(S["setup"], 5)

                def xrstd(s, strip):
                    act.wait_ge(S["xstat"], 2 * (strip + 1))
                    nc.scalar.activation(lnv[s][:, :], mv[s][:, :, 1], ACT.Ln, bias=eps[:, 0:1]).then_inc(S["xrstd"], 1)
                    act.wait_ge(S["xrstd"], 2 * strip + 1)
                    nc.scalar.activation(rstd[s][:, :], lnv[s][:, :], ACT.Exp, scale=-0.5).then_inc(S["xrstd"], 1)

                def wrstd(s, strip):
                    act.wait_ge(S["wstat"], strip + 1)
                    nc.scalar.activation(wln[s][:, :], wmv[s][:, :, 1], ACT.Ln, bias=eps[:, 1:2]).then_inc(S["wrstd"], 1)
                    act.wait_ge(S["wrstd"], 2 * strip + 1)
                    nc.scalar.activation(wrs[s][:, :], wln[s][:, :], ACT.Exp, scale=-0.5).then_inc(S["wrstd"], 1)

                def emit(p):
                    if p.u == 0 or p.u == -3:
                        nc.scalar.preload_act_table_set("natural_log_exp_and_others")
                    if p.u == -3 and p.first:
                        xrstd(0, 0)
                    if p.has(2):
                        r = p.slot(2)
                        vb = vbd[(p.u + 2) % PPS]
                        p.wait("qkvp", 2)
                        p.wait("qkn", 0)
                        p.wait("sq", 0)
                        p.wait("outp", -5)
                        nc.scalar.activation(qk[r][:, 0:P], p_qkv[:, 0, :], ACT.Identity, bias=consts[:, 0:1])
                        nc.scalar.activation(qk[r][:, P:2 * P], p_qkv[:, 1, :], ACT.Copy).then_inc(S["qk"], 1)
                        pv = p_qkv[:, 2:4, :].rearrange("p w (g k) -> p w g k", g=GRP)
                        nc.scalar.activation(vb[0:64, :, :, 0:16], pv[0:64, :, :, 0:16], ACT.Copy)
                        nc.scalar.activation(vb[64:128, :, :, 16:32], pv[64:128, ::-1, :, 16:32], ACT.Copy).then_inc(S["v"], 1)
                    if p.has(0):
                        p.wait("logit", 0, 3)
                        p.wait("pTp", -2)
                        nc.scalar.activation(pr[p.slot(0)][:, :], lm[p.slot(0)][:, :, :].rearrange("p h k -> p (h k)"), ACT.Exp).then_inc(S["prob"], 1)
                    if p.has(-2):
                        p.wait("oTp", -2)
                        p.wait("xTp", 3)
                        p.wait("proj", -4)
                        nc.scalar.activation(oT[p.slot(-2)][:, :], p_oT, ACT.Copy).then_inc(S["oT"], 1)
                    if p.has(3):
                        p.wait("xTp", 3)
                        p.wait("qkvp", 1)
                        nc.scalar.activation(xT[p.slot(3)][:, :], p_xT, ACT.Copy).then_inc(S["xT"], 1)
                    if p.has(2):
                        r = p.slot(2)
                        p.wait("nmax", 2)
                        nc.scalar.activation(nl[r][:, :], nm[r][:, :], ACT.Ln).then_inc(S["rs"], 1)
                        p.wait("rs", 2, 2, 1)
                        p.wait("qkn", 0)
                        nc.scalar.activation(rs[r][:, :], nl[r][:, :], ACT.Exp, scale=-0.5).then_inc(S["rs"], 1)
                    if p.has(0):
                        p.wait("pTp", 0)
                        p.wait("outp", -2)
                        nc.scalar.activation(pT[p.slot(0)][:, :, :], p_pT[:, :, :], ACT.Copy).then_inc(S["pT"], 1)
                    strip, s, j = p.strip(0)
                    if j == 3 and p.has(0) and p.has(PPS):
                        p.wait("xh", 3 - PPS)
                        xrstd(1 - s, strip + 1)
                    strip, s, j = p.strip(-3)
                    if j == PPS - 1 and p.has(-3):
                        wrstd(s, strip)
                pairs_of(act, emit)

            @block.vector
            def _(v):
                nc.vector.memset(eps[:, 0:1], 1e-6)
                nc.vector.memset(eps[:, 1:2], 1e-5)
                nc.vector.memset(ones[:, :], 1.0)
                for i in range(PPS):
                    nc.vector.memset(vbd[i][:, :, :, :], 0.0)
                nc.vector.memset(vb_cols[:, :], 0.0).then_inc(S["setup"], 1)
                v.wait_ge(S["setup"], 1)
                for i in range(PPS):
                    nc.vector.memset(vbd[i][0:64, :, :, 32:33], 1.0)
                    nc.vector.memset(vbd[i][64:128, :, :, 33:34], 1.0)
                v.wait_ge(S["consts_in"], 16 * 8)
                nc.vector.tensor_scalar(vb_cols[:, :], vb_cols[:, :], consts[:, 5:6], None, ALU.add).then_inc(S["setup"], 1)
                nc.vector.tensor_reduce(nswr[:, 0:1], wr[:, :], AX_X, ALU.add).then_inc(S["setup"], 1)
                v.wait_ge(S["setup"], 3)
                v.wait_ge(S["ks"], 1)
                nc.vector.tensor_scalar(nswr[:, 1:2], nswr[:, 0:1], -1.0, None, ALU.mult)
                for e in range(2):
                    nc.vector.tensor_scalar(kscale[:, 1 + e:2 + e], kscale[:, 0:1], consts[:, 2 + e:3 + e], None, ALU.mult).then_inc(S["setup"], 1)
                v.wait_ge(S["beff_p"], 1)
                nc.vector.tensor_copy(beff[:, :], p_proj).then_inc(S["setup"], 1)
                v.wait_ge(S["setup"], 6)

                def stats(s, strip):
                    v.wait_ge(S[f"x_in{s}"], (strip // 2 + 1) * 16 if isinstance(strip, int) else (strip >> 1) * 16 + 16)
                    for j in range(PPS):
                        ins = nc.vector.bn_stats(st[s][:, j, :], xs[s][:, j, :])
                    ins.then_inc(S["xstat"], 1)
                    v.wait_ge(S["xstat"], 2 * strip + 1)
                    v.sem_inc(S["passed"], 1)
                    for j in range(PPS):
                        ins = nc.vector.bn_aggr(mv[s][:, j, :], st[s][:, j, :])
                    ins.then_inc(S["xstat"], 1)
                    be = beff[:, :].rearrange("p (o c) -> p o c", o=1).to_broadcast([P, PPS, C])
                    nc.vector.tensor_tensor(xb[s][:, :, :], xs[s][:, :, :], be, ALU.add).then_inc(S["xb"], 1)

                def score(s, strip):
                    v.wait_ge(S["wrstd"], 2 * (strip + 1))
                    nc.vector.scalar_tensor_tensor(wtmp[s][:, 0, :], wmv[s][:, :, 0], nswr[:, 1:2], wdot[s][:, :],
                                                   ALU.mult, ALU.add).then_inc(S["score"], 1)
                    v.wait_ge(S["score"], 3 * strip + 1)
                    nc.vector.tensor_tensor(wtmp[s][:, 1, :], wtmp[s][:, 0, :], wrs[s][:, :], ALU.mult).then_inc(S["score"], 1)
                    v.wait_ge(S["score"], 3 * strip + 2)
                    nc.vector.tensor_copy(stats_sb[:, bass.ds(strip * PPS, PPS), 0], wmv[s][:, :, 0])
                    nc.vector.tensor_copy(stats_sb[:, bass.ds(strip * PPS, PPS), 1], wrs[s][:, :])
                    nc.vector.tensor_scalar(score_sb[:, bass.ds(strip * PPS, PPS)], wtmp[s][:, 1, :], consts[:, 4:5], None,
                                            ALU.add).then_inc(S["score"], 1)

                def emit(p):
                    if p.u == -3 and p.first:
                        stats(0, 0)
                    if p.has(0):
                        q = p.slot(0)
                        strip, _, j = p.strip(0)
                        p.wait("scores", 0)
                        p.wait("prob", -2)
                        bias = bm[:, bass.ds(last_row(v, strip) * 2 + int(j == PPS - 1), 1), :].rearrange("p o (g k) -> p (o g) k", g=GRP)
                        nc.vector.tensor_tensor(lg[q][:, :, :].rearrange("p (g e) k -> p g (e k)", g=GRP),
                                                p_s[:, :, 0:P], bias, ALU.add).then_inc(S["logit"], 1)
                        p.wait("logit", 0, 3, 1)
                        nc.vector.tensor_reduce(mx[q][:, :], lg[q][:, :, :], AX_X, ALU.max).then_inc(S["logit"], 1)
                        p.wait("logit", 0, 3, 2)
                        top = mx[q][:, :].rearrange("p (h o) -> p h o", o=1).to_broadcast([P, HEADS, 64])
                        nc.vector.tensor_tensor(lm[q][:, :, :], lg[q][:, :, :], top, ALU.subtract).then_inc(S["logit"], 1)
                    if p.has(3):
                        strip, s, j = p.strip(3)
                        if j == 0 or p.u == -3:
                            v.wait_ge(S["xrstd"], 2 * (strip + 1))
                        p.wait("xTp", 1)
                        nc.vector.tensor_scalar(xh[p.slot(3)][:, :], xs[s][:, j, :], mv[s][:, j, 0:1], rstd[s][:, j:j + 1],
                                                ALU.subtract, ALU.mult).then_inc(S["xh"], 1)
                    if p.has(2):
                        p.wait("norm", 2)
                        p.wait("rs", 0, 2)
                        nc.vector.tensor_scalar(nm[p.slot(2)][:, :], p_n[:, 0:256], QK_EPS, None, ALU.max).then_inc(S["nmax"], 1)
                    if p.has(-1):
                        r = p.slot(-1)
                        p.wait("outp", -1)
                        p.wait("oTp", -3)
                        nc.vector.reciprocal(rc[r][:, :].rearrange("p (g e) -> p g e", g=GRP), p_O[:, :, 32:34]).then_inc(S["on"], 1)
                        p.wait("on", -1, 2, 1)
                        rr = rc[r][:, :].rearrange("p (g e o) -> p g e o", g=GRP, o=1).to_broadcast([P, GRP, 2, HD])
                        nc.vector.tensor_tensor(on[r][:, :].rearrange("p (g e c) -> p g e c", g=GRP, e=2),
                                                p_O[:, :, 0:32].rearrange("p g (e c) -> p g e c", e=2), rr, ALU.mult).then_inc(S["on"], 1)
                    if p.has(2):
                        r = p.slot(2)
                        p.wait("rs", 2, 2)
                        p.wait("qk", 2)
                        p.wait("scores", 0)
                        nc.vector.tensor_tensor(qn[r][:, :], qk[r][:, 0:P], rs[r][:, 0:P], ALU.mult)
                        for e in range(2):
                            ins = nc.vector.scalar_tensor_tensor(
                                kn[r][:, :, e, :], qk[r][:, P:2 * P].rearrange("p (w k) -> p w k", w=2), kscale[:, 1 + e:2 + e],
                                rs[r][:, P:2 * P].rearrange("p (w k) -> p w k", w=2), ALU.mult, ALU.mult)
                        ins.then_inc(S["qkn"], 1)
                    if p.has(-3):
                        strip, s, j = p.strip(-3)
                        p.wait("proj", -3)
                        if j == 0 and not (p.first and p.u - 3 < HALF):
                            v.wait_ge(S[f"x_out{s}"], (p.s0 >> 1) * 16)
                        nc.vector.tensor_tensor(x1[s][:, j, :], p_proj, xb[s][:, j, :], ALU.add).then_inc(S["x1"], 1)
                        p.wait("x1", -3)
                        nc.vector.tensor_tensor_reduce(out=junk[p.slot(-3)][:, :], in0=x1[s][:, j, :], in1=wr[:, :], scale=1.0, scalar=0.0,
                                                       op0=ALU.mult, op1=ALU.add, accum_out=wdot[s][:, j:j + 1])
                        nc.vector.bn_stats(wst[s][:, j, :], x1[s][:, j, :]).then_inc(S["dot"], 1)
                        if j == PPS - 1:
                            p.wait("dot", -3)
                            v.sem_inc(S["passed"], 1)
                            for j in range(PPS):
                                ins = nc.vector.bn_aggr(wmv[s][:, j, :], wst[s][:, j, :])
                            ins.then_inc(S["wstat"], 1)
                            if p.last and p.u == HALF + 2:
                                score(s, strip)
                    strip, s, j = p.strip(0)
                    if j == 3 and p.has(0) and p.has(PPS):
                        stats(1 - s, strip + 1)
                    if j == 4 and not (p.first and p.u < PPS) and p.u < HALF:
                        score(1 - s, strip - 1)
                pairs_of(v, emit)
        clear(nc, S.values())


TPI = H * W
KSEL = TPI // 2 - 1
CPI = TPI // P
MAGIC = 1.5 * 2 ** 23
PADW = W + 2
X2_OUT = 2 * PPS * 16


def select_tokens(nc, d, score_sb, gate_sb):
    with ExitStack() as ctx:
        def sb(name, shape, dt=F32):
            return ctx.enter_context(nc.sbuf_tensor("se_" + name, shape, dt))

        ones = sb("ones", [P, P])
        ridx = sb("ridx", [P, PAIRS])
        cmp = sb("cmp", [P, PAIRS])
        ws = sb("ws", [P, PAIRS])
        tie = sb("tie", [P, PAIRS])
        cnt = sb("cnt", [P, B])
        sgn = sb("sgn", [P, B])
        need = sb("need", [P, B])
        cur = sb("cur", [P, B], I32)
        cand = sb("cand", [P, B], I32)
        keep = sb("keep", [P, B], I32)
        thr = sb("thr", [P, B])
        cut = sb("cut", [P, B])
        cutc = sb("cutc", [P, B])
        tot = ctx.enter_context(nc.psum_tensor("se_tot", [P, B], F32))
        loaded, counted, summed = (ctx.enter_context(nc.semaphore("se_" + n)) for n in ("loaded", "counted", "summed"))
        step = Steps(ctx.enter_context(nc.semaphore("se_step")))
        TRIPS = 1 + 31 + 1 + 14

        with nc.Block() as block:
            @block.sync
            def _(sp):
                sp.dma_start(ridx[:, :], d["raster"]).then_inc(loaded, 16)

            @block.tensor
            def _(pe):
                for n in range(TRIPS):
                    pe.wait_ge(counted, n + 1)
                    nc.tensor.matmul(tot[:, :], ones[:, :], cnt[:, :], start=True, stop=True).then_inc(summed, 1)

            @block.vector
            def _(v):
                trips = [0]

                def do(ins):
                    v.wait_ge(step.sem, step.done_by(ins))

                def cols(t, b):
                    return t[:, CPI * b:CPI * (b + 1)]

                def count(values, limit, op):
                    for b in range(B):
                        ins = nc.vector.tensor_scalar(cols(cmp, b), cols(values, b), limit(b), None, op, ALU.add, accum_out=cnt[:, b:b + 1])
                    ins.then_inc(counted, 1)
                    trips[0] += 1
                    v.wait_ge(summed, trips[0])

                def bit_column(t):
                    return lambda b: t[:, b:b + 1]

                do(nc.vector.memset(ones[:, :], 1.0))
                v.wait_ge(loaded, 16)
                count(score_sb, lambda b: 0.0, ALU.is_ge)
                do(nc.vector.tensor_scalar(sgn[:, :], tot[:, :], float(KSEL), 2.0, ALU.is_ge, ALU.mult))
                do(nc.vector.tensor_scalar(sgn[:, :], sgn[:, :], 1.0, None, ALU.subtract))
                mid, half = (TPI + 1) / 2, KSEL - (TPI + 1) / 2
                do(nc.vector.tensor_scalar(need[:, :], sgn[:, :], half, mid, ALU.mult, ALU.add))
                for b in range(B):
                    ins = nc.vector.tensor_scalar(cols(ws, b), cols(score_sb, b), sgn[:, b:b + 1], None, ALU.mult)
                do(ins)
                do(nc.vector.memset(cur[:, :], 0))
                for bit in range(30, -1, -1):
                    do(nc.vector.tensor_scalar(cand[:, :], cur[:, :], 1 << bit, None, ALU.bitwise_or))
                    count(ws, lambda b: cand[:, b:b + 1].bitcast(F32), ALU.is_ge)
                    do(nc.vector.tensor_tensor(keep[:, :], tot[:, :], need[:, :], ALU.is_ge))
                    do(nc.vector.scalar_tensor_tensor(cur[:, :], keep[:, :], bit, cur[:, :], ALU.logical_shift_left, ALU.bitwise_or))
                do(nc.vector.tensor_tensor(thr[:, :], cur[:, :].bitcast(F32), sgn[:, :], ALU.mult))
                count(score_sb, bit_column(thr), ALU.is_gt)
                do(nc.vector.tensor_scalar(need[:, :], tot[:, :], -1.0, float(KSEL), ALU.mult, ALU.add))
                for b in range(B):
                    ins = nc.vector.tensor_scalar(cols(tie, b), cols(score_sb, b), thr[:, b:b + 1], 1e6, ALU.not_equal, ALU.mult)
                do(ins)
                do(nc.vector.tensor_tensor(tie[:, :], tie[:, :], ridx[:, :], ALU.add))
                do(nc.vector.memset(cut[:, :], 0.0))
                for bit in range(13, -1, -1):
                    do(nc.vector.tensor_scalar(cutc[:, :], cut[:, :], float(1 << bit), None, ALU.add))
                    count(tie, bit_column(cutc), ALU.is_lt)
                    do(nc.vector.tensor_tensor(cutc[:, :], tot[:, :], need[:, :], ALU.is_lt))
                    do(nc.vector.scalar_tensor_tensor(cut[:, :], cutc[:, :], float(1 << bit), cut[:, :], ALU.mult, ALU.add))
                for b in range(B):
                    nc.vector.tensor_scalar(cols(cmp, b), cols(score_sb, b), thr[:, b:b + 1], None, ALU.is_gt)
                    ins = nc.vector.tensor_scalar(cols(tie, b), cols(tie, b), cut[:, b:b + 1], None, ALU.is_le)
                do(ins)
                do(nc.vector.tensor_tensor(cmp[:, :], cmp[:, :], tie[:, :], ALU.add))
                do(nc.vector.tensor_tensor(gate_sb[:, :], cmp[:, :], score_sb[:, :], ALU.mult))
        clear(nc, (loaded, counted, summed, step.sem))


class Trip:

    def __init__(self, eng, sems, count, span, i, u):
        self.eng, self.sems, self.count, self.span, self.i, self.u = eng, sems, count, span, i, u
        self.t = i * span + u

    def next(self):
        return Trip(self.eng, self.sems, self.count, self.span, self.i, self.u + 1)

    def has(self, off):
        return not isinstance(self.t, int) or 0 <= self.t + off < self.count

    def wait(self, name, off, per=1, k=None):
        if self.has(off):
            self.eng.wait_ge(self.sems[name], (self.t + off) * per + (per if k is None else k))

    def wait_slot(self, name, off):
        self.wait_lot(name, off, 16)

    def wait_lot(self, name, off, lot):
        if self.has(off):
            self.eng.wait_ge(self.sems[f"{name}{self.slot(off)}"], self.turns(off) * lot)

    def turns(self, off):
        return self.i * (self.span // 2) + ((self.u + off) // 2 + 1)

    def slot(self, off):
        return (self.u + off) % 2


def trips(eng, sems, count, span, ahead, behind, emit, peel=1):
    for t in range(-ahead, peel * span):
        emit(Trip(eng, sems, count, span, t // span, t % span))
    with eng.Fori(peel, count // span - 1) as i:
        for u in range(span):
            emit(Trip(eng, sems, count, span, i, u))
    for t in range(count - span, count + behind):
        emit(Trip(eng, sems, count, span, t // span, t % span))


def image_rows(nc, strip, half, rows):
    if isinstance(strip, int):
        b, i = strip // SPI, strip % SPI
        return b * PADW + (WIN * i + SHIFT + SHIFT * half) % H
    row = strip * WIN + ((strip * 147) >> 11) * 2 + SHIFT + SHIFT * half
    if half:
        row = row - last_row(None, strip) * H
    return nc.s_assert_within(row, 0, B * PADW - rows, skip_runtime_bounds_check_because="strip < STRIPS")


def token_row(nc, strip, half):
    if isinstance(strip, int):
        b, i = strip // SPI, strip % SPI
        return b * H + (WIN * i + SHIFT + SHIFT * half) % H
    row = strip * WIN + SHIFT + SHIFT * half
    if half:
        row = row - last_row(None, strip) * H
    return nc.s_assert_within(row, 0, B * H - SHIFT, skip_runtime_bounds_check_because="strip < STRIPS")


def routed_ffn(nc, d, x1_dram, x2_dram, stats_sb, gate_sb, pixels):
    HID = 4 * C
    with ExitStack() as ctx:
        def sb(name, shape, dt=F32):
            return ctx.enter_context(nc.sbuf_tensor("ff_" + name, shape, dt))

        def two(name, shape, dt=F32):
            return [sb(f"{name}{i}", shape, dt) for i in range(2)]

        def ps(name, shape, dt=F32):
            return ctx.enter_context(nc.psum_tensor("ff_" + name, shape, dt))

        ident = sb("ident", [P, P])
        identb = sb("identb", [P, P], BF16)
        w1 = sb("w1", [P, HID])
        w2 = sb("w2", [P, 4, C])
        b1 = sb("b1", [P, 4])
        b2 = sb("b2", [1, C])
        ones = sb("ones", [1, P])
        half = sb("half", [P, PPS])
        x1, t1, t12, x2 = (two(n, [P, PPS, C]) for n in ("x1", "t1", "t12", "x2"))
        tT = two("tT", [P, PPS * P])
        gate = two("gate", [P, PPS])
        hT = [sb(f"hT{h}", [P, 4, 448]) for h in range(2)]
        st = two("st", [P, PPS, 6])
        mv = two("mv", [P, PPS, 2])
        ve = two("ve", [P, PPS])
        rstd = two("rstd", [P, PPS])
        xq = two("xq", [P, PPS, C])
        xi = two("xi", [P, PPS, C], BF16)
        p_t = [ps(f"p_t{i}", [P, 512]) for i in range(2)]
        p_h = [ps(f"p_h{i}", [P, 512]) for i in range(2)]
        p_y = [ps(f"p_y{i}", [P, 4, P]) for i in range(2)]
        p_q = ps("p_q", [P, 1024], BF16)
        S = {n: ctx.enter_context(nc.semaphore("ff_" + n)) for n in (
            "consts_in", "ready", "x_in0", "x_in1", "x_out0", "x_out1", "t1", "t12", "trp", "tT", "hp", "hT", "yp",
            "x2", "stat", "ve", "rstd", "xq", "xi", "qp", "pix", "passed")}
        groups = ((0, 4), (4, 7))

        with nc.Block() as block:
            @block.sync
            def _(sp):
                for dst, src in ((ident[:, :], d["ident"]), (w1[:, :], d["f_w1"]), (w2[:, :, :], d["f_w2"]),
                                 (b1[:, :], d["f_b1"]), (b2[:, :], d["f_b2"])):
                    sp.dma_start(dst, src).then_inc(S["consts_in"], 16)

                def emit(p):
                    if p.has(2):
                        p.wait("t1", 0)
                        p.wait("t12", 0)
                        sp.dma_start(x1[p.slot(2)][:, :, :], x1_dram[bass.ds(p.t + 2, 1)].rearrange("o p u c -> (o p) u c")).then_inc(S[f"x_in{p.slot(2)}"], 16)
                    if p.has(0):
                        p.wait("x2", 0, 2)
                        s = p.slot(0)
                        for w in range(2):
                            for j in range(PPS):
                                dst = bass.AP(x2_dram.tensor, p.t * (W * WIN * C) + (2 * j + w) * WIN * WIN * C,
                                              [[C, WIN], [WIN * C, WIN], [1, C]])
                                sp.dma_start(dst, x2[s][64 * w:64 * w + 64, j, :]).then_inc(S[f"x_out{s}"], 16)
                trips(sp, S, STRIPS, 2, 2, 0, emit)
                for s in range(2):
                    sp.wait_ge(S[f"x_out{s}"], X2_OUT * (STRIPS // 2))

            @block.tensor
            def _(pe):
                pe.wait_ge(S["consts_in"], 16 * 5)
                pe.wait_ge(S["ready"], 1)

                def emit(p):
                    if p.has(0):
                        s = p.slot(0)
                        for n in range(8):
                            h, m = n // 4, n % 4
                            p.wait("tT", 0, 2)
                            if n < 2:
                                p.wait("hT", -1, 8, 7 + n)
                            else:
                                p.wait("hT", 0, 8, n - 1)
                            nc.tensor.matmul(p_h[n % 2][:, 0:448], w1[:, P * m:P * (m + 1)], tT[s][:, 448 * h:448 * h + 448],
                                             start=True, stop=True).then_inc(S["hp"], 1)
                    if p.has(1):
                        for g, (a, b) in enumerate(groups):
                            p.wait("t1", 1)
                            p.wait("tT", 0, 2, g + 1)
                            for j in range(a, b):
                                mm = nc.tensor.transpose(p_t[g][:, P * (j - a):P * (j - a + 1)], t1[p.slot(1)][:, j, :], ident[:, :])
                            mm.then_inc(S["trp"], 1)
                    if p.has(0):
                        for g, (a, b) in enumerate(groups):
                            p.wait("x2", -1, 2, g + 1)
                            for j in range(a, b):
                                p.wait("hT", 0, 8, 4 if (j + 1) * P <= 448 else 8)
                                for m in range(4):
                                    lo, hi = j * P, (j + 1) * P
                                    for h in range(2):
                                        x, y = max(lo, 448 * h), min(hi, 448 * h + 448)
                                        if x < y and hi - lo == y - x:
                                            nc.tensor.matmul(p_y[g][:, j - a, :], hT[h][:, m, x - 448 * h:y - 448 * h], w2[:, m, :],
                                                             start=m == 0, stop=False)
                                        elif x < y:
                                            nc.tensor.matmul(p_y[g][x - lo:y - lo, j - a, :], hT[h][:, m, x - 448 * h:y - 448 * h], w2[:, m, :],
                                                             start=m == 0, stop=False)
                                mm = nc.tensor.matmul(p_y[g][:, j - a, :], ones[:, :], b2[:, :], start=False, stop=True)
                            mm.then_inc(S["yp"], 1)
                    if p.has(-1):
                        p.wait("xi", -1)
                        p.wait("pix", -2)
                        for j in range(PPS):
                            mm = nc.tensor.transpose(p_q[:, P * j:P * (j + 1)], xi[p.slot(-1)][:, j, :], identb[:, :])
                        mm.then_inc(S["qp"], 1)
                trips(pe, S, STRIPS, 2, 1, 1, emit)

            @block.gpsimd
            def _(pool):
                def emit(p):
                    if p.has(1):
                        s = p.slot(1)
                        p.wait("t1", 1)
                        p.wait("x2", -1, 2)
                        nc.gpsimd.tensor_tensor(t12[s][:, :, :], x1[s][:, :, :], t1[s][:, :, :], ALU.add).then_inc(S["t12"], 1)
                    if p.has(0):
                        s = p.slot(0)
                        p.wait("ve", 0)
                        nc.gpsimd.tensor_tensor(rstd[s][:, :], ve[s][:, :], half[:, :], ALU.pow).then_inc(S["rstd"], 1)
                trips(pool, S, STRIPS, 2, 1, 1, emit)

            @block.scalar
            def _(act):
                act.wait_ge(S["consts_in"], 16 * 5)

                def emit(p):
                    if p.has(0):
                        s = p.slot(0)
                        for n in range(8):
                            h, m = n // 4, n % 4
                            p.wait("hp", 0, 8, n + 1)
                            if n % 4 == 0:
                                p.wait("yp", -1, 2, h + 1)
                            nc.scalar.activation(hT[h][:, m, :], p_h[n % 2][:, 0:448], ACT.Gelu_apprx_tanh, bias=b1[:, m:m + 1]).then_inc(S["hT"], 1)
                    if p.has(1):
                        for g, (a, b) in enumerate(groups):
                            p.wait("trp", 1, 2, g + 1)
                            p.wait("hp", -1, 8)
                            nc.scalar.activation(tT[p.slot(1)][:, P * a:P * b], p_t[g][:, 0:P * (b - a)], ACT.Copy).then_inc(S["tT"], 1)
                    if p.has(-1):
                        p.wait("qp", -1)
                        q = p_q[:, 0:PPS * P].rearrange("p (k r c) -> p r k c", k=14, r=WIN)
                        for hf in range(2):
                            rows = pixels[:, bass.ds(image_rows(nc, p.t - 1, hf, 6) + 1, SHIFT), :]
                            src = q[:, SHIFT * hf:SHIFT * hf + SHIFT, :, :]
                            nc.scalar.activation(rows[:, :, 5:109].rearrange("p r (k c) -> p r k c", c=WIN), src[:, :, 0:13, :], ACT.Copy)
                            nc.scalar.activation(rows[:, :, 109:113], src[:, :, 13, 0:4], ACT.Copy)
                            ins = nc.scalar.activation(rows[:, :, 1:5], src[:, :, 13, 4:8], ACT.Copy)
                        ins.then_inc(S["pix"], 1)
                trips(act, S, STRIPS, 2, 1, 1, emit)

            @block.vector
            def _(v):
                nc.vector.memset(pixels[:, 0:B * PADW:PADW, :], 0.0)
                nc.vector.memset(pixels[:, PADW - 1:B * PADW:PADW, :], 0.0)
                inner = pixels[:, :, :].rearrange("p (b y) x -> p b y x", b=B)[:, :, 1:PADW - 1, :]
                nc.vector.memset(inner[:, :, :, 0:1], 0.0)
                nc.vector.memset(inner[:, :, :, PADW - 1:PADW], 0.0)
                nc.vector.memset(half[:, :], -0.5)
                nc.vector.memset(ones[:, :], 1.0)
                v.wait_ge(S["consts_in"], 16 * 5)
                nc.vector.tensor_copy(identb[:, :], ident[:, :]).then_inc(S["ready"], 1)
                v.wait_ge(S["ready"], 1)

                def emit(p):
                    if p.has(1):
                        s = p.slot(1)
                        p.wait_slot("x_in", 1)
                        p.wait("trp", -1, 2)
                        p.wait("t12", -1)
                        for j in range(PPS):
                            col = stats_sb[:, bass.ds((p.t + 1) * PPS + j, 1), :].rearrange("p o k -> p (o k)")
                            ins = nc.vector.tensor_scalar(t1[s][:, j, :], x1[s][:, j, :], col[:, 0:1], col[:, 1:2], ALU.subtract, ALU.mult)
                        ins.then_inc(S["t1"], 1)
                        nc.vector.tensor_copy(gate[s][:, :], gate_sb[:, bass.ds((p.t + 1) * PPS, PPS)])
                    if p.has(-1):
                        s = p.slot(-1)
                        p.wait("rstd", -1)
                        nc.vector.tensor_scalar(rstd[s][:, :], rstd[s][:, :], 3.0, None, ALU.mult).then_inc(S["xq"], 1)
                        p.wait("xq", -1, 3, 1)
                        for j in range(PPS):
                            ins = nc.vector.tensor_scalar(xq[s][:, j, :], x2[s][:, j, :], mv[s][:, j, 0:1], rstd[s][:, j:j + 1], ALU.subtract, ALU.mult)
                        ins.then_inc(S["xq"], 1)
                        p.wait("xq", -1, 3, 2)
                        nc.vector.tensor_scalar(xq[s][:, :, :], xq[s][:, :, :], 0.0, 3.0, ALU.max, ALU.min).then_inc(S["xq"], 1)
                        p.wait("xq", -1, 3, 3)
                        p.wait("qp", -3)
                        nc.vector.tensor_scalar(xi[s][:, :, :], xq[s][:, :, :], MAGIC, MAGIC, ALU.add, ALU.subtract).then_inc(S["xi"], 1)
                    if p.has(0):
                        s = p.slot(0)
                        p.wait("t12", 0)
                        p.wait_lot("x_out", -2, X2_OUT)
                        for g, (a, b) in enumerate(groups):
                            p.wait("yp", 0, 2, g + 1)
                            for j in range(a, b):
                                ins = nc.vector.scalar_tensor_tensor(x2[s][:, j, :], p_y[g][:, j - a, :], gate[s][:, j:j + 1], t12[s][:, j, :], ALU.mult, ALU.add)
                            ins.then_inc(S["x2"], 1)
                        p.wait("x2", 0, 2)
                        for j in range(PPS):
                            ins = nc.vector.bn_stats(st[s][:, j, :], x2[s][:, j, :])
                        ins.then_inc(S["stat"], 1)
                        p.wait("stat", 0, 2, 1)
                        v.sem_inc(S["passed"], 1)
                        for j in range(PPS):
                            ins = nc.vector.bn_aggr(mv[s][:, j, :], st[s][:, j, :])
                        ins.then_inc(S["stat"], 1)
                        p.wait("stat", 0, 2)
                        nc.vector.tensor_scalar(ve[s][:, :], mv[s][:, :, 1], 1e-6, None, ALU.add).then_inc(S["ve"], 1)
                trips(v, S, STRIPS, 2, 1, 1, emit, peel=2)
        clear(nc, S.values())


TAPS = 9
ROWS = WIN
HROWS = ROWS // 2
FEAT = 16
GH = 4
REC = FEAT + 2 * GH


def convolve(nc, d, pixels, x2_dram, x3_dram, tT_dram, rec_dram, recs_dram):
    with ExitStack() as ctx:
        def sb(name, shape, dt=F32):
            return ctx.enter_context(nc.sbuf_tensor("co_" + name, shape, dt))

        def two(name, shape, dt=F32):
            return [sb(f"{name}{i}", shape, dt) for i in range(2)]

        def ps(name, shape, dt=F32):
            return ctx.enter_context(nc.psum_tensor("co_" + name, shape, dt))

        ident = sb("ident", [P, P])
        w = sb("w", [P, TAPS, C])
        wt = sb("wt", [P, TAPS, C])
        wq = sb("wq", [P, TAPS, C], BF16)
        ext = sb("ext", [P, 4])
        gat = sb("gat", [P, 3, FEAT])
        att = sb("att", [P, 2, FEAT])
        wcat = sb("wcat", [P, REC])
        half = sb("half", [P, ROWS])
        win = two("win", [P, 2, HROWS + 2, PADW], BF16)
        x2, x3, t = (two(n, [W, ROWS, C]) for n in ("x2", "x3", "t"))
        st = two("st", [W, ROWS, 6])
        mv = two("mv", [W, ROWS, 2])
        ve = two("ve", [W, ROWS])
        rstd = two("rstd", [W, ROWS])
        tT = two("tT", [P, ROWS, W])
        rec = two("rec", [W, ROWS, REC])
        p_c = [ps(f"p_c{i}", [W, HROWS, P]) for i in range(2)]
        p_t = [ps(f"p_t{i}", [P, HROWS, W]) for i in range(2)]
        p_r = ps("p_r", [W, ROWS, REC])
        S = {n: ctx.enter_context(nc.semaphore("co_" + n)) for n in (
            "consts_in", "tanh", "ext", "top", "wq", "x_in0", "x_in1", "out0", "out1", "win", "conv", "x3", "stat", "ve",
            "rstd", "t", "trp", "tT", "recp", "rec", "passed")}

        with nc.Block() as block:
            @block.sync
            def _(sp):
                for dst, src in ((w[:, :, :], d["c_w"].rearrange("t i o -> i t o")), (ident[:, :], d["ident"]),
                                 (gat[:, 0, :], d["g_wgat"]), (att[:, :, :], d["g_att"])):
                    sp.dma_start(dst, src).then_inc(S["consts_in"], 16)

                def emit(p):
                    if p.has(1):
                        s = p.slot(1)
                        p.wait("x3", -1, 2)
                        base = (p.t + 1) * (W * ROWS * C)
                        for lo, n, c0 in ((SHIFT, W - SHIFT, 0), (0, SHIFT, W - SHIFT)):
                            src = bass.AP(x2_dram.tensor, base + c0 * ROWS * C, [[ROWS * C, n], [1, ROWS * C]])
                            sp.dma_start(x2[s][lo:lo + n, :, :].rearrange("p r c -> p (r c)"), src).then_inc(S[f"x_in{s}"], 16)
                    if p.has(-1):
                        s = p.slot(-1)
                        p.wait("rec", -1)
                        p.wait("tT", -1, 2)
                        sp.dma_start(tT_dram[:, bass.ds((p.t - 1) * (ROWS * W), ROWS * W)],
                                     tT[s][:, :, :].rearrange("p r x -> p (r x)")).then_inc(S[f"out{s}"], 16)
                        for dram, tile in ((x3_dram, x3), (recs_dram, rec)):
                            dst = dram.rearrange("(y x) c -> x y c", x=W)[:, bass.ds((p.t - 1) * ROWS, ROWS), :]
                            sp.dma_start(dst, tile[s][:, :, :]).then_inc(S[f"out{s}"], 16)
                        for h in range(2):
                            dst = rec_dram.rearrange("(y x) c -> x y c", x=W)[:, bass.ds(token_row(nc, p.t - 1, h), HROWS), :]
                            sp.dma_start(dst, rec[s][:, HROWS * h:HROWS * h + HROWS, :]).then_inc(S[f"out{s}"], 16)
                trips(sp, S, STRIPS, 2, 1, 1, emit)
                for s in range(2):
                    sp.wait_ge(S[f"out{s}"], CONV_OUT * (STRIPS // 2))

            @block.tensor
            def _(pe):
                pe.wait_ge(S["consts_in"], 16 * 4)
                pe.wait_ge(S["wq"], 7)

                def emit(p):
                    if p.has(0):
                        s = p.slot(0)
                        p.wait("win", 0)
                        for h in range(2):
                            p.wait("x3", -1, 2, h + 1)
                            for r in range(HROWS):
                                for k in range(TAPS):
                                    dy, dx = k // 3, k % 3
                                    mm = nc.tensor.matmul(p_c[h][:, r, :], win[s][:, h, r + dy, dx:dx + W], wq[:, k, :],
                                                          start=k == 0, stop=k == TAPS - 1)
                            mm.then_inc(S["conv"], 1)
                    if p.has(-1):
                        s = p.slot(-1)
                        p.wait("t", -1)
                        for h in range(2):
                            p.wait("tT", -2, 2, h + 1)
                            for r in range(HROWS):
                                mm = nc.tensor.transpose(p_t[h][:, r, :], t[s][:, HROWS * h + r, :], ident[0:W, 0:W])
                            mm.then_inc(S["trp"], 1)
                        p.wait("tT", -1, 2)
                        p.wait("rec", -2)
                        for r in range(ROWS):
                            mm = nc.tensor.matmul(p_r[:, r, :], tT[s][:, r, :], wcat[:, :], start=True, stop=True)
                        mm.then_inc(S["recp"], 1)
                trips(pe, S, STRIPS, 2, 1, 1, emit)

            @block.gpsimd
            def _(pool):
                pool.wait_ge(S["ext"], 3)
                nc.gpsimd.partition_all_reduce(ext[:, 3:4], ext[:, 2:3], P, bass.bass_isa.ReduceOp.max).then_inc(S["top"], 1)

                def emit(p):
                    if p.has(1):
                        s = p.slot(1)
                        p.wait("conv", -1, 2)
                        for h in range(2):
                            ins = nc.gpsimd.tensor_copy(win[s][:, h, :, :], pixels[:, bass.ds(image_rows(nc, p.t + 1, h, HROWS + 2), HROWS + 2), :])
                        ins.then_inc(S["win"], 1)
                    if p.has(0):
                        s = p.slot(0)
                        p.wait("ve", 0)
                        nc.gpsimd.tensor_tensor(rstd[s][:, :], ve[s][:, :], half[0:W, :], ALU.pow).then_inc(S["rstd"], 1)
                trips(pool, S, STRIPS, 2, 1, 1, emit)

            @block.scalar
            def _(act):
                act.wait_ge(S["consts_in"], 16 * 4)
                nc.scalar.activation(wt[:, :, :], w[:, :, :], ACT.Tanh).then_inc(S["tanh"], 1)

                def emit(p):
                    if p.has(-1):
                        s = p.slot(-1)
                        for h in range(2):
                            p.wait("trp", -1, 2, h + 1)
                            if h == 0:
                                p.wait_lot("out", -3, CONV_OUT)
                            nc.scalar.activation(tT[s][:, HROWS * h:HROWS * h + HROWS, :], p_t[h][:, :, :], ACT.Copy).then_inc(S["tT"], 1)
                        p.wait("recp", -1)
                        nc.scalar.activation(rec[s][:, :, :], p_r[:, :, :], ACT.Copy).then_inc(S["rec"], 1)
                trips(act, S, STRIPS, 2, 1, 1, emit, peel=2)

            @block.vector
            def _(v):
                nc.vector.memset(half[:, :], -0.5)
                v.wait_ge(S["consts_in"], 16 * 4)
                for k in range(2):
                    nc.vector.tensor_tensor(gat[:, 1 + k, :], gat[:, 0, :], att[:, k, :], ALU.mult)
                nc.vector.tensor_copy(wcat[:, 0:FEAT], gat[:, 0, :]).then_inc(S["wq"], 1)
                v.wait_ge(S["wq"], 1)
                nc.vector.tensor_reduce(wcat[:, FEAT:FEAT + 2 * GH].rearrange("p (k h) -> p k h", k=2),
                                        gat[:, 1:3, :].rearrange("p k (h e) -> p k h e", e=GH), AX_X, ALU.add).then_inc(S["wq"], 1)
                v.wait_ge(S["tanh"], 1)
                nc.vector.tensor_reduce(ext[:, 0:1], wt[:, :, :].rearrange("p t c -> p (t c)"), AX_X, ALU.max)
                nc.vector.tensor_reduce(ext[:, 1:2], wt[:, :, :].rearrange("p t c -> p (t c)"), AX_X, ALU.min).then_inc(S["ext"], 1)
                v.wait_ge(S["ext"], 1)
                nc.vector.tensor_scalar(ext[:, 1:2], ext[:, 1:2], -1.0, None, ALU.mult).then_inc(S["ext"], 1)
                v.wait_ge(S["ext"], 2)
                nc.vector.tensor_tensor(ext[:, 2:3], ext[:, 0:1], ext[:, 1:2], ALU.max).then_inc(S["ext"], 1)
                v.wait_ge(S["top"], 1)
                nc.vector.reciprocal(ext[:, 0:1], ext[:, 3:4]).then_inc(S["wq"], 1)
                v.wait_ge(S["wq"], 3)
                nc.vector.tensor_scalar(wt[:, :, :], wt[:, :, :], ext[:, 0:1], 0.5, ALU.mult, ALU.mult).then_inc(S["wq"], 1)
                v.wait_ge(S["wq"], 4)
                nc.vector.tensor_scalar(wt[:, :, :], wt[:, :, :], 0.5, 3.0, ALU.add, ALU.mult).then_inc(S["wq"], 1)
                v.wait_ge(S["wq"], 5)
                nc.vector.tensor_scalar(wt[:, :, :], wt[:, :, :], MAGIC, MAGIC, ALU.add, ALU.subtract).then_inc(S["wq"], 1)
                v.wait_ge(S["wq"], 6)
                nc.vector.tensor_scalar(wq[:, :, :], wt[:, :, :], 2.0, 3.0, ALU.mult, ALU.subtract).then_inc(S["wq"], 1)

                def emit(p):
                    if p.has(0):
                        s = p.slot(0)
                        p.wait_lot("x_in", 0, 32)
                        p.wait_lot("out", -2, CONV_OUT)
                        for h in range(2):
                            rr = slice(HROWS * h, HROWS * h + HROWS)
                            p.wait("conv", 0, 2, h + 1)
                            nc.vector.scalar_tensor_tensor(x3[s][:, rr, :], p_c[h][:, :, :], 1.0 / 9.0, x2[s][:, rr, :], ALU.mult, ALU.add).then_inc(S["x3"], 1)
                        p.wait("x3", 0, 2)
                        for r in range(ROWS):
                            ins = nc.vector.bn_stats(st[s][:, r, :], x3[s][:, r, :])
                        ins.then_inc(S["stat"], 1)
                        p.wait("stat", 0, 2, 1)
                        v.sem_inc(S["passed"], 1)
                        for r in range(ROWS):
                            ins = nc.vector.bn_aggr(mv[s][:, r, :], st[s][:, r, :])
                        ins.then_inc(S["stat"], 1)
                        p.wait("stat", 0, 2)
                        nc.vector.tensor_scalar(ve[s][:, :], mv[s][:, :, 1], 1e-5, None, ALU.add).then_inc(S["ve"], 1)
                        p.wait("rstd", 0)
                        p.wait("trp", -2, 2)
                        for r in range(ROWS):
                            ins = nc.vector.tensor_scalar(t[s][:, r, :], x3[s][:, r, :], mv[s][:, r, 0:1], rstd[s][:, r:r + 1], ALU.subtract, ALU.mult)
                        ins.then_inc(S["t"], 1)
                trips(v, S, STRIPS, 2, 1, 1, emit)
        clear(nc, S.values())


CONV_OUT = 5 * 16


def node_ids():
    return np.arange(M, dtype=np.float32).reshape(P, NPP)


IMG = H * W
ROLL = SHIFT * W
NONE = float(2 ** 21)
LOW = -1e30


def rolled(image):
    a = image * IMG
    return (a, a + ROLL, IMG - ROLL), (a + IMG - ROLL, a, ROLL)


def search_edges(nc, d, dst_dram, first_dram, rp_dram):
    with ExitStack() as ctx:
        def sb(name, shape, dt=F32):
            return ctx.enter_context(nc.sbuf_tensor("es_" + name, shape, dt))

        def two(name, shape, dt=F32):
            return [sb(f"{name}{i}", shape, dt) for i in range(2)]
        blocks = dst_dram.rearrange("(n e) -> n e", e=BLK)
        ids = sb("ids", [P, NPP])
        ident = sb("ident", [P, P])
        diag = sb("diag", [P, P])
        ones = sb("ones", [P, P])
        mine = sb("mine", [P, EP // BLK])
        heads = sb("heads", [P, P])
        rp = sb("rp", [P, NPP])
        total = sb("total", [1, 1])
        q, c0, c1, c2, r0, r1 = (two(n, [P, PPS]) for n in ("q", "c0", "c1", "c2", "r0", "r1"))
        i0, i1 = (two(n, [P, PPS], I32) for n in ("i0", "i1"))
        got0, got1 = (two(n, [P, PPS, BLK]) for n in ("got0", "got1"))
        junk = sb("junk", [P, PPS, P])
        p_heads = ctx.enter_context(nc.psum_tensor("es_p", [P, P], F32))
        own = {n: ctx.enter_context(nc.semaphore("es_" + n)) for n in (
            "in", "set", "headsp", "lv0", "lv1", "lv2", "out", "passed")}
        S = {**own, **dict(zip(("first0", "first1", "block0", "block1"), d["soft"][0:4]))}

        with nc.Block() as block:
            @block.sync
            def _(sp):
                sp.dma_start(ids[:, :], d["node_ids"]).then_inc(S["in"], 16)
                sp.dma_start(ident[:, :], d["ident"]).then_inc(S["in"], 16)
                sp.dma_start(mine[:, :], first_dram).then_inc(S["in"], 16)
                sp.wait_ge(S["lv2"], 3 * STRIPS)
                sp.dma_start(rp_dram[0:M].rearrange("(p i) -> p i", p=P), rp[:, :]).then_inc(S["out"], 16)
                sp.dma_start(rp_dram[M:M + 1].rearrange("(p i) -> p i", p=1), total[:, :]).then_inc(S["out"], 16)
                sp.wait_ge(S["out"], 32)

            @block.tensor
            def _(pe):
                pe.wait_ge(S["set"], 2)
                nc.tensor.matmul(p_heads[:, :], ones[:, :], diag[:, :], start=True, stop=True).then_inc(S["headsp"], 1)

            @block.gpsimd
            def _(pool):
                def emit(p):
                    if p.has(0):
                        s = p.slot(0)
                        p.wait("lv0", 0, 4)
                        p.wait("lv1", -2, 4)
                        pool.sem_inc(S["passed"], 1)
                        for j in range(PPS):
                            nc.gpsimd.indirect_dma_start(out=got0[s][:, j, :], out_offset=None, in_=first_dram,
                                                         in_offset=bass.IndirectOffsetOnAxis(ap=i0[s][:, j:j + 1], axis=0)).then_inc(S[f"first{s}"], 16)
                    if p.has(0):
                        s = p.slot(0)
                        p.wait("lv1", 0, 4)
                        p.wait("lv2", -2, 3)
                        pool.sem_inc(S["passed"], 1)
                        for j in range(PPS):
                            nc.gpsimd.indirect_dma_start(out=got1[s][:, j, :], out_offset=None, in_=blocks,
                                                         in_offset=bass.IndirectOffsetOnAxis(ap=i1[s][:, j:j + 1], axis=0)).then_inc(S[f"block{s}"], 16)
                trips(pool, S, STRIPS, 2, 1, 1, emit)

            @block.vector
            def _(v):
                def count(out, q_, table):
                    for j in range(PPS):
                        t = table(j)
                        ins = nc.vector.tensor_scalar(junk[:, j, 0:t.shape[-1]], t, q_[:, j:j + 1], None, ALU.is_lt, ALU.add, accum_out=out[:, j:j + 1])
                    return ins

                nc.vector.memset(total[:, :], float(E))
                nc.vector.memset(ones[:, :], 1.0).then_inc(S["set"], 1)
                v.wait_ge(S["in"], 48)
                nc.vector.tensor_scalar(diag[:, :], ident[:, :], mine[:, 0:1], None, ALU.mult).then_inc(S["set"], 1)
                v.wait_ge(S["headsp"], 1)
                nc.vector.tensor_copy(heads[:, :], p_heads[:, :]).then_inc(S["set"], 1)
                v.wait_ge(S["set"], 3)

                def emit(p):
                    if p.has(1):
                        s = p.slot(1)
                        p.wait_lot("first", -1, PPS * 16)
                        nc.vector.tensor_copy(q[s][:, :], ids[:, bass.ds((p.t + 1) * PPS, PPS)]).then_inc(S["lv0"], 1)
                        p.wait("lv0", 1, 4, 1)
                        count(c0[s], q[s], lambda j: heads[:, :]).then_inc(S["lv0"], 1)
                        p.wait("lv0", 1, 4, 2)
                        nc.vector.tensor_scalar(r0[s][:, :], c0[s][:, :], 1.0, 0.0, ALU.subtract, ALU.max).then_inc(S["lv0"], 1)
                        p.wait("lv0", 1, 4, 3)
                        nc.vector.tensor_copy(i0[s][:, :], r0[s][:, :]).then_inc(S["lv0"], 1)
                    if p.has(0):
                        s = p.slot(0)
                        p.wait_lot("first", 0, PPS * 16)
                        p.wait_lot("block", -2, PPS * 16)
                        count(c1[s], q[s], lambda j: got0[s][:, j, :]).then_inc(S["lv1"], 1)
                        p.wait("lv1", 0, 4, 1)
                        nc.vector.tensor_scalar(c1[s][:, :], c1[s][:, :], 1.0, 0.0, ALU.subtract, ALU.max).then_inc(S["lv1"], 1)
                        p.wait("lv1", 0, 4, 2)
                        nc.vector.scalar_tensor_tensor(r1[s][:, :], r0[s][:, :], float(EP // BLK), c1[s][:, :], ALU.mult, ALU.add).then_inc(S["lv1"], 1)
                        p.wait("lv1", 0, 4, 3)
                        nc.vector.tensor_copy(i1[s][:, :], r1[s][:, :]).then_inc(S["lv1"], 1)
                    if p.has(0):
                        s = p.slot(0)
                        p.wait_lot("block", 0, PPS * 16)
                        count(c2[s], q[s], lambda j: got1[s][:, j, :]).then_inc(S["lv2"], 1)
                        p.wait("lv2", 0, 3, 1)
                        nc.vector.scalar_tensor_tensor(c0[s][:, :], r1[s][:, :], float(BLK), c2[s][:, :], ALU.mult, ALU.add).then_inc(S["lv2"], 1)
                        p.wait("lv2", 0, 3, 2)
                        nc.vector.tensor_copy(rp[:, bass.ds(p.t * PPS, PPS)], c0[s][:, :]).then_inc(S["lv2"], 1)
                trips(v, S, STRIPS, 2, 1, 1, emit)
        clear(nc, own.values())


def spans(nc, d, rp_dram, rps_dram, start_dram, end_dram, adst_dram, carry_dram):
    with ExitStack() as ctx:
        def sb(name, shape, dt=F32):
            return ctx.enter_context(nc.sbuf_tensor("sp_" + name, shape, dt))

        lo, hi, none, at = (sb(n, [P, NPP]) for n in ("lo", "hi", "none", "at"))
        start, end = (sb(n, [P, NPP], I32) for n in ("start", "end"))
        zero = sb("zero", [P, EP])
        low = sb("low", [P, NPP // 7, REC])
        copied, loaded, step, stored = (ctx.enter_context(nc.semaphore("sp_" + n)) for n in ("copied", "loaded", "step", "stored"))
        step = Steps(step)

        with nc.Block() as block:
            @block.sync
            def _(sp):
                for b in range(B):
                    for seq, node, n in rolled(b):
                        for k in range(2):
                            sp.dma_start(rps_dram[k:k + 1, seq:seq + n], rp_dram[node + k:node + k + n].rearrange("(o n) -> o n", o=1)).then_inc(copied, 16)
                sp.wait_ge(copied, 16 * 4 * B)
                for k, tile in ((0, lo), (1, hi)):
                    sp.dma_start(tile[:, :], rps_dram[k:k + 1, :].rearrange("o (p i) -> (o p) i", p=P)).then_inc(loaded, 16)
                sp.wait_ge(step.sem, 2)
                flat = adst_dram.rearrange("(p e) h -> p (e h)", p=P)
                for k in range(GH):
                    sp.dma_start(flat[:, EP * k:EP * (k + 1)], zero[:, :]).then_inc(stored, 16)
                flat = carry_dram.rearrange("(p i) c -> p (i c)", p=P)
                for k in range(7):
                    n = NPP // 7 * REC
                    sp.dma_start(flat[:, n * k:n * (k + 1)], low[:, :, :].rearrange("p i c -> p (i c)")).then_inc(stored, 16)
                sp.wait_ge(step.sem, 6)
                sp.dma_start(start_dram, start[:, :]).then_inc(stored, 16)
                sp.dma_start(end_dram, end[:, :]).then_inc(stored, 16)
                sp.wait_ge(stored, 16 * (GH + 7 + 2))

            @block.vector
            def _(v):
                nc.vector.memset(low[:, :, 0:GH], LOW)
                step.done_by(nc.vector.memset(low[:, :, GH:REC], 0.0))
                step.done_by(nc.vector.memset(zero[:, :], 0.0))
                v.wait_ge(loaded, 32)
                step.done_by(nc.vector.tensor_tensor(none[:, :], hi[:, :], lo[:, :], ALU.is_equal))
                v.wait_ge(step.sem, step.n)
                nc.vector.scalar_tensor_tensor(at[:, :], none[:, :], NONE, hi[:, :], ALU.mult, ALU.add)
                step.done_by(nc.vector.scalar_tensor_tensor(start[:, :], none[:, :], NONE, lo[:, :], ALU.mult, ALU.add))
                v.wait_ge(step.sem, step.n)
                step.done_by(nc.vector.tensor_scalar(none[:, :], at[:, :], 1.0, None, ALU.subtract))
                v.wait_ge(step.sem, step.n)
                step.done_by(nc.vector.tensor_copy(end[:, :], none[:, :]))
        clear(nc, (copied, loaded, step.sem, stored))


def scatter_terms(nc, d, start_dram, recs_dram, adst_dram):
    with ExitStack() as ctx:
        start = ctx.enter_context(nc.sbuf_tensor("sc_start", [P, NPP], I32))
        rec = ctx.enter_context(nc.sbuf_tensor("sc_rec", [P, NPP, REC], F32))
        loaded = ctx.enter_context(nc.semaphore("sc_loaded"))
        stored = d["soft"][4]
        with nc.Block() as block:
            @block.sync
            def _(sp):
                sp.dma_start(start[:, :], start_dram).then_inc(loaded, 16)
                sp.dma_start(rec[:, :, :], recs_dram.rearrange("(p i) c -> p i c", p=P)).then_inc(loaded, 16)

            @block.gpsimd
            def _(pool):
                pool.wait_ge(loaded, 32)
                for i in range(NPP):
                    nc.gpsimd.indirect_dma_start(out=adst_dram, out_offset=bass.IndirectOffsetOnAxis(ap=start[:, i:i + 1], axis=0),
                                                 in_=rec[:, i, FEAT + GH:REC], in_offset=None, bounds_check=E - 1,
                                                 oob_is_err=False).then_inc(stored, 16)
                pool.wait_ge(stored, 16 * NPP)
        clear(nc, (loaded,))


EXPERTS = 4
EH = 2 * C
CH = 64
CHUNKS = EP // CH
SROWS = 7
SLAB = SROWS * W
assert M // SLAB == CHUNKS
NG = 10


def graph_and_experts(nc, d, src_dram, dst_dram, same_dram, first_dram, rec_dram, adst_dram, tT_dram, scan_dram, carry_dram, y_dram):
    with ExitStack() as ctx:
        def sb(name, shape, dt=F32):
            return ctx.enter_context(nc.sbuf_tensor("gr_" + name, shape, dt))

        def two(name, shape, dt=F32):
            return [sb(f"{name}{i}", shape, dt) for i in range(2)]

        def ps(name, shape, dt=F32):
            return ctx.enter_context(nc.psum_tensor("gr_" + name, shape, dt))

        ident = sb("ident", [P, P])
        w1 = sb("w1", [P, EXPERTS * EH])
        w2 = sb("w2", [P, 2 * EXPERTS, C])
        b1 = sb("b1", [P, 2 * EXPERTS])
        b2 = sb("b2", [P, EXPERTS * C])
        tT = two("tT", [P, SLAB])
        hT = [sb("hT0", [P, 8, 4 * W]), sb("hT1", [P, 8, 3 * W])]
        y = two("y", [W, SROWS, EXPERTS * C])
        idx = two("idx", [P, CH], I32)
        same = two("same", [P, CH])
        start = two("start", [P, CH, GH])
        rec = two("rec", [P, CH, REC])
        ad = two("ad", [P, GH, CH])
        e = two("e", [P, GH, CH])
        ms = two("ms", [P, GH, CH + 1])
        pen = sb("pen", [P, CH])
        dd = sb("dd", [P, 2, GH, CH])
        ee = sb("ee", [P, 2, GH, CH])
        wt = sb("wt", [P, FEAT, CH])
        out = two("out", [P, CH, REC])
        heads, tails, prior, after = (sb(n, [P, CH]) for n in ("heads", "tails", "before", "after"))
        flag = sb("flag", [P, 8])
        headi = sb("headi", [P, 2], I32)
        headr = sb("headr", [P, REC])
        ends = sb("ends", [P, 3, 20])
        endT = sb("endT", [20, 3, P])
        cm = sb("cm", [20, P + 1])
        cs = sb("cs", [20, P + 1])
        cd = sb("cd", [20, 2, P])
        carry = sb("carry", [P, REC])
        p_h = [ps(f"p_h{i}", [P, 512]) for i in range(4)]
        p_y = [ps(f"p_y{i}", [W, EXPERTS, C]) for i in range(2)]
        p_e = ps("p_e", [20, 3, P])
        p_c = ps("p_c", [P, 2, 20])
        own = {n: ctx.enter_context(nc.semaphore("gr_" + n)) for n in (
            "consts_in", "set", "ld0", "ld1", "tin0", "tin1", "g", "ee", "ro0", "ro1",
            "hp", "hT", "yp", "y", "yo0", "yo1", "endp", "end", "cexp", "passed")}
        S = {**own, **dict(zip(("ga0", "ga1", "gb0", "gb1", "head_in", "carried"), d["soft"][5:11]))}

        with nc.Block() as block:
            @block.sync
            def _(sp):
                sp.wait_ge(S["set"], 1)
                edges = dst_dram.rearrange("(p e) -> p e", p=P)
                for dst, src in ((ident[:, :], d["ident"]), (w1[:, :], d["g_w1"]), (w2[:, :, :], d["g_w2"]), (b1[:, :], d["g_b1"]),
                                 (b2[:, :], d["g_b2"]), (heads[:, :], first_dram), (tails[:, :], edges[:, EP - CH:EP]),
                                 (prior[1:P, :], edges[0:P - 1, EP - CH:EP]), (after[0:P - 1, :], first_dram[1:P, :])):
                    sp.dma_start(dst, src).then_inc(S["consts_in"], 16)

                def emit(p):
                    if p.has(1):
                        s = p.slot(1)
                        p.wait_lot("ga", -1, CH // 2 * 16)
                        p.wait_lot("gb", -1, CH // 2 * 16)
                        p.wait("g", -1, NG)
                        cols = bass.ds((p.t + 1) * CH, CH)
                        sp.dma_start(idx[s][:, :], src_dram.rearrange("(p e) -> p e", p=P)[:, cols]).then_inc(S[f"ld{s}"], 16)
                        sp.dma_start(same[s][:, :], same_dram.rearrange("(p e) -> p e", p=P)[:, cols]).then_inc(S[f"ld{s}"], 16)
                        sp.dma_start(start[s][:, :, :], adst_dram.rearrange("(p e) h -> p e h", p=P)[:, cols, :]).then_inc(S[f"ld{s}"], 16)
                        p.wait("hp", -1, 16)
                        sp.dma_start(tT[s][:, :], tT_dram[:, bass.ds((p.t + 1) * SLAB, SLAB)]).then_inc(S[f"tin{s}"], 16)
                    if p.has(0):
                        s = p.slot(0)
                        p.wait("y", 0, SROWS)
                        dst = bass.AP(y_dram.tensor, p.t * (SLAB * EXPERTS * C), [[EXPERTS * C, W], [W * EXPERTS * C, SROWS], [1, EXPERTS * C]])
                        sp.dma_start(dst, y[s][:, :, :]).then_inc(S[f"yo{s}"], 16)
                    if p.has(-1):
                        s = p.slot(-1)
                        p.wait("g", -1, NG)
                        p.wait("ee", -1, 2)
                        sp.dma_start(scan_dram.rearrange("(p e) c -> p e c", p=P)[:, bass.ds((p.t - 1) * CH, CH), :], out[s][:, :, :]).then_inc(S[f"ro{s}"], 16)
                trips(sp, S, CHUNKS, 2, 1, 1, emit)
                for s in range(2):
                    sp.wait_ge(S[f"yo{s}"], 16 * (CHUNKS // 2))
                    sp.wait_ge(S[f"ro{s}"], 16 * (CHUNKS // 2))

            @block.gpsimd
            def _(pool):
                def emit(p):
                    if p.has(0):
                        s = p.slot(0)
                        p.wait_lot("ld", 0, 48)
                        p.wait("g", -2, NG, 8)
                        pool.sem_inc(S["passed"], 1)
                        for j in range(CH):
                            half = "ga" if j < CH // 2 else "gb"
                            nc.gpsimd.indirect_dma_start(out=rec[s][:, j, :], out_offset=None, in_=rec_dram,
                                                         in_offset=bass.IndirectOffsetOnAxis(ap=idx[s][:, j:j + 1], axis=0)).then_inc(S[f"{half}{s}"], 16)
                pool.wait_ge(S["set"], 2)
                nc.gpsimd.indirect_dma_start(out=headr[:, :], out_offset=None, in_=rec_dram,
                                             in_offset=bass.IndirectOffsetOnAxis(ap=headi[:, 0:1], axis=0)).then_inc(S["head_in"], 16)
                trips(pool, S, CHUNKS, 2, 0, 0, emit)
                pool.wait_ge(S["end"], 14)
                nc.gpsimd.indirect_dma_start(out=carry_dram, out_offset=bass.IndirectOffsetOnAxis(ap=headi[:, 1:2], axis=0),
                                             in_=carry[:, :], in_offset=None, bounds_check=M - 1, oob_is_err=False).then_inc(S["carried"], 16)
                pool.wait_ge(S["carried"], 16)

            @block.tensor
            def _(pe):
                pe.wait_ge(S["consts_in"], 16 * 9)

                def emit(p):
                    if p.has(0):
                        s = p.slot(0)
                        p.wait_slot("tin", 0)
                        for n in range(16):
                            h, m = n // 8, n % 8
                            if n < 4:
                                p.wait("hT", -1, 16, 13 + n)
                            else:
                                p.wait("hT", 0, 16, n - 3)
                            nt = (4 - h) * W
                            nc.tensor.matmul(p_h[n % 4][:, 0:nt], w1[:, P * m:P * (m + 1)], tT[s][:, 4 * W * h:4 * W * h + nt],
                                             start=True, stop=True).then_inc(S["hp"], 1)
                        for r in range(SROWS):
                            h = r // 4
                            bank = p_y[(s + r) % 2]
                            if r < 2:
                                p.wait("y", -1, SROWS, SROWS - 1 + r)
                            else:
                                p.wait("y", 0, SROWS, r - 1)
                            p.wait("hT", 0, 16, 8 * h + 8)
                            for x in range(EXPERTS):
                                for k in range(2):
                                    mm = nc.tensor.matmul(bank[:, x, :], hT[h][:, 2 * x + k, W * (r - 4 * h):W * (r - 4 * h + 1)], w2[:, 2 * x + k, :],
                                                          start=k == 0, stop=k == 1)
                            mm.then_inc(S["yp"], 1)
                trips(pe, S, CHUNKS, 2, 0, 0, emit)
                pe.wait_ge(S["end"], 2)
                for k in range(3):
                    mm = nc.tensor.transpose(p_e[:, k, :], ends[:, k, :], ident[:, :])
                mm.then_inc(S["endp"], 1)
                pe.wait_ge(S["end"], 12)
                for k, tile in enumerate((cm, cs)):
                    mm = nc.tensor.transpose(p_c[:, k, :], tile[:, 0:P], ident[0:20, 0:20])
                mm.then_inc(S["endp"], 1)

            @block.scalar
            def _(act):
                act.wait_ge(S["consts_in"], 16 * 9)

                def emit(p):
                    if p.has(-1):
                        s = p.slot(-1)
                        nc.scalar.preload_act_table_set("natural_log_exp_and_others")
                        p.wait("g", -1, NG, 7)
                        p.wait_slot("ro", -3)
                        nc.scalar.activation(ee[:, :, :, :], dd[:, :, :, :], ACT.Exp).then_inc(S["ee"], 1)
                        nc.scalar.activation(out[s][:, :, 0:GH], ms[s][:, :, 1:CH + 1].rearrange("p h j -> p j h"), ACT.Copy).then_inc(S["ee"], 1)
                    if p.has(0):
                        nc.scalar.preload_act_table(ACT.Gelu)
                        for n in range(16):
                            h, m = n // 8, n % 8
                            nt = (4 - h) * W
                            p.wait("hp", 0, 16, n + 1)
                            if m == 0:
                                p.wait("yp", -1, SROWS, 4 + 3 * h)
                            nc.scalar.activation(hT[h][:, m, :], p_h[n % 4][:, 0:nt], ACT.Gelu, bias=b1[:, m:m + 1]).then_inc(S["hT"], 1)
                trips(act, S, CHUNKS, 2, 0, 1, emit, peel=2)
                nc.scalar.preload_act_table_set("natural_log_exp_and_others")
                act.wait_ge(S["end"], 10)
                nc.scalar.activation(cd[:, :, :], cd[:, :, :], ACT.Exp).then_inc(S["cexp"], 1)

            @block.vector
            def _(v):
                nc.vector.memset(prior[:, :], -1.0)
                nc.vector.memset(after[:, :], -1.0).then_inc(S["set"], 1)
                v.wait_ge(S["consts_in"], 16 * 9)
                nc.vector.tensor_copy(headi[:, 0:1], heads[:, 0:1]).then_inc(S["set"], 1)
                nc.vector.tensor_tensor(flag[:, 0:1], heads[:, 0:1], prior[:, CH - 1:CH], ALU.is_equal)
                nc.vector.tensor_tensor(flag[:, 1:2], heads[:, 0:1], tails[:, CH - 1:CH], ALU.is_equal)
                nc.vector.tensor_tensor(flag[:, 2:3], tails[:, CH - 1:CH], after[:, 0:1], ALU.is_equal)
                nc.vector.tensor_scalar(flag[:, 4:5], heads[:, 0:1], float(IMG), None, ALU.is_ge)
                nc.vector.tensor_scalar(flag[:, 5:6], heads[:, 0:1], float(2 * IMG), None, ALU.is_ge)
                nc.vector.tensor_scalar(flag[:, 6:7], heads[:, 0:1], float(3 * IMG), None, ALU.is_ge).then_inc(S["set"], 1)
                v.wait_ge(S["set"], 3)
                nc.vector.tensor_tensor(flag[:, 3:4], flag[:, 0:1], flag[:, 1:2], ALU.mult)
                nc.vector.tensor_tensor(flag[:, 7:8], flag[:, 4:5], flag[:, 5:6], ALU.add).then_inc(S["set"], 1)
                v.wait_ge(S["set"], 4)
                nc.vector.tensor_tensor(flag[:, 4:5], flag[:, 7:8], flag[:, 6:7], ALU.add)
                nc.vector.tensor_tensor(flag[:, 5:6], flag[:, 2:3], flag[:, 1:2], ALU.mult).then_inc(S["set"], 1)
                v.wait_ge(S["set"], 5)
                nc.vector.scalar_tensor_tensor(flag[:, 6:7], flag[:, 5:6], 1.0, flag[:, 0:1], ALU.subtract, ALU.mult)
                nc.vector.scalar_tensor_tensor(flag[:, 7:8], flag[:, 4:5], float(-IMG), heads[:, 0:1], ALU.mult, ALU.add).then_inc(S["set"], 1)
                v.wait_ge(S["set"], 6)
                nc.vector.tensor_scalar(flag[:, 4:5], flag[:, 7:8], float(ROLL), float(IMG), ALU.is_lt, ALU.mult)
                nc.vector.tensor_scalar(flag[:, 5:6], flag[:, 6:7], NONE, NONE - ROLL, ALU.mult, ALU.add).then_inc(S["set"], 1)
                v.wait_ge(S["set"], 7)
                nc.vector.tensor_tensor(flag[:, 6:7], flag[:, 4:5], flag[:, 5:6], ALU.add).then_inc(S["set"], 1)
                v.wait_ge(S["set"], 8)
                nc.vector.tensor_tensor(headi[:, 1:2], flag[:, 6:7], heads[:, 0:1], ALU.add).then_inc(S["set"], 1)
                v.wait_ge(S["head_in"], 16)

                def emit(p):
                    if p.has(-1):
                        s = p.slot(-1)
                        o = 1 - s
                        first = isinstance(p.t, int) and p.t == 1

                        def so_far(k):
                            p.wait("g", -1, NG, k)

                        def before(tile):
                            return 0.0 if first else tile
                        p.wait_lot("ld", -1, 48)
                        p.wait_lot("ga", -1, CH // 2 * 16)
                        p.wait_lot("gb", -1, CH // 2 * 16)
                        if first:
                            nc.vector.memset(ms[o][:, :, CH], 0.0)
                            nc.vector.tensor_copy(start[s][:, 0, :], headr[:, FEAT + GH:REC])
                        nc.vector.tensor_scalar(pen[:, :], same[s][:, :], -LOW, LOW, ALU.mult, ALU.add).then_inc(S["g"], 1)
                        so_far(1)
                        for h in range(GH):
                            ins = nc.vector.tensor_tensor_scan(ad[s][:, h, :], same[s][:, :], start[s][:, :, h], before(ad[o][:, h, CH - 1:CH]), ALU.mult, ALU.add)
                        ins.then_inc(S["g"], 1)
                        so_far(2)
                        nc.vector.tensor_tensor(e[s][:, :, :], rec[s][:, :, FEAT:FEAT + GH].rearrange("p j h -> p h j"), ad[s][:, :, :], ALU.add).then_inc(S["g"], 1)
                        so_far(3)
                        nc.vector.scalar_tensor_tensor(e[s][:, :, :], e[s][:, :, :], 0.2, e[s][:, :, :], ALU.mult, ALU.max).then_inc(S["g"], 1)
                        so_far(4)
                        p.wait("ee", -3, 2)
                        nc.vector.tensor_copy(ms[s][:, :, 0], ms[o][:, :, CH])
                        for h in range(GH):
                            ins = nc.vector.tensor_tensor_scan(ms[s][:, h, 1:CH + 1], pen[:, :], e[s][:, h, :], before(ms[o][:, h, CH:CH + 1]), ALU.add, ALU.max)
                        ins.then_inc(S["g"], 1)
                        so_far(5)
                        nc.vector.tensor_tensor(dd[:, 0, :, :], ms[s][:, :, 0:CH], ms[s][:, :, 1:CH + 1], ALU.subtract)
                        nc.vector.tensor_tensor(dd[:, 1, :, :], e[s][:, :, :], ms[s][:, :, 1:CH + 1], ALU.subtract).then_inc(S["g"], 1)
                        so_far(6)
                        nc.vector.tensor_tensor(dd[:, 0, :, :], dd[:, 0, :, :], pen[:, :].rearrange("p (o j) -> p o j", o=1).to_broadcast([P, GH, CH]), ALU.add).then_inc(S["g"], 1)
                        p.wait("ee", -1, 2)
                        nc.vector.tensor_tensor(wt[:, :, :].rearrange("p (h x) j -> p h x j", h=GH),
                                                rec[s][:, :, 0:FEAT].rearrange("p j (h x) -> p h x j", h=GH),
                                                ee[:, 1, :, :].rearrange("p h (o j) -> p h o j", o=1).to_broadcast([P, GH, EXPERTS, CH]), ALU.mult).then_inc(S["g"], 1)
                        so_far(8)
                        p.wait_slot("ro", -3)
                        for h in range(GH):
                            ins = nc.vector.tensor_tensor_scan(out[s][:, :, GH + h], ee[:, 0, h, :], ee[:, 1, h, :], before(out[o][:, CH - 1, GH + h:GH + h + 1]), ALU.mult, ALU.add)
                        ins.then_inc(S["g"], 1)
                        for f in range(FEAT):
                            c = 2 * GH + f
                            ins = nc.vector.tensor_tensor_scan(out[s][:, :, c], ee[:, 0, f // EXPERTS, :], wt[:, f, :], before(out[o][:, CH - 1, c:c + 1]), ALU.mult, ALU.add)
                        ins.then_inc(S["g"], 1)
                        so_far(10)
                    if p.has(0):
                        s = p.slot(0)
                        p.wait_slot("yo", -2)
                        for r in range(SROWS):
                            p.wait("yp", 0, SROWS, r + 1)
                            nc.vector.tensor_tensor(y[s][:, r, :], p_y[(s + r) % 2][:, :, :].rearrange("p x c -> p (x c)"), b2[0:W, :], ALU.add).then_inc(S["y"], 1)
                trips(v, S, CHUNKS, 2, 0, 1, emit, peel=2)
                end = Steps(S["end"])

                def do(ins):
                    v.wait_ge(end.sem, end.done_by(ins))
                m = ms[1][:, :, CH:CH + 1]
                nc.vector.tensor_copy(ends[:, 0, 0:GH], ms[1][:, :, CH])
                nc.vector.tensor_copy(ends[:, 0, GH:20].rearrange("p (h x) -> p h x", h=GH), m.to_broadcast([P, GH, EXPERTS]))
                do(nc.vector.tensor_copy(ends[:, 1, :], out[1][:, CH - 1, GH:REC]))
                do(nc.vector.tensor_copy(ends[:, 2, :], flag[:, 3:4].to_broadcast([P, 20])))
                v.wait_ge(S["endp"], 1)
                do(nc.vector.tensor_copy(endT[:, :, :], p_e[:, :, :]))
                do(nc.vector.tensor_scalar(endT[:, 2, :], endT[:, 2, :], -LOW, LOW, ALU.mult, ALU.add))
                do(nc.vector.memset(cm[:, 0:1], LOW))
                do(nc.vector.memset(cs[:, 0:1], 0.0))
                do(nc.vector.tensor_tensor_scan(cm[:, 1:P + 1], endT[:, 2, :], endT[:, 0, :], 0.0, ALU.add, ALU.max))
                do(nc.vector.tensor_tensor(cd[:, 0, :], cm[:, 0:P], cm[:, 1:P + 1], ALU.subtract))
                do(nc.vector.tensor_tensor(cd[:, 1, :], endT[:, 0, :], cm[:, 1:P + 1], ALU.subtract))
                do(nc.vector.tensor_tensor(cd[:, 0, :], cd[:, 0, :], endT[:, 2, :], ALU.add))
                v.wait_ge(S["cexp"], 1)
                do(nc.vector.tensor_tensor(endT[:, 1, :], endT[:, 1, :], cd[:, 1, :], ALU.mult))
                do(nc.vector.tensor_tensor_scan(cs[:, 1:P + 1], cd[:, 0, :], endT[:, 1, :], 0.0, ALU.mult, ALU.add))
                v.wait_ge(S["endp"], 2)
                do(nc.vector.tensor_copy(carry[:, 0:GH], p_c[:, 0, 0:GH]))
                do(nc.vector.tensor_copy(carry[:, GH:REC], p_c[:, 1, :]))
        clear(nc, own.values())


FB = 14
FBLOCKS = NPP // FB
NF = 36


def combine(nc, d, end_dram, scan_dram, carry_dram, recs_dram, x3_dram, y_dram, out_dram):
    with ExitStack() as ctx:
        def sb(name, shape, dt=F32):
            return ctx.enter_context(nc.sbuf_tensor("cb_" + name, shape, dt))

        def two(name, shape, dt=F32):
            return [sb(f"{name}{i}", shape, dt) for i in range(2)]

        end = sb("end", [P, NPP], I32)
        low = sb("low", [P, FB, REC])
        cst = sb("cst", [P, 3, FEAT])
        order = sb("order", [P, 2, 4, 4])
        eps = sb("eps", [P, 1])
        x, y = two("x", [P, FB, C]), two("y", [P, FB, EXPERTS * C])
        a, b, r = (two(n, [P, FB, REC]) for n in ("a", "b", "r"))
        es = sb("es", [P, FB, GH])
        top = sb("top", [P, FB, GH])
        df = sb("df", [P, 3, FB, GH])
        ex = sb("ex", [P, 3, FB, GH])
        s0, s1 = (sb(n, [P, FB, GH]) for n in ("s0", "s1"))
        v0, v1, v2 = (sb(n, [P, FB, FEAT]) for n in ("v0", "v1", "v2"))
        mu, var, lnv, rstd, best, tot, rtot = (sb(n, [P, FB]) for n in ("mu", "var", "lnv", "rstd", "best", "tot", "rtot"))
        sc, rank, q, pq = (sb(n, [P, FB, EXPERTS]) for n in ("sc", "rank", "q", "pq"))
        c0, c1 = (sb(n, [P, FB, 16]) for n in ("c0", "c1"))
        gate = two("gate", [P, FB, EXPERTS])
        S = {n: ctx.enter_context(nc.semaphore("cb_" + n)) for n in (
            "consts_in", "set", "in0", "in1", "xy0", "xy1", "pre", "f", "sq", "act", "sum", "out0", "out1", "passed", "passed_sp")}
        S.update(zip(("ga0", "ga1"), d["soft"][11:13]))

        with nc.Block() as block:
            @block.sync
            def _(sp):
                for dst, src in ((end[:, :], end_dram), (cst[:, :, :], d["g_ln"]), (order[:, :, :, :], d["order"])):
                    sp.dma_start(dst, src).then_inc(S["consts_in"], 16)

                def emit(p):
                    if p.has(2):
                        s = p.slot(2)
                        p.wait("f", 0, NF)
                        cols = bass.ds((p.t + 2) * FB, FB)
                        for dst, src in ((b[s], carry_dram), (r[s], recs_dram)):
                            sp.dma_start(dst[:, :, :], src.rearrange("(p i) c -> p i c", p=P)[:, cols, :]).then_inc(S[f"in{s}"], 16)
                    if p.has(1):
                        s = p.slot(1)
                        p.wait("sum", -1, EXPERTS)
                        sp.sem_inc(S["passed_sp"], 1)
                        p.wait_slot("out", -1)
                        cols = bass.ds((p.t + 1) * FB, FB)
                        for dst, src in ((x[s], x3_dram), (y[s], y_dram)):
                            sp.dma_start(dst[:, :, :], src.rearrange("(p i) c -> p i c", p=P)[:, cols, :]).then_inc(S[f"xy{s}"], 16)
                    if p.has(0):
                        s = p.slot(0)
                        p.wait("sum", 0, EXPERTS)
                        sp.sem_inc(S["passed_sp"], 1)
                        sp.dma_start(out_dram.rearrange("(p i) c -> p i c", p=P)[:, bass.ds(p.t * FB, FB), :], x[s][:, :, :]).then_inc(S[f"out{s}"], 16)
                trips(sp, S, FBLOCKS, 2, 2, 0, emit)
                for s in range(2):
                    sp.wait_ge(S[f"out{s}"], 16 * (FBLOCKS // 2))

            @block.gpsimd
            def _(pool):
                idx = [sb(f"idx{i}", [P, FB], I32) for i in range(2)]
                copied = ctx.enter_context(nc.semaphore("cb_copied"))
                pool.wait_ge(S["consts_in"], 48)
                pool.wait_ge(S["set"], 1)

                def emit(p):
                    if p.has(0):
                        s = p.slot(0)
                        p.wait("f", -2, NF)
                        p.wait_lot("ga", -2, FB * 16)
                        pool.sem_inc(S["passed"], 1)
                        nc.gpsimd.tensor_copy(a[s][:, :, :], low[:, :, :])
                        nc.gpsimd.tensor_copy(idx[s][:, :], end[:, bass.ds(p.t * FB, FB)]).then_inc(copied, 1)
                        pool.wait_ge(copied, p.t + 1)
                        pool.sem_inc(S["passed"], 1)
                        for j in range(FB):
                            nc.gpsimd.indirect_dma_start(out=a[s][:, j, :], out_offset=None, in_=scan_dram,
                                                         in_offset=bass.IndirectOffsetOnAxis(ap=idx[s][:, j:j + 1], axis=0),
                                                         bounds_check=E - 1, oob_is_err=False).then_inc(S[f"ga{s}"], 16)
                trips(pool, S, FBLOCKS, 2, 0, 0, emit)

            @block.scalar
            def _(act):
                nc.scalar.preload_act_table_set("natural_log_exp_and_others")
                act.wait_ge(S["set"], 1)

                def emit(p):
                    if p.has(0):
                        if p.u == 0:
                            nc.scalar.preload_act_table_set("natural_log_exp_and_others")
                        p.wait("f", 0, NF, 5)
                        nc.scalar.activation(ex[:, :, :, :], df[:, :, :, :], ACT.Exp).then_inc(S["act"], 1)
                        p.wait("f", 0, NF, 19)
                        nc.scalar.activation(lnv[:, :], var[:, :], ACT.Ln, bias=eps[:, 0:1], scale=1.0 / FEAT).then_inc(S["act"], 1)
                        p.wait("act", 0, 4, 2)
                        nc.scalar.activation(rstd[:, :], lnv[:, :], ACT.Exp, scale=-0.5).then_inc(S["act"], 1)
                        p.wait("f", 0, NF, 32)
                        nc.scalar.activation(q[:, :, :], q[:, :, :], ACT.Exp).then_inc(S["act"], 1)
                trips(act, S, FBLOCKS, 2, 0, 0, emit)

            @block.vector
            def _(v):
                nc.vector.memset(eps[:, :], 1e-5)
                nc.vector.memset(low[:, :, 0:GH], LOW)
                nc.vector.memset(low[:, :, GH:REC], 0.0).then_inc(S["set"], 1)
                v.wait_ge(S["consts_in"], 48)

                def wide(t, n):
                    return t.rearrange("p i (h o) -> p i h o", o=1).to_broadcast([P, FB, GH, n])

                def parts(t):
                    return t.rearrange("p i (h x) -> p i h x", h=GH)

                def row(k):
                    return cst[:, k:k + 1, :].to_broadcast([P, FB, FEAT])

                def per(t, n):
                    return t[:, :].rearrange("p (i o) -> p i o", o=1).to_broadcast([P, FB, n])

                def small(p):
                    s = p.slot(0)
                    k = [0]
                    A, Bc, R = a[s], b[s], r[s]
                    tt = nc.vector.tensor_tensor

                    def did(ins):
                        ins.then_inc(S["f"], 1)
                        k[0] += 1

                    def ready():
                        p.wait("f", 0, NF, k[0])
                    p.wait_lot("in", 0, 32)
                    p.wait_lot("ga", 0, FB * 16)
                    did(tt(es[:, :, :], R[:, :, FEAT:FEAT + GH], R[:, :, FEAT + GH:REC], ALU.add)); ready()
                    did(nc.vector.scalar_tensor_tensor(es[:, :, :], es[:, :, :], 0.2, es[:, :, :], ALU.mult, ALU.max))
                    did(tt(top[:, :, :], A[:, :, 0:GH], Bc[:, :, 0:GH], ALU.max)); ready()
                    did(tt(top[:, :, :], top[:, :, :], es[:, :, :], ALU.max)); ready()
                    tt(df[:, 0, :, :], A[:, :, 0:GH], top[:, :, :], ALU.subtract)
                    tt(df[:, 1, :, :], Bc[:, :, 0:GH], top[:, :, :], ALU.subtract)
                    did(tt(df[:, 2, :, :], es[:, :, :], top[:, :, :], ALU.subtract))
                    yield
                    p.wait("act", 0, 4, 1)
                    did(tt(s0[:, :, :], A[:, :, GH:2 * GH], ex[:, 0, :, :], ALU.mult))
                    did(tt(s1[:, :, :], Bc[:, :, GH:2 * GH], ex[:, 1, :, :], ALU.mult))
                    did(tt(parts(v0[:, :, :]), parts(A[:, :, 2 * GH:REC]), wide(ex[:, 0, :, :], 4), ALU.mult))
                    did(tt(parts(v1[:, :, :]), parts(Bc[:, :, 2 * GH:REC]), wide(ex[:, 1, :, :], 4), ALU.mult))
                    did(tt(parts(v2[:, :, :]), parts(R[:, :, 0:FEAT]), wide(ex[:, 2, :, :], 4), ALU.mult)); ready()
                    did(tt(s0[:, :, :], s0[:, :, :], s1[:, :, :], ALU.add))
                    did(tt(v0[:, :, :], v0[:, :, :], v1[:, :, :], ALU.add)); ready()
                    did(nc.vector.scalar_tensor_tensor(s1[:, :, :], s0[:, :, :], 1e-16, ex[:, 2, :, :], ALU.add, ALU.add))
                    did(tt(v1[:, :, :], v0[:, :, :], v2[:, :, :], ALU.add)); ready()
                    did(nc.vector.reciprocal(s0[:, :, :], s1[:, :, :])); ready()
                    did(tt(parts(v2[:, :, :]), parts(v1[:, :, :]), wide(s0[:, :, :], 4), ALU.mult)); ready()
                    did(tt(v0[:, :, :], v2[:, :, :], row(0), ALU.add)); ready()
                    yield
                    nc.vector.tensor_reduce(mu[:, :], v0[:, :, :], AX_X, ALU.add).then_inc(S["f"], 1)
                    k[0] += 1
                    ready()
                    nc.vector.scalar_tensor_tensor(v1[:, :, :], per(mu, FEAT), -1.0 / FEAT, v0[:, :, :], ALU.mult, ALU.add).then_inc(S["sq"], 1)
                    p.wait("sq", 0, 2, 1)
                    nc.vector.tensor_tensor(v2[:, :, :], v1[:, :, :], v1[:, :, :], ALU.mult).then_inc(S["sq"], 1)
                    p.wait("sq", 0, 2, 2)
                    did(nc.vector.tensor_reduce(var[:, :], v2[:, :, :], AX_X, ALU.add))
                    yield
                    p.wait("act", 0, 4, 3)
                    did(tt(v0[:, :, :], v1[:, :, :], per(rstd, FEAT), ALU.mult)); ready()
                    did(tt(v1[:, :, :], v0[:, :, :], row(1), ALU.mult)); ready()
                    did(tt(v2[:, :, :], v1[:, :, :], row(2), ALU.add)); ready()
                    did(nc.vector.tensor_reduce(pq[:, :, :], v2[:, :, :].rearrange("p i (h x) -> p i x h", h=GH), AX_X, ALU.add)); ready()
                    did(nc.vector.tensor_scalar(sc[:, :, :], pq[:, :, :], 1.0 / GH, None, ALU.mult)); ready()
                    mine = sc[:, :, :].rearrange("p i (e o) -> p i e o", o=1).to_broadcast([P, FB, 4, 4])
                    theirs = sc[:, :, :].rearrange("p i (o f) -> p i o f", o=1).to_broadcast([P, FB, 4, 4])

                    def mask(n):
                        return order[:, n, :, :].rearrange("p (o e) f -> p o (e f)", o=1).to_broadcast([P, FB, 16])
                    did(tt(parts(c0[:, :, :]), theirs, mine, ALU.is_ge))
                    did(tt(parts(c1[:, :, :]), theirs, mine, ALU.is_gt))
                    did(nc.vector.tensor_reduce(best[:, :], sc[:, :, :], AX_X, ALU.max)); ready()
                    did(tt(c0[:, :, :], c0[:, :, :], mask(0), ALU.mult))
                    did(tt(c1[:, :, :], c1[:, :, :], mask(1), ALU.mult))
                    did(tt(q[:, :, :], sc[:, :, :], per(best, EXPERTS), ALU.subtract)); ready()
                    did(tt(c0[:, :, :], c0[:, :, :], c1[:, :, :], ALU.add)); ready()
                    did(nc.vector.tensor_reduce(rank[:, :, :], parts(c0[:, :, :]), AX_X, ALU.add)); ready()
                    yield
                    p.wait("act", 0, 4, 4)
                    did(nc.vector.scalar_tensor_tensor(pq[:, :, :], rank[:, :, :], 1.5, q[:, :, :], ALU.is_le, ALU.mult)); ready()
                    did(nc.vector.tensor_reduce(tot[:, :], pq[:, :, :], AX_X, ALU.add)); ready()
                    did(nc.vector.reciprocal(rtot[:, :], tot[:, :])); ready()
                    did(tt(gate[s][:, :, :], pq[:, :, :], per(rtot, EXPERTS), ALU.mult)); ready()
                    assert k[0] == NF, k[0]

                def emit(p):
                    nxt = iter(())
                    if p.has(1):
                        nxt = small(p.next())
                    next(nxt, None)
                    for n in range(EXPERTS):
                        if p.has(0):
                            s = p.slot(0)
                            if n:
                                p.wait("sum", 0, EXPERTS, n)
                            else:
                                p.wait_lot("xy", 0, 32)
                            for j in range(FB):
                                ins = nc.vector.scalar_tensor_tensor(x[s][:, j, :], y[s][:, j, C * n:C * (n + 1)], gate[s][:, j, n:n + 1], x[s][:, j, :], ALU.mult, ALU.add)
                            ins.then_inc(S["sum"], 1)
                        next(nxt, None)
                    assert next(nxt, None) is None
                trips(v, S, FBLOCKS, 2, 1, 0, emit)
def shape_tables():
    coords = np.arange(1 - WIN, WIN, dtype=np.float32)
    tab = np.stack(np.meshgrid(coords, coords, indexing="ij"), axis=-1) * np.float32(8.0 / 7.0)
    tab = (np.sign(tab) * np.log1p(np.abs(tab)) / np.log(8.0)).reshape(-1, 2).astype(np.float32)
    head = np.arange(P) // HD
    region = np.repeat([1, 2], WIN - SHIFT)
    masks = np.zeros((P, 4, WIN * WIN), np.float32)
    for row in range(2):
        for col in range(2):
            for w in range(2):
                rr = region if row else np.zeros(WIN, int)
                cc = region if col and w else np.zeros(WIN, int)
                reg = (rr[:, None] * 3 + cc[None, :]).reshape(-1)
                masks[64 * w:64 * w + 64, row * 2 + col] = np.where(reg[:, None] == reg[None, :], 0.0, -100.0)
    return {
        "ident": np.eye(P, dtype=np.float32),
        "rel_tab": np.ascontiguousarray(tab[::-1].T),
        "masks": masks,
        "same_head": (head[:, None] == head[None, :]).astype(np.float32),
        "row_signs": row_signs(),
        "head_parity": np.stack([head % 2 == 0, head % 2 == 1], 1).astype(np.float32),
    }


def windows(x):
    x = np.roll(x, (-SHIFT, -SHIFT), axis=(1, 2))
    x = x.reshape(B, SPI, WIN, PPS, 2, WIN, C).transpose(0, 1, 4, 2, 5, 3, 6)
    return np.ascontiguousarray(x.reshape(STRIPS, P, PPS, C))


def expert_order():
    e = np.arange(EXPERTS)
    return np.ascontiguousarray(np.broadcast_to(np.stack([e[None, :] < e[:, None], e[None, :] > e[:, None]]), (P, 2, 4, 4))).astype(np.float32)


def metaformer(nc, d, out_dram):
    def dram(name, shape, dt=F32):
        return nc.dram_tensor(name, shape, dt, kind="Internal").ap()

    src, dst, same, first = dram("src", (E,), I32), dram("dst", (E,)), dram("same", (E,)), dram("first", (P, EP // BLK))
    rowptr, rowptrs = dram("rowptr", (M + 1,)), dram("rowptrs", (2, M))
    start, end = dram("start", (P, NPP), I32), dram("end", (P, NPP), I32)
    adst, carry, scan = dram("adst", (E, GH)), dram("carry", (M, REC)), dram("scan", (E, REC))
    tables = {"bt": dram("bt", (HEADS, (2 * WIN - 1) ** 2)), "bias": dram("bias", (WIN * WIN, 512)), "bm": dram("bm", (4, P, 512))}
    x1, x2, x3 = dram("x1", (STRIPS, P, PPS, C)), dram("x2", (STRIPS, W, WIN, C)), dram("x3", (M, C))
    tT, rec, recs, y = dram("tT", (P, M)), dram("rec", (M, REC)), dram("recs", (M, REC)), dram("y", (M, EXPERTS * C))

    d = {**d, "soft": [nc.alloc_semaphore(f"soft{k}") for k in range(13)]}
    sort_edges(nc, d["edges"], d["row_signs"], d["ident"], src, dst, same, first)
    search_edges(nc, d, dst, first, rowptr)
    spans(nc, d, rowptr, rowptrs, start, end, adst, carry)
    make_bias(nc, d, tables)
    with ExitStack() as ctx:
        score = ctx.enter_context(nc.sbuf_tensor("score", [P, PAIRS], F32))
        gate = ctx.enter_context(nc.sbuf_tensor("gate", [P, PAIRS], F32))
        stats = ctx.enter_context(nc.sbuf_tensor("stats", [P, PAIRS, 2], F32))
        attention(nc, d, tables, x1, score, stats)
        select_tokens(nc, d, score, gate)
        pixels = ctx.enter_context(nc.sbuf_tensor("pixels", [P, B * PADW, PADW], BF16))
        routed_ffn(nc, d, x1, x2, stats, gate, pixels)
        convolve(nc, d, pixels, x2, x3, tT, rec, recs)
    scatter_terms(nc, d, start, recs, adst)
    graph_and_experts(nc, d, src, dst, same, first, rec, adst, tT, scan, carry, y)
    combine(nc, d, end, scan, carry, recs, x3, y, out_dram)


def kernel(**inputs):
    import concourse.bacc as bacc
    from concourse.bass_utils import run_bass_kernel_spmd

    i = {name: np.asarray(a) for name, a in inputs.items()}

    def spread(a):
        return np.ascontiguousarray(np.broadcast_to(a, (P, *a.shape)))

    def hidden(a, n):
        return np.ascontiguousarray(a.reshape(n, P).T)

    raster = np.broadcast_to(np.arange(H * W, dtype=np.float32).reshape(1, H, W, 1), (B, H, W, C))
    shapes = shape_tables()
    consts = np.zeros((P, 8), np.float32)
    consts[:, 0] = i["L0_conv_q_bias"]
    consts[:, 1] = np.repeat(i["L0_conv_scale"].reshape(-1), HD)
    consts[:, 2:4] = shapes["head_parity"]
    consts[:, 4] = i["L0_ffn_br"][0]
    consts[:, 5] = i["L0_conv_v_bias"]
    arrays = {
        **{name: shapes[name] for name in ("ident", "rel_tab", "masks", "same_head", "row_signs")},
        "node_ids": node_ids(),
        "order": expert_order(),
        "raster": np.ascontiguousarray(windows(raster)[..., 0].transpose(1, 0, 2).reshape(P, PAIRS)),
        "x_win": windows(i["x"]),
        "consts": consts,
        "w_qkv": i["L0_conv_w_qkv"],
        "w_proj": i["L0_conv_w_proj"],
        "b_proj": i["L0_conv_b_proj"][None],
        "cpb_w1": i["L0_conv_cpb_w1"],
        "cpb_b1": hidden(i["L0_conv_cpb_b1"], 2),
        "cpb_w2": i["L0_conv_cpb_w2"].reshape(2, P, HEADS).transpose(1, 0, 2),
        "wr": spread(i["L0_ffn_wr"][:, 0]),
        "f_w1": i["L0_ffn_w1"],
        "f_w2": i["L0_ffn_w2"].reshape(4, P, C).transpose(1, 0, 2),
        "f_b1": hidden(i["L0_ffn_b1"], 4),
        "f_b2": i["L0_ffn_b2"][None],
        "c_w": i["L1_conv_w"].reshape(TAPS, C, C),
        "g_wgat": i["L1_ffn_W_gat"],
        "g_att": spread(np.stack([i["L1_ffn_att_src"].reshape(-1), i["L1_ffn_att_dst"].reshape(-1)])),
        "g_w1": i["L1_ffn_W1"].transpose(1, 0, 2).reshape(C, EXPERTS * EH),
        "g_w2": i["L1_ffn_W2"].reshape(2 * EXPERTS, P, C).transpose(1, 0, 2),
        "g_b1": hidden(i["L1_ffn_b1"], 2 * EXPERTS),
        "g_b2": spread(i["L1_ffn_b2"].reshape(-1)),
        "g_ln": spread(np.stack([i["L1_ffn_b_gat"], i["L1_ffn_ln_gamma"], i["L1_ffn_ln_beta"]])),
        "edges": i["L1_ffn_edge_index"],
    }
    arrays = {f"in_{name}": np.ascontiguousarray(a) for name, a in arrays.items()}
    nc = bacc.Bacc("TRN2", target_bir_lowering=False, num_devices=1)
    d = {name[3:]: nc.dram_tensor(name, a.shape, mybir.dt.from_np(a.dtype), kind="ExternalInput").ap()
         for name, a in arrays.items()}
    out = nc.dram_tensor("out", (M, C), F32, kind="ExternalOutput").ap()
    metaformer(nc, d, out)
    r = run_bass_kernel_spmd(nc, [arrays], core_ids=[0])
    return np.roll(r.results[0]["out"].reshape(B, H, W, C), SHIFT, axis=1)
```

```python
from contextlib import ExitStack

import numpy as np

import concourse.bass as bass
from concourse import mybir

F32 = mybir.dt.float32
BF16 = mybir.dt.bfloat16
I32 = mybir.dt.int32
ALU = mybir.AluOpType
ACT = mybir.ActivationFunctionType
AX_X = mybir.AxisListType.X

P = 128
B, H, W, C = 4, 112, 112, 128
M = B * H * W
E = 524288
EP = E // P
NPP = M // P
BLK = 64
DST_MID = M / 2 - 0.5


class Steps:

    def __init__(self, sem):
        self.sem, self.n = sem, 0

    def done_by(self, ins, by=1):
        ins.then_inc(self.sem, by)
        self.n += by
        return self.n


def clear(nc, sems):
    with nc.Block() as block:
        @block.gpsimd
        def _(pool):
            for sem in sems:
                pool.sem_clear(sem)


WIN, SHIFT, HEADS, HD = 8, 4, 8, 16
PAIRS = M // P
PPS = 7
STRIPS = PAIRS // PPS
SPI = H // WIN
GRP = 4
VW = 2 * HD + 2
QK_EPS = 1.55e-05


class Bias:

    T, HID = (2 * WIN - 1) ** 2, 256

    def __init__(self, nc, ctx, d, tables):
        def sb(name, shape, dt=F32):
            return ctx.enter_context(nc.sbuf_tensor("mb_" + name, shape, dt))
        T, HID = self.T, self.HID
        self.nc, self.d, self.tables = nc, d, tables
        self.w1, self.rel = sb("w1", [2, HID]), sb("rel", [2, T])
        self.b1, self.w2 = sb("b1", [P, 2]), sb("w2", [P, 2, HEADS])
        self.hid, self.bt = sb("hid", [P, 2, T]), sb("bt", [HEADS, 3, T])
        self.bias, self.masks = sb("bias", [P, HEADS, WIN * WIN]), sb("masks", [P, 4, WIN * WIN])
        self.full = sb("full", [P, 4, HEADS, WIN * WIN])
        self.sem = {n: ctx.enter_context(nc.semaphore("mb_" + n)) for n in
                    ("loaded", "masks_in", "hidden", "relu", "table", "exp", "sig", "bt_out", "spread", "bias_in", "sum", "full_out")}

    def sync(self, sp):
        d, sem, T, bt_dram, bias_dram = self.d, self.sem, self.T, self.tables["bt"], self.tables["bias"]
        for dst, src in ((self.w1[:, :], d["cpb_w1"]), (self.rel[:, :], d["rel_tab"]), (self.b1[:, :], d["cpb_b1"]),
                         (self.w2[:, :, :], d["cpb_w2"])):
            sp.dma_start(dst, src).then_inc(sem["loaded"], 16)
        sp.dma_start(self.masks[:, :, :], d["masks"]).then_inc(sem["masks_in"], 16)
        sp.wait_ge(sem["sig"], 3)
        sp.dma_start(bt_dram, self.bt[:, 2, :]).then_inc(sem["bt_out"], 16)
        sp.wait_ge(sem["bt_out"], 16)
        with sp.Fori(0, WIN) as qr:
            with sp.Fori(0, WIN) as qc:
                at = (7 - qr) * 15 + (7 - qc)
                src = bass.AP(bt_dram.tensor, at, [[T, HEADS], [15, WIN], [1, WIN]])
                dst = bass.AP(bias_dram.tensor, (qr * WIN + qc) * 512, [[64, HEADS], [8, WIN], [1, WIN]])
                sp.dma_start(dst, src).then_inc(sem["spread"], 16)
        sp.wait_ge(sem["spread"], 16 * WIN * WIN)
        for w in range(2):
            sp.dma_start(self.bias[64 * w:64 * w + 64, :, :].rearrange("p h k -> p (h k)"), bias_dram).then_inc(sem["bias_in"], 16)
        sp.wait_ge(sem["sum"], 4)
        for m in range(4):
            sp.dma_start(self.tables["bm"][m], self.full[:, m, :, :].rearrange("p h k -> p (h k)")).then_inc(sem["full_out"], 16)
        sp.wait_ge(sem["full_out"], 64)

    def tensor(self, pe, banks):
        nc, sem, T = self.nc, self.sem, self.T
        pe.wait_ge(sem["loaded"], 64)
        for m in range(2):
            nc.tensor.matmul(banks[m][:, 0:T], self.w1[:, P * m:P * (m + 1)], self.rel[:, :], start=True, stop=True).then_inc(sem["hidden"], 1)
        pe.wait_ge(sem["relu"], 2)
        for m in range(2):
            last = nc.tensor.matmul(banks[2][0:HEADS, 0:T], self.w2[:, m, :], self.hid[:, m, :], start=m == 0, stop=m == 1)
        last.then_inc(sem["table"], 1)

    def scalar(self, act, banks):
        nc, sem, T = self.nc, self.sem, self.T
        for m in range(2):
            act.wait_ge(sem["hidden"], m + 1)
            nc.scalar.activation(self.hid[:, m, :], banks[m][:, 0:T], ACT.Relu, bias=self.b1[:, m:m + 1]).then_inc(sem["relu"], 1)
        act.wait_ge(sem["table"], 1)
        nc.scalar.activation(self.bt[:, 0, :], banks[2][0:HEADS, 0:T], ACT.Exp, scale=-1.0).then_inc(sem["exp"], 1)

    def sigmoid(self, v):
        nc, sem, bt = self.nc, self.sem, self.bt
        v.wait_ge(sem["exp"], 1)
        nc.vector.tensor_scalar(bt[:, 1, :], bt[:, 0, :], 1.0, None, ALU.add).then_inc(sem["sig"], 1)
        v.wait_ge(sem["sig"], 1)
        nc.vector.reciprocal(bt[:, 0, :], bt[:, 1, :]).then_inc(sem["sig"], 1)
        v.wait_ge(sem["sig"], 2)
        nc.vector.tensor_scalar(bt[:, 2, :], bt[:, 0, :], 16.0, None, ALU.mult).then_inc(sem["sig"], 1)

    def add_masks(self, v):
        nc, sem = self.nc, self.sem
        v.wait_ge(sem["masks_in"], 16)
        v.wait_ge(sem["bias_in"], 32)
        for m in range(4):
            mk = self.masks[:, m, :].rearrange("p (o k) -> p o k", o=1).to_broadcast([P, HEADS, WIN * WIN])
            nc.vector.tensor_tensor(self.full[:, m, :, :], self.bias[:, :, :], mk, ALU.add).then_inc(sem["sum"], 1)


def sort_edges(nc, edges, sgn_dram, ident_dram, src_dram, dst_dram, same_dram, first_dram, bias):
    with ExitStack() as ctx:
        def sb(name, shape, dt):
            return ctx.enter_context(nc.sbuf_tensor(name, shape, dt))

        def sem(name):
            return ctx.enter_context(nc.semaphore(name))

        src = sb("so_src", [P, EP], I32)
        dst = sb("so_dst", [P, EP], I32)
        ka = sb("so_ka", [P, EP], F32)
        kb = sb("so_kb", [P, EP], F32)
        sgn = sb("so_sgn", [P, 8], F32)
        heads = sb("so_heads", [P, EP // BLK], F32)
        ident = sb("so_ident", [P, P], F32)
        banks = [ctx.enter_context(nc.psum_tensor(f"so_ps{i}", [P, 512], F32)) for i in range(8)]
        loaded = sem("so_loaded")
        stepped = Steps(sem("so_stepped"))
        scaled = Steps(sem("so_scaled"))
        turned = Steps(sem("so_turned"))
        moved = Steps(sem("so_moved"))
        stored = sem("so_stored")

        NCH, LOCAL = 8, 12
        PH = 19
        plan = []
        x, y = ka, kb
        for k in range(1, LOCAL + 1):
            plan.append(("stage", x, y, 1 << (k - 1), True)); x, y = y, x
            for b in range(k - 2, -1, -1):
                plan.append(("stage", x, y, 1 << b, False)); x, y = y, x
        for k in range(LOCAL + 1, PH + 1):
            plan.append(("flip", x, y, k)); x, y = y, x
            plan.append(("turn", x, y)); x, y = y, x
            for b in range(k - 1 - LOCAL, -1, -1):
                plan.append(("stage", x, y, 1 << b, False)); x, y = y, x
            plan.append(("turn", x, y)); x, y = y, x
            for b in range(LOCAL - 1, -1, -1):
                plan.append(("stage", x, y, 1 << b, False)); x, y = y, x
        final, other = x, y

        with nc.Block() as block:
            at, s, m, t, f = [], 7, 0, 0, 0
            for item in plan:
                at.append((s, m, t, f))
                if item[0] == "stage":
                    s += 2
                elif item[0] == "flip":
                    f += NCH
                else:
                    t, m, s = t + NCH, m + NCH // 2, s + NCH // 2
            end = s

            @block.sync
            def _(sp):
                sp.dma_start(src[:, :], edges[0].rearrange("(p e) -> p e", p=P)).then_inc(loaded, 16)
                sp.dma_start(dst[:, :], edges[1].rearrange("(p e) -> p e", p=P)).then_inc(loaded, 16)
                sp.dma_start(sgn[:, :], sgn_dram).then_inc(loaded, 16)
                sp.dma_start(ident[:, :], ident_dram).then_inc(loaded, 16)
                bias.sync(sp)
                sp.wait_ge(stepped.sem, end + 7)
                for dram, tile in ((src_dram, src), (dst_dram, final), (same_dram, other)):
                    sp.dma_start(dram.rearrange("(p e) -> p e", p=P), tile[:, :]).then_inc(stored, 16)
                sp.dma_start(first_dram, heads[:, :]).then_inc(stored, 16)
                sp.wait_ge(stored, 64)

            @block.scalar
            def _(act):
                bias.scalar(act, banks)
                act.wait_ge(loaded, 64)
                for item, (s, m, t, f) in zip(plan, at):
                    if item[0] == "flip":
                        _, a, b, k = item
                        act.wait_ge(stepped.sem, s)
                        for c in range(NCH):
                            w = slice(512 * c, 512 * c + 512)
                            nc.scalar.activation(b[:, w], a[:, w], ACT.Copy,
                                                 scale=sgn[:, k - LOCAL:k - LOCAL + 1]).then_inc(scaled.sem, 1)
                    elif item[0] == "turn":
                        _, a, b = item
                        for c in range(0, NCH, 2):
                            act.wait_ge(turned.sem, t + c + 1)
                            nc.scalar.activation(b[:, 512 * c:512 * c + 512], banks[c][:, :], ACT.Copy).then_inc(moved.sem, 1)

            @block.tensor
            def _(pe):
                bias.tensor(pe, banks)
                pe.wait_ge(loaded, 64)
                for item, (s, m, t, f) in zip(plan, at):
                    if item[0] != "turn":
                        continue
                    _, a, b = item
                    pe.wait_ge(stepped.sem, s)
                    if m:
                        pe.wait_ge(moved.sem, m)
                    for c in range(NCH):
                        if f and t // NCH % 2 == 0:
                            pe.wait_ge(scaled.sem, f - NCH + c + 1)
                        for q in range(4):
                            w = slice(512 * c + P * q, 512 * c + P * (q + 1))
                            last = nc.tensor.transpose(banks[c][:, P * q:P * (q + 1)], a[:, w], ident[:, :])
                        last.then_inc(turned.sem, 1)

            @block.vector
            def _(v):
                done = stepped
                v.wait_ge(loaded, 64)
                done.done_by(nc.vector.tensor_scalar(ka[:, :], dst[:, :], DST_MID, None, ALU.subtract))
                v.wait_ge(done.sem, 1)
                done.done_by(nc.vector.scalar_tensor_tensor(kb[:, :], ka[:, :], -1.0, ka[:, :], ALU.mult, ALU.max))
                v.wait_ge(done.sem, 2)
                done.done_by(nc.vector.tensor_scalar(dst[:, :], kb[:, :], 127.5, None, ALU.add))
                v.wait_ge(done.sem, 3)
                done.done_by(nc.vector.scalar_tensor_tensor(dst[:, :], dst[:, :], 16, src[:, :],
                                                            ALU.logical_shift_left, ALU.bitwise_or))
                done.done_by(nc.vector.tensor_scalar(kb[:, :], ka[:, :], 0.0, 2.0, ALU.is_ge, ALU.mult))
                v.wait_ge(done.sem, 5)
                done.done_by(nc.vector.scalar_tensor_tensor(kb[:, :], kb[:, :], 1.0, dst[:, :].bitcast(F32),
                                                            ALU.subtract, ALU.mult))
                v.wait_ge(done.sem, 6)
                done.done_by(nc.vector.tensor_scalar(ka[:, :], kb[:, :], sgn[:, 0:1], None, ALU.mult))
                for n, (item, (s, m, t, f)) in enumerate(zip(plan, at)):
                    if n == 8:
                        bias.sigmoid(v)
                    if n == 50:
                        bias.add_masks(v)
                    if item[0] == "stage":
                        _, a, b, d, mirror = item
                        v.wait_ge(done.sem, s)
                        if m:
                            v.wait_ge(moved.sem, m)
                        av = a[:, :].rearrange("p (g h s) -> p g h s", h=2, s=d)
                        bv = b[:, :].rearrange("p (g h s) -> p g h s", h=2, s=d)
                        r = slice(None, None, -1) if mirror and d > 1 else slice(None)
                        done.done_by(nc.vector.tensor_tensor(bv[:, :, 0, :], av[:, :, 0, :], av[:, :, 1, r], ALU.min))
                        done.done_by(nc.vector.tensor_tensor(bv[:, :, 1, r], av[:, :, 0, :], av[:, :, 1, r], ALU.max))
                    elif item[0] == "turn":
                        _, a, b = item
                        for c in range(1, NCH, 2):
                            v.wait_ge(turned.sem, t + c + 1)
                            done.done_by(nc.vector.tensor_copy(b[:, 512 * c:512 * c + 512], banks[c][:, :]))
                assert done.n == end
                v.wait_ge(done.sem, end)
                bits = final[:, :].bitcast(I32)
                done.done_by(nc.vector.tensor_scalar(src[:, :], bits, 0xFFFF, None, ALU.bitwise_and))
                done.done_by(nc.vector.tensor_scalar(dst[:, :], bits, 16, 0x7FFF, ALU.logical_shift_right, ALU.bitwise_and))
                done.done_by(nc.vector.tensor_scalar(other[:, :], final[:, :], 0.0, 2.0, ALU.is_ge, ALU.mult))
                v.wait_ge(done.sem, end + 3)
                done.done_by(nc.vector.tensor_scalar(final[:, :], dst[:, :], 127.5, None, ALU.subtract))
                v.wait_ge(done.sem, end + 4)
                done.done_by(nc.vector.scalar_tensor_tensor(final[:, :], other[:, :], 1.0, final[:, :], ALU.subtract, ALU.mult))
                v.wait_ge(done.sem, end + 5)
                done.done_by(nc.vector.tensor_scalar(final[:, :], final[:, :], DST_MID, None, ALU.add))
                v.wait_ge(done.sem, end + 6)
                nc.vector.tensor_copy(heads[:, :], final[:, 0:EP:BLK])
                nc.vector.memset(other[:, 0:1], 0.0)
                done.done_by(nc.vector.tensor_tensor(other[:, 1:EP], final[:, 1:EP], final[:, 0:EP - 1], ALU.is_equal))
        clear(nc, (loaded, stepped.sem, scaled.sem, turned.sem, moved.sem, stored, *bias.sem.values()))


def row_signs():
    p = np.arange(P)
    s = [np.where((p >> (k - 12)) & 1, -1.0, 1.0) for k in range(12, 20)]
    cols = [s[0]] + [s[i - 1] * s[i] for i in range(1, 8)]
    return np.stack(cols, 1).astype(np.float32)


def last_row(eng, strip):
    if isinstance(strip, int):
        return int((strip + 1) % SPI == 0)
    return ((2147 - (strip + 1) * 147 % 2048) >> 11) % 2


def attention(nc, d, tables, x1_dram, score_sb, stats_sb, search):
    with ExitStack() as ctx:
        def sb(name, shape, dt=F32):
            return ctx.enter_context(nc.sbuf_tensor("at_" + name, shape, dt))

        def ps(name, shape):
            return ctx.enter_context(nc.psum_tensor("at_" + name, shape, F32))

        def sem(name):
            return ctx.enter_context(nc.semaphore("at_" + name))

        ident = sb("ident", [P, P])
        wqkv = sb("wqkv", [P, 3 * C])
        wproj = sb("wproj", [P, C])
        same_head = sb("same_head", [P, P])
        consts = sb("consts", [P, 8])
        bproj = sb("bproj", [1, C])
        wr = sb("wr", [P, C])
        bm = sb("bm", [P, 4, 512])
        kscale = sb("kscale", [P, 3])
        eps = sb("eps", [P, 2])
        nswr = sb("nswr", [P, 2])
        vb_cols = sb("vb_cols", [P, P])
        ones = sb("ones", [P, P])
        beff = sb("beff", [P, C])
        xs = [sb(f"xs{i}", [P, PPS, C]) for i in range(2)]
        xb = [sb(f"xb{i}", [P, PPS, C]) for i in range(2)]
        x1 = [sb(f"x1{i}", [P, PPS, C]) for i in range(2)]
        st = [sb(f"st{i}", [P, PPS, 6]) for i in range(2)]
        mv = [sb(f"mv{i}", [P, PPS, 2]) for i in range(2)]
        lnv = [sb(f"lnv{i}", [P, PPS]) for i in range(2)]
        rstd = [sb(f"rstd{i}", [P, PPS]) for i in range(2)]
        wst = [sb(f"wst{i}", [P, PPS, 6]) for i in range(2)]
        wmv = [sb(f"wmv{i}", [P, PPS, 2]) for i in range(2)]
        wln = [sb(f"wln{i}", [P, PPS]) for i in range(2)]
        wrs = [sb(f"wrs{i}", [P, PPS]) for i in range(2)]
        wdot = [sb(f"wdot{i}", [P, PPS]) for i in range(2)]
        wtmp = [sb(f"wtmp{i}", [P, 2, PPS]) for i in range(2)]
        junk = [sb(f"junk{i}", [P, C]) for i in range(2)]
        xh = [sb(f"xh{i}", [P, C]) for i in range(2)]
        xT = [sb(f"xT{i}", [P, 192]) for i in range(2)]
        qk = [sb(f"qk{i}", [P, 2 * P]) for i in range(2)]
        sq = [sb(f"sq{i}", [P, 2 * P]) for i in range(2)]
        nm = [sb(f"nm{i}", [P, 2 * P]) for i in range(2)]
        nl = [sb(f"nl{i}", [P, 2 * P]) for i in range(2)]
        rs = [sb(f"rs{i}", [P, 2 * P]) for i in range(2)]
        qn = [sb(f"qn{i}", [P, P]) for i in range(2)]
        kn = [sb(f"kn{i}", [P, 2, 2, 64]) for i in range(2)]
        vbd = [sb(f"vbd{i}", [P, 2, GRP, VW]) for i in range(PPS)]
        lg = [sb(f"lg{i}", [P, HEADS, 64]) for i in range(2)]
        lm = [sb(f"lm{i}", [P, HEADS, 64]) for i in range(2)]
        mx = [sb(f"mx{i}", [P, HEADS]) for i in range(2)]
        pr = [sb(f"pr{i}", [P, HEADS * 64]) for i in range(2)]
        pT = [sb(f"pT{i}", [P, GRP, P]) for i in range(2)]
        rc = [sb(f"rc{i}", [P, HEADS]) for i in range(2)]
        on = [sb(f"on{i}", [P, C]) for i in range(2)]
        oT = [sb(f"oT{i}", [P, P]) for i in range(2)]

        p_s = ps("p_s", [P, GRP, 512])
        p_proj = p_s[:, 1, P:P + C]
        p_n = ps("p_n", [P, 512])
        p_qkv = ps("p_qkv", [P, 4, P])
        p_tr = ps("p_tr", [P, 512])
        p_xT, p_oT = p_tr[:, 0:192], p_tr[:, 192:320]
        p_O = p_tr[:, 320:320 + GRP * VW].rearrange("p (g v) -> p g v", g=GRP)
        p_pT = ps("p_pT", [P, GRP, P])

        S = {n: sem(n) for n in (
            "consts_in", "setup", "ks", "beff_p", "x_in0", "x_in1", "x_out0", "x_out1", "xstat", "xrstd", "xb",
            "xh", "xTp", "xT", "qkvp", "qk", "v", "sq", "norm", "nmax", "rs", "qkn", "scores",
            "logit", "prob", "pTp", "pT", "outp", "on", "oTp", "oT", "proj", "x1", "dot", "wstat", "wrstd", "score", "passed", "passed_sp")}
        N = PAIRS
        HALF = 2 * PPS

        def pairs_of(eng, emit):
            for u in range(-4, HALF):
                emit(Step(eng, u, u, 0, 0, True, False))
            with eng.Fori(1, STRIPS // 2 - 1) as i:
                for u in range(HALF):
                    emit(Step(eng, u, i * HALF + u, i * 2, i, False, False))
            for u in range(HALF + 3):
                emit(Step(eng, u, N - HALF + u, STRIPS - 2, STRIPS // 2 - 1, False, True))

        class Step:
            def __init__(self, eng, u, t, s0, i, first, last):
                self.eng, self.u, self.t, self.s0, self.i, self.first, self.last = eng, u, t, s0, i, first, last

            def has(self, off):
                return not (self.first and self.u + off < 0) and not (self.last and self.u + off >= HALF)

            def wait(self, name, off, per=1, k=None):
                if self.has(off):
                    self.eng.wait_ge(S[name], (self.t + off) * per + (per if k is None else k))

            def slot(self, off):
                return (self.u + off) % 2

            def strip(self, off):
                s = (self.u + off) // PPS
                return self.s0 + s, s % 2, (self.u + off) % PPS

        with nc.Block() as block:
            @block.sync
            def _(sp):
                for dst, src in ((ident[:, :], d["ident"]), (wqkv[:, :], d["w_qkv"]), (wproj[:, :], d["w_proj"]),
                                 (same_head[:, :], d["same_head"]), (consts[:, :], d["consts"]),
                                 (bproj[:, :], d["b_proj"]), (wr[:, :], d["wr"])):
                    sp.dma_start(dst, src).then_inc(S["consts_in"], 16)
                sp.dma_start(bm[:, :, :], tables["bm"].rearrange("m p k -> p m k")).then_inc(S["consts_in"], 16)
                for s in range(2):
                    sp.dma_start(xs[s][:, :, :], d["x_win"][s]).then_inc(S[f"x_in{s}"], 16)

                def emit(p):
                    strip, s, j = p.strip(4)
                    if p.has(4) and j == PPS - 1 and not p.last and p.u + 4 < HALF:
                        p.wait("xh", 4)
                        sp.sem_inc(S["passed_sp"], 1)
                        sp.wait_ge(S["xb"], strip + 1)
                        sp.dma_start(xs[s][:, :, :], d["x_win"][bass.ds(strip + 2, 1)].rearrange("o p u c -> (o p) u c")).then_inc(S[f"x_in{s}"], 16)
                    strip, s, j = p.strip(-3)
                    if p.has(-3) and j == PPS - 1:
                        p.wait("x1", -3)
                        sp.dma_start(x1_dram[bass.ds(strip, 1)].rearrange("o p u c -> (o p) u c"), x1[s][:, :, :]).then_inc(S[f"x_out{s}"], 16)

                pairs_of(sp, emit)
                for s in range(2):
                    sp.wait_ge(S[f"x_out{s}"], 16 * (STRIPS // 2))

            @block.tensor
            def _(pe):
                pe.wait_ge(S["consts_in"], 16 * 8)
                pe.wait_ge(S["setup"], 5)
                nc.tensor.matmul(p_proj, vb_cols[:, :], wproj[:, :], start=True, stop=False)
                nc.tensor.matmul(p_proj, ones[0:1, :], bproj[:, :], start=False, stop=True).then_inc(S["beff_p"], 1)
                pe.wait_ge(S["setup"], 6)

                def emit(p):
                    if p.has(2):
                        p.wait("sq", 2)
                        p.wait("nmax", 1)
                        nc.tensor.matmul(p_n[:, 0:256], same_head[:, :], sq[p.slot(2)][:, :], start=True, stop=True).then_inc(S["norm"], 1)
                    if p.has(3):
                        r = p.slot(3)
                        p.wait("xT", 3)
                        p.wait("v", 2)
                        for j in range(2):
                            nc.tensor.matmul(p_qkv[:, j, :], wqkv[:, C * j:C * (j + 1)], xT[r][:, 0:P], start=True, stop=True)
                        for j in range(2):
                            mm = nc.tensor.matmul(p_qkv[:, 2 + j, :], xT[r][:, 64 * j:64 * j + P], wqkv[:, 2 * C:3 * C], start=True, stop=True)
                        mm.then_inc(S["qkvp"], 1)
                    if p.has(-1):
                        r = p.slot(-1)
                        vb = vbd[(p.u - 1) % PPS]
                        p.wait("pT", -1)
                        p.wait("v", -1)
                        p.wait("xT", 3)
                        p.wait("oT", -3)
                        p.wait("on", -2, 2)
                        for w in range(2):
                            for g in range(GRP):
                                mm = nc.tensor.matmul(p_O[64 * w:64 * w + 64, g, :], pT[r][:, g, 64 * w:64 * w + 64],
                                                      vb[:, w, g, :], start=True, stop=True)
                        mm.then_inc(S["outp"], 1)
                    if p.has(1):
                        r = p.slot(1)
                        p.wait("qkn", 1)
                        p.wait("logit", 0, 3, 1)
                        p.wait("x1", -4)
                        for w in range(2):
                            for g in range(GRP):
                                rows = slice(32 * g, 32 * g + 32)
                                mm = nc.tensor.matmul(p_s[64 * w:64 * w + 64, g, 0:P], qn[r][rows, 64 * w:64 * w + 64],
                                                      kn[r][rows, w, :, :], start=True, stop=True)
                        mm.then_inc(S["scores"], 1)
                    if p.has(-3):
                        p.wait("oT", -3)
                        p.wait("logit", 0, 3, 1)
                        p.wait("x1", -4)
                        nc.tensor.matmul(p_proj, oT[p.slot(-3)][:, :], wproj[:, :], start=True, stop=True).then_inc(S["proj"], 1)
                    if p.has(-2):
                        p.wait("on", -2, 2)
                        p.wait("on", -1, 2)
                        p.wait("xT", 3)
                        p.wait("oT", -3)
                        nc.tensor.transpose(p_oT, on[p.slot(-2)][:, :], ident[:, :]).then_inc(S["oTp"], 1)
                    if p.has(4):
                        r = p.slot(4)
                        p.wait("xh", 4)
                        p.wait("on", -1, 2)
                        p.wait("xT", 3)
                        p.wait("oT", -3)
                        nc.tensor.transpose(p_xT[:, 0:P], xh[r][:, :], ident[:, :])
                        nc.tensor.transpose(p_xT[:, P:192], xh[r][0:64, :], ident[0:64, 0:64]).then_inc(S["xTp"], 1)
                    if p.has(0):
                        p.wait("prob", 0)
                        p.wait("pT", -1)
                        for g in range(GRP):
                            mm = nc.tensor.transpose(p_pT[:, g, :], pr[p.slot(0)][:, P * g:P * (g + 1)], ident[:, :])
                        mm.then_inc(S["pTp"], 1)
                pairs_of(pe, emit)

            @block.gpsimd
            def _(pool):
                def emit(p):
                    if p.has(3):
                        r = p.slot(3)
                        p.wait("qk", 3)
                        p.wait("norm", 1)
                        nc.gpsimd.tensor_tensor(sq[r][:, :], qk[r][:, :], qk[r][:, :], ALU.mult).then_inc(S["sq"], 1)
                    at, j = (p.i, p.u // PPS), p.u % PPS
                    if 0 <= p.u < HALF and j < 3:
                        search.gather_firsts(pool, at, ((0, 1, 2), (3, 4), (5, 6))[j])
                    if 0 <= p.u < HALF and j > 3:
                        search.gather_blocks(pool, at, ((0, 1, 2), (3, 4), (5, 6))[j - 4])
                pairs_of(pool, emit)

            @block.scalar
            def _(act):
                nc.scalar.preload_act_table_set("natural_log_exp_and_others")
                act.wait_ge(S["consts_in"], 16 * 8)
                nc.scalar.activation(kscale[:, 0:1], consts[:, 1:2], ACT.Exp).then_inc(S["ks"], 1)
                act.wait_ge(S["setup"], 5)

                def xrstd(s, strip):
                    act.wait_ge(S["xstat"], 2 * (strip + 1))
                    nc.scalar.activation(lnv[s][:, :], mv[s][:, :, 1], ACT.Ln, bias=eps[:, 0:1]).then_inc(S["xrstd"], 1)
                    act.wait_ge(S["xrstd"], 2 * strip + 1)
                    nc.scalar.activation(rstd[s][:, :], lnv[s][:, :], ACT.Exp, scale=-0.5).then_inc(S["xrstd"], 1)

                def wrstd(s, strip):
                    act.wait_ge(S["wstat"], strip + 1)
                    nc.scalar.activation(wln[s][:, :], wmv[s][:, :, 1], ACT.Ln, bias=eps[:, 1:2]).then_inc(S["wrstd"], 1)
                    act.wait_ge(S["wrstd"], 2 * strip + 1)
                    nc.scalar.activation(wrs[s][:, :], wln[s][:, :], ACT.Exp, scale=-0.5).then_inc(S["wrstd"], 1)

                def emit(p):
                    if p.u == 0 or p.u == -4:
                        nc.scalar.preload_act_table_set("natural_log_exp_and_others")
                    if p.u == -4 and p.first:
                        xrstd(0, 0)
                    if p.has(3):
                        r = p.slot(3)
                        vb = vbd[(p.u + 3) % PPS]
                        p.wait("qkvp", 3)
                        p.wait("qkn", 1)
                        p.wait("sq", 1)
                        p.wait("outp", -4)
                        nc.scalar.activation(qk[r][:, 0:P], p_qkv[:, 0, :], ACT.Identity, bias=consts[:, 0:1])
                        nc.scalar.activation(qk[r][:, P:2 * P], p_qkv[:, 1, :], ACT.Copy).then_inc(S["qk"], 1)
                        pv = p_qkv[:, 2:4, :].rearrange("p w (g k) -> p w g k", g=GRP)
                        nc.scalar.activation(vb[0:64, :, :, 0:16], pv[0:64, :, :, 0:16], ACT.Copy)
                        nc.scalar.activation(vb[64:128, :, :, 16:32], pv[64:128, ::-1, :, 16:32], ACT.Copy).then_inc(S["v"], 1)
                    if p.has(2):
                        r = p.slot(2)
                        p.wait("nmax", 2)
                        nc.scalar.activation(nl[r][:, :], nm[r][:, :], ACT.Ln).then_inc(S["rs"], 1)
                        p.wait("rs", 2, 2, 1)
                        p.wait("qkn", 0)
                        nc.scalar.activation(rs[r][:, :], nl[r][:, :], ACT.Exp, scale=-0.5).then_inc(S["rs"], 1)
                    if p.has(0):
                        p.wait("logit", 0, 3)
                        p.wait("pTp", -2)
                        nc.scalar.activation(pr[p.slot(0)][:, :], lm[p.slot(0)][:, :, :].rearrange("p h k -> p (h k)"), ACT.Exp).then_inc(S["prob"], 1)
                    if p.has(-2):
                        p.wait("oTp", -2)
                        p.wait("xTp", 4)
                        p.wait("proj", -4)
                        nc.scalar.activation(oT[p.slot(-2)][:, :], p_oT, ACT.Copy).then_inc(S["oT"], 1)
                    if p.has(4):
                        p.wait("xTp", 4)
                        p.wait("qkvp", 2)
                        nc.scalar.activation(xT[p.slot(4)][:, :], p_xT, ACT.Copy).then_inc(S["xT"], 1)
                    if p.has(0):
                        p.wait("pTp", 0)
                        p.wait("outp", -2)
                        nc.scalar.activation(pT[p.slot(0)][:, :, :], p_pT[:, :, :], ACT.Copy).then_inc(S["pT"], 1)
                    strip, s, j = p.strip(0)
                    if j == 2 and p.has(0) and p.has(PPS):
                        p.wait("xh", 4 - PPS)
                        xrstd(1 - s, strip + 1)
                    for off in (-4, -3) if p.last and p.u == HALF + 2 else (-4,):
                        strip, s, j = p.strip(off)
                        if j == PPS - 1 and p.has(off):
                            wrstd(s, strip)
                pairs_of(act, emit)

            @block.vector
            def _(v):
                nc.vector.memset(eps[:, 0:1], 1e-6)
                nc.vector.memset(eps[:, 1:2], 1e-5)
                nc.vector.memset(ones[:, :], 1.0)
                for i in range(PPS):
                    nc.vector.memset(vbd[i][:, :, :, :], 0.0)
                nc.vector.memset(vb_cols[:, :], 0.0).then_inc(S["setup"], 1)
                v.wait_ge(S["setup"], 1)
                for i in range(PPS):
                    nc.vector.memset(vbd[i][0:64, :, :, 32:33], 1.0)
                    nc.vector.memset(vbd[i][64:128, :, :, 33:34], 1.0)
                v.wait_ge(S["consts_in"], 16 * 8)
                nc.vector.tensor_scalar(vb_cols[:, :], vb_cols[:, :], consts[:, 5:6], None, ALU.add).then_inc(S["setup"], 1)
                nc.vector.tensor_reduce(nswr[:, 0:1], wr[:, :], AX_X, ALU.add).then_inc(S["setup"], 1)
                v.wait_ge(S["setup"], 3)
                v.wait_ge(S["ks"], 1)
                nc.vector.tensor_scalar(nswr[:, 1:2], nswr[:, 0:1], -1.0, None, ALU.mult)
                for e in range(2):
                    nc.vector.tensor_scalar(kscale[:, 1 + e:2 + e], kscale[:, 0:1], consts[:, 2 + e:3 + e], None, ALU.mult).then_inc(S["setup"], 1)
                v.wait_ge(S["beff_p"], 1)
                nc.vector.tensor_copy(beff[:, :], p_proj).then_inc(S["setup"], 1)
                v.wait_ge(S["setup"], 6)

                def stats(s, strip):
                    v.wait_ge(S[f"x_in{s}"], (strip // 2 + 1) * 16 if isinstance(strip, int) else (strip >> 1) * 16 + 16)
                    for j in range(PPS):
                        ins = nc.vector.bn_stats(st[s][:, j, :], xs[s][:, j, :])
                    ins.then_inc(S["xstat"], 1)
                    v.wait_ge(S["xstat"], 2 * strip + 1)
                    v.sem_inc(S["passed"], 1)
                    for j in range(PPS):
                        ins = nc.vector.bn_aggr(mv[s][:, j, :], st[s][:, j, :])
                    ins.then_inc(S["xstat"], 1)

                def residual(s):
                    be = beff[:, :].rearrange("p (o c) -> p o c", o=1).to_broadcast([P, PPS, C])
                    nc.vector.tensor_tensor(xb[s][:, :, :], xs[s][:, :, :], be, ALU.add).then_inc(S["xb"], 1)

                def score(s, strip):
                    v.wait_ge(S["wrstd"], 2 * (strip + 1))
                    nc.vector.scalar_tensor_tensor(wtmp[s][:, 0, :], wmv[s][:, :, 0], nswr[:, 1:2], wdot[s][:, :],
                                                   ALU.mult, ALU.add).then_inc(S["score"], 1)
                    v.wait_ge(S["score"], 3 * strip + 1)
                    nc.vector.tensor_tensor(wtmp[s][:, 1, :], wtmp[s][:, 0, :], wrs[s][:, :], ALU.mult).then_inc(S["score"], 1)
                    v.wait_ge(S["score"], 3 * strip + 2)
                    nc.vector.tensor_copy(stats_sb[:, bass.ds(strip * PPS, PPS), 0], wmv[s][:, :, 0])
                    nc.vector.tensor_copy(stats_sb[:, bass.ds(strip * PPS, PPS), 1], wrs[s][:, :])
                    nc.vector.tensor_scalar(score_sb[:, bass.ds(strip * PPS, PPS)], wtmp[s][:, 1, :], consts[:, 4:5], None,
                                            ALU.add).then_inc(S["score"], 1)

                def emit(p):
                    if p.u == -4 and p.first:
                        stats(0, 0)
                        residual(0)
                    if p.has(0):
                        q = p.slot(0)
                        strip, _, j = p.strip(0)
                        p.wait("scores", 0)
                        p.wait("prob", -2)
                        bias = bm[:, bass.ds(last_row(v, strip) * 2 + int(j == PPS - 1), 1), :].rearrange("p o (g k) -> p (o g) k", g=GRP)
                        nc.vector.tensor_tensor(lg[q][:, :, :].rearrange("p (g e) k -> p g (e k)", g=GRP),
                                                p_s[:, :, 0:P], bias, ALU.add).then_inc(S["logit"], 1)
                    if p.has(2):
                        p.wait("norm", 2)
                        p.wait("rs", 0, 2)
                        nc.vector.tensor_scalar(nm[p.slot(2)][:, :], p_n[:, 0:256], QK_EPS, None, ALU.max).then_inc(S["nmax"], 1)
                    if p.has(0):
                        p.wait("logit", 0, 3, 1)
                        nc.vector.tensor_reduce(mx[q][:, :], lg[q][:, :, :], AX_X, ALU.max).then_inc(S["logit"], 1)
                        p.wait("logit", 0, 3, 2)
                        top = mx[q][:, :].rearrange("p (h o) -> p h o", o=1).to_broadcast([P, HEADS, 64])
                        nc.vector.tensor_tensor(lm[q][:, :, :], lg[q][:, :, :], top, ALU.subtract).then_inc(S["logit"], 1)
                    if p.has(-1):
                        r = p.slot(-1)
                        p.wait("outp", -1)
                        p.wait("oTp", -3)
                        nc.vector.reciprocal(rc[r][:, :].rearrange("p (g e) -> p g e", g=GRP), p_O[:, :, 32:34]).then_inc(S["on"], 1)
                        p.wait("on", -1, 2, 1)
                        rr = rc[r][:, :].rearrange("p (g e o) -> p g e o", g=GRP, o=1).to_broadcast([P, GRP, 2, HD])
                        nc.vector.tensor_tensor(on[r][:, :].rearrange("p (g e c) -> p g e c", g=GRP, e=2),
                                                p_O[:, :, 0:32].rearrange("p g (e c) -> p g e c", e=2), rr, ALU.mult).then_inc(S["on"], 1)
                    if p.has(4):
                        strip, s, j = p.strip(4)
                        if j == 0 or p.u == -4:
                            v.wait_ge(S["xrstd"], 2 * (strip + 1))
                        p.wait("xTp", 2)
                        nc.vector.tensor_scalar(xh[p.slot(4)][:, :], xs[s][:, j, :], mv[s][:, j, 0:1], rstd[s][:, j:j + 1],
                                                ALU.subtract, ALU.mult).then_inc(S["xh"], 1)
                    if p.has(2):
                        r = p.slot(2)
                        p.wait("rs", 2, 2)
                        p.wait("qk", 2)
                        p.wait("scores", 0)
                        nc.vector.tensor_tensor(qn[r][:, :], qk[r][:, 0:P], rs[r][:, 0:P], ALU.mult)
                        for e in range(2):
                            ins = nc.vector.scalar_tensor_tensor(
                                kn[r][:, :, e, :], qk[r][:, P:2 * P].rearrange("p (w k) -> p w k", w=2), kscale[:, 1 + e:2 + e],
                                rs[r][:, P:2 * P].rearrange("p (w k) -> p w k", w=2), ALU.mult, ALU.mult)
                        ins.then_inc(S["qkn"], 1)
                    if p.has(-3):
                        strip, s, j = p.strip(-3)
                        p.wait("proj", -3)
                        if j == 0 and not (p.first and p.u - 3 < HALF):
                            v.wait_ge(S[f"x_out{s}"], (p.s0 >> 1) * 16)
                        nc.vector.tensor_tensor(x1[s][:, j, :], p_proj, xb[s][:, j, :], ALU.add).then_inc(S["x1"], 1)
                        p.wait("x1", -3)
                        nc.vector.tensor_tensor_reduce(out=junk[p.slot(-3)][:, :], in0=x1[s][:, j, :], in1=wr[:, :], scale=1.0, scalar=0.0,
                                                       op0=ALU.mult, op1=ALU.add, accum_out=wdot[s][:, j:j + 1])
                        nc.vector.bn_stats(wst[s][:, j, :], x1[s][:, j, :]).then_inc(S["dot"], 1)
                        if j == PPS - 1:
                            p.wait("dot", -3)
                            v.sem_inc(S["passed"], 1)
                            for j in range(PPS):
                                ins = nc.vector.bn_aggr(wmv[s][:, j, :], wst[s][:, j, :])
                            ins.then_inc(S["wstat"], 1)
                            if p.last and p.u == HALF + 2:
                                score(s, strip)
                    strip, s, j = p.strip(0)
                    if j == 1 and p.has(0) and p.has(PPS):
                        stats(1 - s, strip + 1)
                    if j == 2 and p.has(0) and p.has(PPS):
                        residual(1 - s)
                    if j == 4 and not (p.first and p.u < PPS) and p.u < HALF:
                        score(1 - s, strip - 1)
                    if 0 <= p.u < HALF:
                        k = p.u // PPS
                        if j == 0 and not (p.first and k == 0):
                            search.edge_of(v, (p.i, k - 1))
                        if j == 3:
                            search.block_of(v, (p.i, k))
                        if j == 5 and not (p.last and k == 1):
                            search.partition_of(v, (p.i, k + 1))
                search.partition_of(v, (0, 0))
                pairs_of(v, emit)
                search.edge_of(v, (STRIPS // 2 - 1, 1))
        clear(nc, [*S.values(), *search.own.values()])


TPI = H * W
KSEL = TPI // 2 - 1
CPI = TPI // P
MAGIC = 1.5 * 2 ** 23
PADW = W + 2
X2_OUT = 2 * PPS * 16


def select_tokens(nc, d, score_sb, gate_sb, spans):
    with ExitStack() as ctx:
        def sb(name, shape, dt=F32):
            return ctx.enter_context(nc.sbuf_tensor("se_" + name, shape, dt))

        ones = sb("ones", [P, P])
        ridx = sb("ridx", [P, PAIRS])
        cmp = sb("cmp", [P, PAIRS])
        ws = sb("ws", [P, PAIRS])
        tie = sb("tie", [P, PAIRS])
        cnt = sb("cnt", [P, B])
        sgn = sb("sgn", [P, B])
        need = sb("need", [P, B])
        cur = sb("cur", [P, B], I32)
        cand = sb("cand", [P, B], I32)
        keep = sb("keep", [P, B], I32)
        thr = sb("thr", [P, B])
        cut = sb("cut", [P, B])
        cutc = sb("cutc", [P, B])
        tot = ctx.enter_context(nc.psum_tensor("se_tot", [P, B], F32))
        loaded, counted, summed = (ctx.enter_context(nc.semaphore("se_" + n)) for n in ("loaded", "counted", "summed"))
        step = Steps(ctx.enter_context(nc.semaphore("se_step")))
        TRIPS = 1 + 31 + 1 + 14

        with nc.Block() as block:
            @block.sync
            def _(sp):
                sp.dma_start(ridx[:, :], d["raster"]).then_inc(loaded, 16)
                spans.tables(sp)
                spans.store(sp)

            @block.tensor
            def _(pe):
                for n in range(TRIPS):
                    pe.wait_ge(counted, n + 1)
                    nc.tensor.matmul(tot[:, :], ones[:, :], cnt[:, :], start=True, stop=True).then_inc(summed, 1)

            @block.vector
            def _(v):
                trips = [0]

                def do(ins):
                    v.wait_ge(step.sem, step.done_by(ins))

                def cols(t, b):
                    return t[:, CPI * b:CPI * (b + 1)]

                def count(values, limit, op):
                    for b in range(B):
                        ins = nc.vector.tensor_scalar(cols(cmp, b), cols(values, b), limit(b), None, op, ALU.add, accum_out=cnt[:, b:b + 1])
                    ins.then_inc(counted, 1)
                    trips[0] += 1
                    v.wait_ge(summed, trips[0])

                def bit_column(t):
                    return lambda b: t[:, b:b + 1]

                spans.constants()
                do(nc.vector.memset(ones[:, :], 1.0))
                v.wait_ge(loaded, 16)
                count(score_sb, lambda b: 0.0, ALU.is_ge)
                do(nc.vector.tensor_scalar(sgn[:, :], tot[:, :], float(KSEL), 2.0, ALU.is_ge, ALU.mult))
                do(nc.vector.tensor_scalar(sgn[:, :], sgn[:, :], 1.0, None, ALU.subtract))
                mid, half = (TPI + 1) / 2, KSEL - (TPI + 1) / 2
                do(nc.vector.tensor_scalar(need[:, :], sgn[:, :], half, mid, ALU.mult, ALU.add))
                for b in range(B):
                    ins = nc.vector.tensor_scalar(cols(ws, b), cols(score_sb, b), sgn[:, b:b + 1], None, ALU.mult)
                do(ins)
                do(nc.vector.memset(cur[:, :], 0))
                for bit in range(30, -1, -1):
                    do(nc.vector.tensor_scalar(cand[:, :], cur[:, :], 1 << bit, None, ALU.bitwise_or))
                    count(ws, lambda b: cand[:, b:b + 1].bitcast(F32), ALU.is_ge)
                    do(nc.vector.tensor_tensor(keep[:, :], tot[:, :], need[:, :], ALU.is_ge))
                    do(nc.vector.scalar_tensor_tensor(cur[:, :], keep[:, :], bit, cur[:, :], ALU.logical_shift_left, ALU.bitwise_or))
                do(nc.vector.tensor_tensor(thr[:, :], cur[:, :].bitcast(F32), sgn[:, :], ALU.mult))
                count(score_sb, bit_column(thr), ALU.is_gt)
                do(nc.vector.tensor_scalar(need[:, :], tot[:, :], -1.0, float(KSEL), ALU.mult, ALU.add))
                for b in range(B):
                    ins = nc.vector.tensor_scalar(cols(tie, b), cols(score_sb, b), thr[:, b:b + 1], 1e6, ALU.not_equal, ALU.mult)
                do(ins)
                do(nc.vector.tensor_tensor(tie[:, :], tie[:, :], ridx[:, :], ALU.add))
                do(nc.vector.memset(cut[:, :], 0.0))
                for bit in range(13, -1, -1):
                    do(nc.vector.tensor_scalar(cutc[:, :], cut[:, :], float(1 << bit), None, ALU.add))
                    count(tie, bit_column(cutc), ALU.is_lt)
                    do(nc.vector.tensor_tensor(cutc[:, :], tot[:, :], need[:, :], ALU.is_lt))
                    do(nc.vector.scalar_tensor_tensor(cut[:, :], cutc[:, :], float(1 << bit), cut[:, :], ALU.mult, ALU.add))
                for b in range(B):
                    nc.vector.tensor_scalar(cols(cmp, b), cols(score_sb, b), thr[:, b:b + 1], None, ALU.is_gt)
                    ins = nc.vector.tensor_scalar(cols(tie, b), cols(tie, b), cut[:, b:b + 1], None, ALU.is_le)
                do(ins)
                do(nc.vector.tensor_tensor(cmp[:, :], cmp[:, :], tie[:, :], ALU.add))
                do(nc.vector.tensor_tensor(gate_sb[:, :], cmp[:, :], score_sb[:, :], ALU.mult))
                spans.indices(v)
        clear(nc, (loaded, counted, summed, step.sem, *spans.sems))


class Trip:

    def __init__(self, eng, sems, count, span, i, u):
        self.eng, self.sems, self.count, self.span, self.i, self.u = eng, sems, count, span, i, u
        self.t = i * span + u

    def next(self):
        return Trip(self.eng, self.sems, self.count, self.span, self.i, self.u + 1)

    def has(self, off):
        return not isinstance(self.t, int) or 0 <= self.t + off < self.count

    def wait(self, name, off, per=1, k=None):
        if self.has(off):
            self.eng.wait_ge(self.sems[name], (self.t + off) * per + (per if k is None else k))

    def wait_slot(self, name, off):
        self.wait_lot(name, off, 16)

    def wait_lot(self, name, off, lot):
        if self.has(off):
            self.eng.wait_ge(self.sems[f"{name}{self.slot(off)}"], self.turns(off) * lot)

    def turns(self, off):
        return self.i * (self.span // 2) + ((self.u + off) // 2 + 1)

    def slot(self, off):
        return (self.u + off) % 2


def trips(eng, sems, count, span, ahead, behind, emit, peel=1):
    for t in range(-ahead, peel * span):
        emit(Trip(eng, sems, count, span, t // span, t % span))
    with eng.Fori(peel, count // span - 1) as i:
        for u in range(span):
            emit(Trip(eng, sems, count, span, i, u))
    for t in range(count - span, count + behind):
        emit(Trip(eng, sems, count, span, t // span, t % span))


def image_rows(nc, strip, half, rows):
    if isinstance(strip, int):
        b, i = strip // SPI, strip % SPI
        return b * PADW + (WIN * i + SHIFT + SHIFT * half) % H
    row = strip * WIN + ((strip * 147) >> 11) * 2 + SHIFT + SHIFT * half
    if half:
        row = row - last_row(None, strip) * H
    return nc.s_assert_within(row, 0, B * PADW - rows, skip_runtime_bounds_check_because="strip < STRIPS")


def token_row(nc, strip, half):
    if isinstance(strip, int):
        b, i = strip // SPI, strip % SPI
        return b * H + (WIN * i + SHIFT + SHIFT * half) % H
    row = strip * WIN + SHIFT + SHIFT * half
    if half:
        row = row - last_row(None, strip) * H
    return nc.s_assert_within(row, 0, B * H - SHIFT, skip_runtime_bounds_check_because="strip < STRIPS")


def routed_ffn(nc, d, x1_dram, x2_dram, stats_sb, gate_sb, pixels):
    HID = 4 * C
    with ExitStack() as ctx:
        def sb(name, shape, dt=F32):
            return ctx.enter_context(nc.sbuf_tensor("ff_" + name, shape, dt))

        def two(name, shape, dt=F32):
            return [sb(f"{name}{i}", shape, dt) for i in range(2)]

        def ps(name, shape, dt=F32):
            return ctx.enter_context(nc.psum_tensor("ff_" + name, shape, dt))

        ident = sb("ident", [P, P])
        identb = sb("identb", [P, P], BF16)
        w1 = sb("w1", [P, HID])
        w2 = sb("w2", [P, 4, C])
        b1 = sb("b1", [P, 4])
        b2 = sb("b2", [1, C])
        ones = sb("ones", [1, P])
        half = sb("half", [P, PPS])
        x1, t1, t12, x2 = (two(n, [P, PPS, C]) for n in ("x1", "t1", "t12", "x2"))
        tT = two("tT", [P, PPS * P])
        gate = two("gate", [P, PPS])
        hT = [sb(f"hT{h}", [P, 4, 448]) for h in range(2)]
        st = two("st", [P, PPS, 6])
        mv = two("mv", [P, PPS, 2])
        ve = two("ve", [P, PPS])
        rstd = two("rstd", [P, PPS])
        xq = two("xq", [P, PPS, C])
        xi = two("xi", [P, PPS, C], BF16)
        p_t = [ps(f"p_t{i}", [P, 512]) for i in range(2)]
        p_h = [ps(f"p_h{i}", [P, 512]) for i in range(2)]
        p_y = [ps(f"p_y{i}", [P, 4, P]) for i in range(2)]
        p_q = ps("p_q", [P, 1024], BF16)
        S = {n: ctx.enter_context(nc.semaphore("ff_" + n)) for n in (
            "consts_in", "ready", "x_in0", "x_in1", "x_out0", "x_out1", "t1", "t12", "trp", "tT", "hp", "hT", "yp",
            "x2", "stat", "ve", "rstd", "xq", "xi", "qp", "pix", "passed")}
        groups = ((0, 4), (4, 7))

        with nc.Block() as block:
            @block.sync
            def _(sp):
                for dst, src in ((ident[:, :], d["ident"]), (w1[:, :], d["f_w1"]), (w2[:, :, :], d["f_w2"]),
                                 (b1[:, :], d["f_b1"]), (b2[:, :], d["f_b2"])):
                    sp.dma_start(dst, src).then_inc(S["consts_in"], 16)

                def emit(p):
                    if p.has(2):
                        p.wait("t1", 0)
                        p.wait("t12", 0)
                        sp.dma_start(x1[p.slot(2)][:, :, :], x1_dram[bass.ds(p.t + 2, 1)].rearrange("o p u c -> (o p) u c")).then_inc(S[f"x_in{p.slot(2)}"], 16)
                    if p.has(0):
                        p.wait("x2", 0, 2)
                        s = p.slot(0)
                        for w in range(2):
                            for j in range(PPS):
                                dst = bass.AP(x2_dram.tensor, p.t * (W * WIN * C) + (2 * j + w) * WIN * WIN * C,
                                              [[C, WIN], [WIN * C, WIN], [1, C]])
                                sp.dma_start(dst, x2[s][64 * w:64 * w + 64, j, :]).then_inc(S[f"x_out{s}"], 16)
                trips(sp, S, STRIPS, 2, 2, 0, emit)
                for s in range(2):
                    sp.wait_ge(S[f"x_out{s}"], X2_OUT * (STRIPS // 2))

            @block.tensor
            def _(pe):
                pe.wait_ge(S["consts_in"], 16 * 5)
                pe.wait_ge(S["ready"], 1)

                def emit(p):
                    if p.has(0):
                        s = p.slot(0)
                        for n in range(8):
                            h, m = n // 4, n % 4
                            p.wait("tT", 0, 2)
                            if n < 2:
                                p.wait("hT", -1, 8, 7 + n)
                            else:
                                p.wait("hT", 0, 8, n - 1)
                            nc.tensor.matmul(p_h[n % 2][:, 0:448], w1[:, P * m:P * (m + 1)], tT[s][:, 448 * h:448 * h + 448],
                                             start=True, stop=True).then_inc(S["hp"], 1)
                    if p.has(1):
                        for g, (a, b) in enumerate(groups):
                            p.wait("t1", 1)
                            p.wait("tT", 0, 2, g + 1)
                            for j in range(a, b):
                                mm = nc.tensor.transpose(p_t[g][:, P * (j - a):P * (j - a + 1)], t1[p.slot(1)][:, j, :], ident[:, :])
                            mm.then_inc(S["trp"], 1)
                    if p.has(0):
                        for g, (a, b) in enumerate(groups):
                            p.wait("x2", -1, 2, g + 1)
                            for j in range(a, b):
                                p.wait("hT", 0, 8, 4 if (j + 1) * P <= 448 else 8)
                                for m in range(4):
                                    lo, hi = j * P, (j + 1) * P
                                    for h in range(2):
                                        x, y = max(lo, 448 * h), min(hi, 448 * h + 448)
                                        if x < y and hi - lo == y - x:
                                            nc.tensor.matmul(p_y[g][:, j - a, :], hT[h][:, m, x - 448 * h:y - 448 * h], w2[:, m, :],
                                                             start=m == 0, stop=False)
                                        elif x < y:
                                            nc.tensor.matmul(p_y[g][x - lo:y - lo, j - a, :], hT[h][:, m, x - 448 * h:y - 448 * h], w2[:, m, :],
                                                             start=m == 0, stop=False)
                                mm = nc.tensor.matmul(p_y[g][:, j - a, :], ones[:, :], b2[:, :], start=False, stop=True)
                            mm.then_inc(S["yp"], 1)
                    if p.has(-1):
                        p.wait("xi", -1)
                        p.wait("pix", -2)
                        for j in range(PPS):
                            mm = nc.tensor.transpose(p_q[:, P * j:P * (j + 1)], xi[p.slot(-1)][:, j, :], identb[:, :])
                        mm.then_inc(S["qp"], 1)
                trips(pe, S, STRIPS, 2, 1, 1, emit)

            @block.gpsimd
            def _(pool):
                def emit(p):
                    if p.has(1):
                        s = p.slot(1)
                        p.wait("t1", 1)
                        p.wait("x2", -1, 2)
                        nc.gpsimd.tensor_tensor(t12[s][:, :, :], x1[s][:, :, :], t1[s][:, :, :], ALU.add).then_inc(S["t12"], 1)
                    if p.has(0):
                        s = p.slot(0)
                        p.wait("ve", 0)
                        nc.gpsimd.tensor_tensor(rstd[s][:, :], ve[s][:, :], half[:, :], ALU.pow).then_inc(S["rstd"], 1)
                trips(pool, S, STRIPS, 2, 1, 1, emit)

            @block.scalar
            def _(act):
                act.wait_ge(S["consts_in"], 16 * 5)

                def emit(p):
                    if p.has(0):
                        s = p.slot(0)
                        for n in range(8):
                            h, m = n // 4, n % 4
                            p.wait("hp", 0, 8, n + 1)
                            if n % 4 == 0:
                                p.wait("yp", -1, 2, h + 1)
                            nc.scalar.activation(hT[h][:, m, :], p_h[n % 2][:, 0:448], ACT.Gelu_apprx_tanh, bias=b1[:, m:m + 1]).then_inc(S["hT"], 1)
                    if p.has(1):
                        for g, (a, b) in enumerate(groups):
                            p.wait("trp", 1, 2, g + 1)
                            p.wait("hp", -1, 8)
                            nc.scalar.activation(tT[p.slot(1)][:, P * a:P * b], p_t[g][:, 0:P * (b - a)], ACT.Copy).then_inc(S["tT"], 1)
                    if p.has(-1):
                        p.wait("qp", -1)
                        q = p_q[:, 0:PPS * P].rearrange("p (k r c) -> p r k c", k=14, r=WIN)
                        for hf in range(2):
                            rows = pixels[:, bass.ds(image_rows(nc, p.t - 1, hf, 6) + 1, SHIFT), :]
                            src = q[:, SHIFT * hf:SHIFT * hf + SHIFT, :, :]
                            nc.scalar.activation(rows[:, :, 5:109].rearrange("p r (k c) -> p r k c", c=WIN), src[:, :, 0:13, :], ACT.Copy)
                            nc.scalar.activation(rows[:, :, 109:113], src[:, :, 13, 0:4], ACT.Copy)
                            ins = nc.scalar.activation(rows[:, :, 1:5], src[:, :, 13, 4:8], ACT.Copy)
                        ins.then_inc(S["pix"], 1)
                trips(act, S, STRIPS, 2, 1, 1, emit)

            @block.vector
            def _(v):
                nc.vector.memset(pixels[:, 0:B * PADW:PADW, :], 0.0)
                nc.vector.memset(pixels[:, PADW - 1:B * PADW:PADW, :], 0.0)
                inner = pixels[:, :, :].rearrange("p (b y) x -> p b y x", b=B)[:, :, 1:PADW - 1, :]
                nc.vector.memset(inner[:, :, :, 0:1], 0.0)
                nc.vector.memset(inner[:, :, :, PADW - 1:PADW], 0.0)
                nc.vector.memset(half[:, :], -0.5)
                nc.vector.memset(ones[:, :], 1.0)
                v.wait_ge(S["consts_in"], 16 * 5)
                nc.vector.tensor_copy(identb[:, :], ident[:, :]).then_inc(S["ready"], 1)
                v.wait_ge(S["ready"], 1)

                def emit(p):
                    if p.has(1):
                        s = p.slot(1)
                        p.wait_slot("x_in", 1)
                        p.wait("trp", -1, 2)
                        p.wait("t12", -1)
                        for j in range(PPS):
                            col = stats_sb[:, bass.ds((p.t + 1) * PPS + j, 1), :].rearrange("p o k -> p (o k)")
                            ins = nc.vector.tensor_scalar(t1[s][:, j, :], x1[s][:, j, :], col[:, 0:1], col[:, 1:2], ALU.subtract, ALU.mult)
                        ins.then_inc(S["t1"], 1)
                        nc.vector.tensor_copy(gate[s][:, :], gate_sb[:, bass.ds((p.t + 1) * PPS, PPS)])
                    if p.has(-1):
                        s = p.slot(-1)
                        p.wait("rstd", -1)
                        nc.vector.tensor_scalar(rstd[s][:, :], rstd[s][:, :], 3.0, None, ALU.mult).then_inc(S["xq"], 1)
                        p.wait("xq", -1, 3, 1)
                        for j in range(PPS):
                            ins = nc.vector.tensor_scalar(xq[s][:, j, :], x2[s][:, j, :], mv[s][:, j, 0:1], rstd[s][:, j:j + 1], ALU.subtract, ALU.mult)
                        ins.then_inc(S["xq"], 1)
                        p.wait("xq", -1, 3, 2)
                        nc.vector.tensor_scalar(xq[s][:, :, :], xq[s][:, :, :], 0.0, 3.0, ALU.max, ALU.min).then_inc(S["xq"], 1)
                        p.wait("xq", -1, 3, 3)
                        p.wait("qp", -3)
                        nc.vector.tensor_scalar(xi[s][:, :, :], xq[s][:, :, :], MAGIC, MAGIC, ALU.add, ALU.subtract).then_inc(S["xi"], 1)
                    if p.has(0):
                        s = p.slot(0)
                        p.wait("t12", 0)
                        p.wait_lot("x_out", -2, X2_OUT)
                        for g, (a, b) in enumerate(groups):
                            p.wait("yp", 0, 2, g + 1)
                            for j in range(a, b):
                                ins = nc.vector.scalar_tensor_tensor(x2[s][:, j, :], p_y[g][:, j - a, :], gate[s][:, j:j + 1], t12[s][:, j, :], ALU.mult, ALU.add)
                            ins.then_inc(S["x2"], 1)
                        p.wait("x2", 0, 2)
                        for j in range(PPS):
                            ins = nc.vector.bn_stats(st[s][:, j, :], x2[s][:, j, :])
                        ins.then_inc(S["stat"], 1)
                        p.wait("stat", 0, 2, 1)
                        v.sem_inc(S["passed"], 1)
                        for j in range(PPS):
                            ins = nc.vector.bn_aggr(mv[s][:, j, :], st[s][:, j, :])
                        ins.then_inc(S["stat"], 1)
                        p.wait("stat", 0, 2)
                        nc.vector.tensor_scalar(ve[s][:, :], mv[s][:, :, 1], 1e-6, None, ALU.add).then_inc(S["ve"], 1)
                trips(v, S, STRIPS, 2, 1, 1, emit, peel=2)
        clear(nc, S.values())


TAPS = 9
ROWS = WIN
HROWS = ROWS // 2
FEAT = 16
GH = 4
REC = FEAT + 2 * GH


def convolve(nc, d, pixels, x2_dram, x3_dram, tT_dram, rec_dram, recs_dram, start_dram, adst_dram):
    with ExitStack() as ctx:
        def sb(name, shape, dt=F32):
            return ctx.enter_context(nc.sbuf_tensor("co_" + name, shape, dt))

        def two(name, shape, dt=F32):
            return [sb(f"{name}{i}", shape, dt) for i in range(2)]

        def ps(name, shape, dt=F32):
            return ctx.enter_context(nc.psum_tensor("co_" + name, shape, dt))

        ident = sb("ident", [P, P])
        w = sb("w", [P, TAPS, C])
        wt = sb("wt", [P, TAPS, C])
        wq = sb("wq", [P, TAPS, C], BF16)
        ext = sb("ext", [P, 4])
        gat = sb("gat", [P, 3, FEAT])
        att = sb("att", [P, 2, FEAT])
        wcat = sb("wcat", [P, REC])
        half = sb("half", [P, ROWS])
        win = two("win", [P, 2, HROWS + 2, PADW], BF16)
        x2, x3, t = (two(n, [W, ROWS, C]) for n in ("x2", "x3", "t"))
        st = two("st", [W, ROWS, 6])
        mv = two("mv", [W, ROWS, 2])
        ve = two("ve", [W, ROWS])
        rstd = two("rstd", [W, ROWS])
        tT = two("tT", [P, ROWS, W])
        rec = two("rec", [W, ROWS, REC])
        p_c = [ps(f"p_c{i}", [W, HROWS, P]) for i in range(2)]
        p_t = [ps(f"p_t{i}", [P, HROWS, W]) for i in range(2)]
        p_r = ps("p_r", [W, ROWS, REC])
        first_i = sb("first_i", [H, B, W], I32)
        first_f = sb("first_f", [H, B, W])
        first = sb("first", [W, B * H], I32)
        idx = two("idx", [W, ROWS], I32)
        p_f = ps("p_f", [W, B, H])
        own = {n: ctx.enter_context(nc.semaphore("co_" + n)) for n in (
            "consts_in", "tanh", "ext", "top", "wq", "x_in0", "x_in1", "out0", "out1", "win", "conv", "x3", "stat", "ve",
            "rstd", "t", "trp", "tT", "recp", "rec", "first", "firstp", "idx", "passed")}
        S = {**own, **dict(zip(("sc0", "sc1"), d["soft"][13:15]))}

        with nc.Block() as block:
            @block.sync
            def _(sp):
                for dst, src in ((w[:, :, :], d["c_w"].rearrange("t i o -> i t o")), (ident[:, :], d["ident"]),
                                 (gat[:, 0, :], d["g_wgat"]), (att[:, :, :], d["g_att"]),
                                 (first_i[:, :, :], start_dram.rearrange("p i -> (p i)").rearrange("(b y x) -> y b x", b=B, x=W))):
                    sp.dma_start(dst, src).then_inc(S["consts_in"], 16)

                def emit(p):
                    if p.has(1):
                        s = p.slot(1)
                        p.wait("x3", -1, 2)
                        base = (p.t + 1) * (W * ROWS * C)
                        for lo, n, c0 in ((SHIFT, W - SHIFT, 0), (0, SHIFT, W - SHIFT)):
                            src = bass.AP(x2_dram.tensor, base + c0 * ROWS * C, [[ROWS * C, n], [1, ROWS * C]])
                            sp.dma_start(x2[s][lo:lo + n, :, :].rearrange("p r c -> p (r c)"), src).then_inc(S[f"x_in{s}"], 16)
                    if p.has(-1):
                        s = p.slot(-1)
                        p.wait("rec", -1)
                        p.wait("tT", -1, 2)
                        sp.dma_start(tT_dram[:, bass.ds((p.t - 1) * (ROWS * W), ROWS * W)],
                                     tT[s][:, :, :].rearrange("p r x -> p (r x)")).then_inc(S[f"out{s}"], 16)
                        for dram, tile in ((x3_dram, x3), (recs_dram, rec)):
                            dst = dram.rearrange("(y x) c -> x y c", x=W)[:, bass.ds((p.t - 1) * ROWS, ROWS), :]
                            sp.dma_start(dst, tile[s][:, :, :]).then_inc(S[f"out{s}"], 16)
                        for h in range(2):
                            dst = rec_dram.rearrange("(y x) c -> x y c", x=W)[:, bass.ds(token_row(nc, p.t - 1, h), HROWS), :]
                            sp.dma_start(dst, rec[s][:, HROWS * h:HROWS * h + HROWS, :]).then_inc(S[f"out{s}"], 16)
                trips(sp, S, STRIPS, 2, 1, 1, emit)
                for s in range(2):
                    sp.wait_ge(S[f"out{s}"], CONV_OUT * (STRIPS // 2))

            @block.tensor
            def _(pe):
                pe.wait_ge(S["consts_in"], 16 * 5)
                pe.wait_ge(S["first"], 1)
                for b in range(B):
                    mm = nc.tensor.transpose(p_f[:, b, :], first_f[:, b, :], ident[0:H, 0:H])
                mm.then_inc(S["firstp"], 1)
                pe.wait_ge(S["wq"], 7)

                def emit(p):
                    if p.has(0):
                        s = p.slot(0)
                        p.wait("win", 0)
                        for h in range(2):
                            p.wait("x3", -1, 2, h + 1)
                            for r in range(HROWS):
                                for k in range(TAPS):
                                    dy, dx = k // 3, k % 3
                                    mm = nc.tensor.matmul(p_c[h][:, r, :], win[s][:, h, r + dy, dx:dx + W], wq[:, k, :],
                                                          start=k == 0, stop=k == TAPS - 1)
                            mm.then_inc(S["conv"], 1)
                    if p.has(-1):
                        s = p.slot(-1)
                        p.wait("t", -1)
                        for h in range(2):
                            p.wait("tT", -2, 2, h + 1)
                            for r in range(HROWS):
                                mm = nc.tensor.transpose(p_t[h][:, r, :], t[s][:, HROWS * h + r, :], ident[0:W, 0:W])
                            mm.then_inc(S["trp"], 1)
                        p.wait("tT", -1, 2)
                        p.wait("rec", -2)
                        for r in range(ROWS):
                            mm = nc.tensor.matmul(p_r[:, r, :], tT[s][:, r, :], wcat[:, :], start=True, stop=True)
                        mm.then_inc(S["recp"], 1)
                trips(pe, S, STRIPS, 2, 1, 1, emit)

            @block.gpsimd
            def _(pool):
                pool.wait_ge(S["ext"], 3)
                nc.gpsimd.partition_all_reduce(ext[:, 3:4], ext[:, 2:3], P, bass.bass_isa.ReduceOp.max).then_inc(S["top"], 1)

                def emit(p):
                    if p.has(0):
                        s = p.slot(0)
                        p.wait("ve", 0)
                        nc.gpsimd.tensor_tensor(rstd[s][:, :], ve[s][:, :], half[0:W, :], ALU.pow).then_inc(S["rstd"], 1)
                    if p.has(-1):
                        s = p.slot(-1)
                        p.wait_lot("sc", -3, ROWS * 16)
                        p.wait("rec", -1)
                        pool.sem_inc(S["passed"], 1)
                        nc.gpsimd.tensor_copy(idx[s][:, :], first[:, bass.ds((p.t - 1) * ROWS, ROWS)]).then_inc(S["idx"], 1)
                        p.wait("idx", -1)
                        pool.sem_inc(S["passed"], 1)
                        for r in range(ROWS):
                            nc.gpsimd.indirect_dma_start(out=adst_dram, out_offset=bass.IndirectOffsetOnAxis(ap=idx[s][:, r:r + 1], axis=0),
                                                         in_=rec[s][:, r, FEAT + GH:REC], in_offset=None, bounds_check=E - 1,
                                                         oob_is_err=False).then_inc(S[f"sc{s}"], 16)
                pool.wait_ge(S["first"], 2)
                trips(pool, S, STRIPS, 2, 0, 1, emit, peel=2)
                for s in range(2):
                    pool.wait_ge(S[f"sc{s}"], ROWS * 16 * (STRIPS // 2))

            @block.scalar
            def _(act):
                act.wait_ge(S["consts_in"], 16 * 5)
                nc.scalar.activation(wt[:, :, :], w[:, :, :], ACT.Tanh).then_inc(S["tanh"], 1)

                def emit(p):
                    if p.has(1):
                        s = p.slot(1)
                        p.wait("conv", -1, 2)
                        for h in range(2):
                            rows = bass.ds(image_rows(nc, p.t + 1, h, HROWS + 2), HROWS + 2)
                            ins = nc.scalar.activation(win[s][:, h, :, :], pixels[:, rows, :], ACT.Copy)
                        ins.then_inc(S["win"], 1)
                    if p.has(-1):
                        s = p.slot(-1)
                        for h in range(2):
                            p.wait("trp", -1, 2, h + 1)
                            if h == 0:
                                p.wait_lot("out", -3, CONV_OUT)
                            nc.scalar.activation(tT[s][:, HROWS * h:HROWS * h + HROWS, :], p_t[h][:, :, :], ACT.Copy).then_inc(S["tT"], 1)
                        p.wait("recp", -1)
                        p.wait_lot("sc", -3, ROWS * 16)
                        nc.scalar.activation(rec[s][:, :, :], p_r[:, :, :], ACT.Copy).then_inc(S["rec"], 1)
                trips(act, S, STRIPS, 2, 1, 1, emit, peel=2)

            @block.vector
            def _(v):
                nc.vector.memset(half[:, :], -0.5)
                v.wait_ge(S["consts_in"], 16 * 5)
                nc.vector.tensor_copy(first_f[:, :, :], first_i[:, :, :]).then_inc(S["first"], 1)
                v.wait_ge(S["firstp"], 1)
                nc.vector.tensor_copy(first[:, :], p_f[:, :, :].rearrange("x b y -> x (b y)")).then_inc(S["first"], 1)
                for k in range(2):
                    nc.vector.tensor_tensor(gat[:, 1 + k, :], gat[:, 0, :], att[:, k, :], ALU.mult)
                nc.vector.tensor_copy(wcat[:, 0:FEAT], gat[:, 0, :]).then_inc(S["wq"], 1)
                v.wait_ge(S["wq"], 1)
                nc.vector.tensor_reduce(wcat[:, FEAT:FEAT + 2 * GH].rearrange("p (k h) -> p k h", k=2),
                                        gat[:, 1:3, :].rearrange("p k (h e) -> p k h e", e=GH), AX_X, ALU.add).then_inc(S["wq"], 1)
                v.wait_ge(S["tanh"], 1)
                nc.vector.tensor_reduce(ext[:, 0:1], wt[:, :, :].rearrange("p t c -> p (t c)"), AX_X, ALU.max)
                nc.vector.tensor_reduce(ext[:, 1:2], wt[:, :, :].rearrange("p t c -> p (t c)"), AX_X, ALU.min).then_inc(S["ext"], 1)
                v.wait_ge(S["ext"], 1)
                nc.vector.tensor_scalar(ext[:, 1:2], ext[:, 1:2], -1.0, None, ALU.mult).then_inc(S["ext"], 1)
                v.wait_ge(S["ext"], 2)
                nc.vector.tensor_tensor(ext[:, 2:3], ext[:, 0:1], ext[:, 1:2], ALU.max).then_inc(S["ext"], 1)
                v.wait_ge(S["top"], 1)
                nc.vector.reciprocal(ext[:, 0:1], ext[:, 3:4]).then_inc(S["wq"], 1)
                v.wait_ge(S["wq"], 3)
                nc.vector.tensor_scalar(wt[:, :, :], wt[:, :, :], ext[:, 0:1], 0.5, ALU.mult, ALU.mult).then_inc(S["wq"], 1)
                v.wait_ge(S["wq"], 4)
                nc.vector.tensor_scalar(wt[:, :, :], wt[:, :, :], 0.5, 3.0, ALU.add, ALU.mult).then_inc(S["wq"], 1)
                v.wait_ge(S["wq"], 5)
                nc.vector.tensor_scalar(wt[:, :, :], wt[:, :, :], MAGIC, MAGIC, ALU.add, ALU.subtract).then_inc(S["wq"], 1)
                v.wait_ge(S["wq"], 6)
                nc.vector.tensor_scalar(wq[:, :, :], wt[:, :, :], 2.0, 3.0, ALU.mult, ALU.subtract).then_inc(S["wq"], 1)

                def emit(p):
                    if p.has(0):
                        s = p.slot(0)
                        p.wait_lot("x_in", 0, 32)
                        p.wait_lot("out", -2, CONV_OUT)
                        for h in range(2):
                            rr = slice(HROWS * h, HROWS * h + HROWS)
                            p.wait("conv", 0, 2, h + 1)
                            nc.vector.scalar_tensor_tensor(x3[s][:, rr, :], p_c[h][:, :, :], 1.0 / 9.0, x2[s][:, rr, :], ALU.mult, ALU.add).then_inc(S["x3"], 1)
                        p.wait("x3", 0, 2)
                        for r in range(ROWS):
                            ins = nc.vector.bn_stats(st[s][:, r, :], x3[s][:, r, :])
                        ins.then_inc(S["stat"], 1)
                        p.wait("stat", 0, 2, 1)
                        v.sem_inc(S["passed"], 1)
                        for r in range(ROWS):
                            ins = nc.vector.bn_aggr(mv[s][:, r, :], st[s][:, r, :])
                        ins.then_inc(S["stat"], 1)
                        p.wait("stat", 0, 2)
                        nc.vector.tensor_scalar(ve[s][:, :], mv[s][:, :, 1], 1e-5, None, ALU.add).then_inc(S["ve"], 1)
                        p.wait("rstd", 0)
                        p.wait("trp", -2, 2)
                        for r in range(ROWS):
                            ins = nc.vector.tensor_scalar(t[s][:, r, :], x3[s][:, r, :], mv[s][:, r, 0:1], rstd[s][:, r:r + 1], ALU.subtract, ALU.mult)
                        ins.then_inc(S["t"], 1)
                trips(v, S, STRIPS, 2, 1, 1, emit)
        clear(nc, own.values())


CONV_OUT = 5 * 16


def node_ids():
    return np.arange(M, dtype=np.float32).reshape(P, NPP)


IMG = H * W
ROLL = SHIFT * W
NONE = float(2 ** 21)
LOW = -1e30


def rolled(image):
    a = image * IMG
    return (a, a + ROLL, IMG - ROLL), (a + IMG - ROLL, a, ROLL)


class Search:

    def __init__(self, nc, ctx, d, dst_dram, first_dram):
        def sb(name, shape, dt=F32):
            return ctx.enter_context(nc.sbuf_tensor("es_" + name, shape, dt))

        def two(name, shape, dt=F32):
            return [sb(f"{name}{i}", shape, dt) for i in range(2)]
        self.nc, self.d, self.first_dram = nc, d, first_dram
        self.blocks = dst_dram.rearrange("(n e) -> n e", e=BLK)
        self.ids = sb("ids", [P, NPP])
        self.heads = sb("heads", [P, P])
        self.rp = sb("rp", [P, NPP])
        self.q, self.c0, self.c1, self.c2, self.r0, self.r1 = (two(n, [P, PPS]) for n in ("q", "c0", "c1", "c2", "r0", "r1"))
        self.i0, self.i1 = (two(n, [P, PPS], I32) for n in ("i0", "i1"))
        self.got0, self.got1 = (two(n, [P, PPS, BLK]) for n in ("got0", "got1"))
        self.junk = sb("junk", [P, PPS, P])
        self.own = {n: ctx.enter_context(nc.semaphore("es_" + n)) for n in ("lv0", "lv1", "lv2", "passed")}
        self.S = {**self.own, **dict(zip(("first0", "first1", "block0", "block1"), d["soft"][0:4]))}

    def load(self):
        nc, d = self.nc, self.d
        with ExitStack() as ctx:
            ident, diag, ones = (ctx.enter_context(nc.sbuf_tensor("es_" + n, [P, P], F32)) for n in ("ident", "diag", "ones"))
            mine = ctx.enter_context(nc.sbuf_tensor("es_mine", [P, EP // BLK], F32))
            p_heads = ctx.enter_context(nc.psum_tensor("es_p", [P, P], F32))
            loaded, ready, summed = (ctx.enter_context(nc.semaphore("es_" + n)) for n in ("loaded", "ready", "summed"))
            with nc.Block() as block:
                @block.sync
                def _(sp):
                    for dst, src in ((self.ids[:, :], d["node_ids"]), (ident[:, :], d["ident"]), (mine[:, :], self.first_dram)):
                        sp.dma_start(dst, src).then_inc(loaded, 16)

                @block.tensor
                def _(pe):
                    pe.wait_ge(ready, 2)
                    nc.tensor.matmul(p_heads[:, :], ones[:, :], diag[:, :], start=True, stop=True).then_inc(summed, 1)

                @block.vector
                def _(v):
                    nc.vector.memset(ones[:, :], 1.0).then_inc(ready, 1)
                    v.wait_ge(loaded, 48)
                    nc.vector.tensor_scalar(diag[:, :], ident[:, :], mine[:, 0:1], None, ALU.mult).then_inc(ready, 1)
                    v.wait_ge(summed, 1)
                    nc.vector.tensor_copy(self.heads[:, :], p_heads[:, :])
            clear(nc, (loaded, ready, summed))

    def wait(self, eng, name, at, per, k=None, back=0):
        item = at[0] * 2 + at[1] - back
        if not isinstance(item, int) or item >= 0:
            eng.wait_ge(self.S[name], item * per + (per if k is None else k))

    def wait_gathers(self, eng, name, at, back=0):
        c = at[1] - back
        if not isinstance(at[0], int) or at[0] * 2 + c >= 0:
            eng.wait_ge(self.S[f"{name}{c % 2}"], (at[0] + (c // 2 + 1)) * (PPS * 16))

    def gather_firsts(self, pool, at, cols):
        s = at[1] % 2
        self.wait(pool, "lv0", at, 4)
        self.wait(pool, "lv1", at, 4, back=2)
        pool.sem_inc(self.S["passed"], 1)
        for j in cols:
            self.nc.gpsimd.indirect_dma_start(out=self.got0[s][:, j, :], out_offset=None, in_=self.first_dram,
                                              in_offset=bass.IndirectOffsetOnAxis(ap=self.i0[s][:, j:j + 1], axis=0)).then_inc(self.S[f"first{s}"], 16)

    def gather_blocks(self, pool, at, cols):
        s = at[1] % 2
        self.wait(pool, "lv1", at, 4)
        self.wait(pool, "lv2", at, 3, back=2)
        pool.sem_inc(self.S["passed"], 1)
        for j in cols:
            self.nc.gpsimd.indirect_dma_start(out=self.got1[s][:, j, :], out_offset=None, in_=self.blocks,
                                              in_offset=bass.IndirectOffsetOnAxis(ap=self.i1[s][:, j:j + 1], axis=0)).then_inc(self.S[f"block{s}"], 16)

    def count(self, out, q, table):
        for j in range(PPS):
            t = table(j)
            ins = self.nc.vector.tensor_scalar(self.junk[:, j, 0:t.shape[-1]], t, q[:, j:j + 1], None, ALU.is_lt, ALU.add, accum_out=out[:, j:j + 1])
        return ins

    def partition_of(self, v, at):
        s, S, vec = at[1] % 2, self.S, self.nc.vector
        self.wait_gathers(v, "first", at, back=2)
        vec.tensor_copy(self.q[s][:, :], self.ids[:, bass.ds((at[0] * 2 + at[1]) * PPS, PPS)]).then_inc(S["lv0"], 1)
        self.wait(v, "lv0", at, 4, 1)
        self.count(self.c0[s], self.q[s], lambda j: self.heads[:, :]).then_inc(S["lv0"], 1)
        self.wait(v, "lv0", at, 4, 2)
        vec.tensor_scalar(self.r0[s][:, :], self.c0[s][:, :], 1.0, 0.0, ALU.subtract, ALU.max).then_inc(S["lv0"], 1)
        self.wait(v, "lv0", at, 4, 3)
        vec.tensor_copy(self.i0[s][:, :], self.r0[s][:, :]).then_inc(S["lv0"], 1)

    def block_of(self, v, at):
        s, S, vec = at[1] % 2, self.S, self.nc.vector
        self.wait_gathers(v, "first", at)
        self.wait_gathers(v, "block", at, back=2)
        self.count(self.c1[s], self.q[s], lambda j: self.got0[s][:, j, :]).then_inc(S["lv1"], 1)
        self.wait(v, "lv1", at, 4, 1)
        vec.tensor_scalar(self.c1[s][:, :], self.c1[s][:, :], 1.0, 0.0, ALU.subtract, ALU.max).then_inc(S["lv1"], 1)
        self.wait(v, "lv1", at, 4, 2)
        vec.scalar_tensor_tensor(self.r1[s][:, :], self.r0[s][:, :], float(EP // BLK), self.c1[s][:, :], ALU.mult, ALU.add).then_inc(S["lv1"], 1)
        self.wait(v, "lv1", at, 4, 3)
        vec.tensor_copy(self.i1[s][:, :], self.r1[s][:, :]).then_inc(S["lv1"], 1)

    def edge_of(self, v, at):
        s, S, vec = at[1] % 2, self.S, self.nc.vector
        self.wait_gathers(v, "block", at)
        self.count(self.c2[s], self.q[s], lambda j: self.got1[s][:, j, :]).then_inc(S["lv2"], 1)
        self.wait(v, "lv2", at, 3, 1)
        vec.scalar_tensor_tensor(self.c0[s][:, :], self.r1[s][:, :], float(BLK), self.c2[s][:, :], ALU.mult, ALU.add).then_inc(S["lv2"], 1)
        self.wait(v, "lv2", at, 3, 2)
        vec.tensor_copy(self.rp[:, bass.ds((at[0] * 2 + at[1]) * PPS, PPS)], self.c0[s][:, :]).then_inc(S["lv2"], 1)


class Spans:

    def __init__(self, nc, ctx, rp_sb, rp_dram, rps_dram, start_dram, end_dram, adst_dram, carry_dram):
        def sb(name, shape, dt=F32):
            return ctx.enter_context(nc.sbuf_tensor("sp_" + name, shape, dt))
        self.nc, self.rp_sb = nc, rp_sb
        self.drams = rp_dram, rps_dram, start_dram, end_dram, adst_dram, carry_dram
        self.lo, self.hi, self.none, self.at = (sb(n, [P, NPP]) for n in ("lo", "hi", "none", "at"))
        self.start, self.end = (sb(n, [P, NPP], I32) for n in ("start", "end"))
        self.zero = sb("zero", [P, EP])
        self.low = sb("low", [P, NPP // 7, REC])
        self.total = sb("total", [1, 1])
        self.saved, self.copied, self.loaded, step, self.stored = self.sems = [
            ctx.enter_context(nc.semaphore("sp_" + n)) for n in ("saved", "copied", "loaded", "step", "stored")]
        self.step = Steps(step)

    def tables(self, sp):
        rp_dram, rps_dram, _, _, adst_dram, carry_dram = self.drams
        sp.wait_ge(self.step.sem, 1)
        sp.dma_start(rp_dram[0:M].rearrange("(p i) -> p i", p=P), self.rp_sb[:, :]).then_inc(self.saved, 16)
        sp.dma_start(rp_dram[M:M + 1].rearrange("(p i) -> p i", p=1), self.total[:, :]).then_inc(self.saved, 16)
        sp.wait_ge(self.saved, 32)
        for b in range(B):
            for seq, node, n in rolled(b):
                for k in range(2):
                    sp.dma_start(rps_dram[k:k + 1, seq:seq + n], rp_dram[node + k:node + k + n].rearrange("(o n) -> o n", o=1)).then_inc(self.copied, 16)
        sp.wait_ge(self.copied, 16 * 4 * B)
        for k, tile in ((0, self.lo), (1, self.hi)):
            sp.dma_start(tile[:, :], rps_dram[k:k + 1, :].rearrange("o (p i) -> (o p) i", p=P)).then_inc(self.loaded, 16)
        sp.wait_ge(self.step.sem, 3)
        flat = adst_dram.rearrange("(p e) h -> p (e h)", p=P)
        for k in range(GH):
            sp.dma_start(flat[:, EP * k:EP * (k + 1)], self.zero[:, :]).then_inc(self.stored, 16)
        flat = carry_dram.rearrange("(p i) c -> p (i c)", p=P)
        for k in range(7):
            n = NPP // 7 * REC
            sp.dma_start(flat[:, n * k:n * (k + 1)], self.low[:, :, :].rearrange("p i c -> p (i c)")).then_inc(self.stored, 16)

    def store(self, sp):
        _, _, start_dram, end_dram, _, _ = self.drams
        sp.wait_ge(self.step.sem, 7)
        sp.dma_start(start_dram, self.start[:, :]).then_inc(self.stored, 16)
        sp.dma_start(end_dram, self.end[:, :]).then_inc(self.stored, 16)
        sp.wait_ge(self.stored, 16 * (GH + 7 + 2))

    def constants(self):
        vec = self.nc.vector
        self.step.done_by(vec.memset(self.total[:, :], float(E)))
        vec.memset(self.low[:, :, 0:GH], LOW)
        self.step.done_by(vec.memset(self.low[:, :, GH:REC], 0.0))
        self.step.done_by(vec.memset(self.zero[:, :], 0.0))

    def indices(self, v):
        vec, step = self.nc.vector, self.step
        v.wait_ge(self.loaded, 32)
        step.done_by(vec.tensor_tensor(self.none[:, :], self.hi[:, :], self.lo[:, :], ALU.is_equal))
        v.wait_ge(step.sem, step.n)
        vec.scalar_tensor_tensor(self.at[:, :], self.none[:, :], NONE, self.hi[:, :], ALU.mult, ALU.add)
        step.done_by(vec.scalar_tensor_tensor(self.start[:, :], self.none[:, :], NONE, self.lo[:, :], ALU.mult, ALU.add))
        v.wait_ge(step.sem, step.n)
        step.done_by(vec.tensor_scalar(self.none[:, :], self.at[:, :], 1.0, None, ALU.subtract))
        v.wait_ge(step.sem, step.n)
        step.done_by(vec.tensor_copy(self.end[:, :], self.none[:, :]))


EXPERTS = 4
EH = 2 * C
CH = 64
CHUNKS = EP // CH
SROWS = 7
SLAB = SROWS * W
assert M // SLAB == CHUNKS
NG = 10


def graph_and_experts(nc, d, src_dram, dst_dram, same_dram, first_dram, rec_dram, adst_dram, tT_dram, scan_dram, carry_dram, y_dram):
    with ExitStack() as ctx:
        def sb(name, shape, dt=F32):
            return ctx.enter_context(nc.sbuf_tensor("gr_" + name, shape, dt))

        def two(name, shape, dt=F32):
            return [sb(f"{name}{i}", shape, dt) for i in range(2)]

        def ps(name, shape, dt=F32):
            return ctx.enter_context(nc.psum_tensor("gr_" + name, shape, dt))

        ident = sb("ident", [P, P])
        w1 = sb("w1", [P, EXPERTS * EH])
        w2 = sb("w2", [P, 2 * EXPERTS, C])
        b1 = sb("b1", [P, 2 * EXPERTS])
        b2 = sb("b2", [P, EXPERTS * C])
        tT = two("tT", [P, SLAB])
        hT = [sb("hT0", [P, 8, 4 * W]), sb("hT1", [P, 8, 3 * W])]
        y = two("y", [W, SROWS, EXPERTS * C])
        idx = two("idx", [P, CH], I32)
        same = two("same", [P, CH])
        start = two("start", [P, CH, GH])
        rec = two("rec", [P, CH, REC])
        ad = two("ad", [P, GH, CH])
        e = two("e", [P, GH, CH])
        ms = two("ms", [P, GH, CH + 1])
        pen = sb("pen", [P, CH])
        dd = sb("dd", [P, 2, GH, CH])
        ee = sb("ee", [P, 2, GH, CH])
        wt = sb("wt", [P, FEAT, CH])
        out = two("out", [P, CH, REC])
        heads, tails, prior, after = (sb(n, [P, CH]) for n in ("heads", "tails", "before", "after"))
        flag = sb("flag", [P, 8])
        headi = sb("headi", [P, 2], I32)
        headr = sb("headr", [P, REC])
        ends = sb("ends", [P, 3, 20])
        endT = sb("endT", [20, 3, P])
        cm = sb("cm", [20, P + 1])
        cs = sb("cs", [20, P + 1])
        cd = sb("cd", [20, 2, P])
        carry = sb("carry", [P, REC])
        p_h = [ps(f"p_h{i}", [P, 512]) for i in range(4)]
        p_y = [ps(f"p_y{i}", [W, EXPERTS, C]) for i in range(2)]
        p_e = ps("p_e", [20, 3, P])
        p_c = ps("p_c", [P, 2, 20])
        own = {n: ctx.enter_context(nc.semaphore("gr_" + n)) for n in (
            "consts_in", "set", "ld0", "ld1", "tin0", "tin1", "g", "ee", "ro0", "ro1",
            "hp", "hT", "yp", "y", "yo0", "yo1", "endp", "end", "cexp", "passed")}
        S = {**own, **dict(zip(("ga0", "ga1", "gb0", "gb1", "head_in", "carried"), d["soft"][5:11]))}

        with nc.Block() as block:
            @block.sync
            def _(sp):
                sp.wait_ge(S["set"], 1)
                edges = dst_dram.rearrange("(p e) -> p e", p=P)
                for dst, src in ((ident[:, :], d["ident"]), (w1[:, :], d["g_w1"]), (w2[:, :, :], d["g_w2"]), (b1[:, :], d["g_b1"]),
                                 (b2[:, :], d["g_b2"]), (heads[:, :], first_dram), (tails[:, :], edges[:, EP - CH:EP]),
                                 (prior[1:P, :], edges[0:P - 1, EP - CH:EP]), (after[0:P - 1, :], first_dram[1:P, :])):
                    sp.dma_start(dst, src).then_inc(S["consts_in"], 16)

                def emit(p):
                    if p.has(1):
                        s = p.slot(1)
                        p.wait_lot("ga", -1, CH // 2 * 16)
                        p.wait_lot("gb", -1, CH // 2 * 16)
                        p.wait("g", -1, NG)
                        cols = bass.ds((p.t + 1) * CH, CH)
                        sp.dma_start(idx[s][:, :], src_dram.rearrange("(p e) -> p e", p=P)[:, cols]).then_inc(S[f"ld{s}"], 16)
                        sp.dma_start(same[s][:, :], same_dram.rearrange("(p e) -> p e", p=P)[:, cols]).then_inc(S[f"ld{s}"], 16)
                        sp.dma_start(start[s][:, :, :], adst_dram.rearrange("(p e) h -> p e h", p=P)[:, cols, :]).then_inc(S[f"ld{s}"], 16)
                        p.wait("hp", -1, 16)
                        sp.dma_start(tT[s][:, :], tT_dram[:, bass.ds((p.t + 1) * SLAB, SLAB)]).then_inc(S[f"tin{s}"], 16)
                    if p.has(0):
                        s = p.slot(0)
                        p.wait("y", 0, SROWS)
                        dst = bass.AP(y_dram.tensor, p.t * (SLAB * EXPERTS * C), [[EXPERTS * C, W], [W * EXPERTS * C, SROWS], [1, EXPERTS * C]])
                        sp.dma_start(dst, y[s][:, :, :]).then_inc(S[f"yo{s}"], 16)
                    if p.has(-1):
                        s = p.slot(-1)
                        p.wait("g", -1, NG)
                        p.wait("ee", -1, 2)
                        sp.dma_start(scan_dram.rearrange("(p e) c -> p e c", p=P)[:, bass.ds((p.t - 1) * CH, CH), :], out[s][:, :, :]).then_inc(S[f"ro{s}"], 16)
                trips(sp, S, CHUNKS, 2, 1, 1, emit)
                for s in range(2):
                    sp.wait_ge(S[f"yo{s}"], 16 * (CHUNKS // 2))
                    sp.wait_ge(S[f"ro{s}"], 16 * (CHUNKS // 2))

            @block.gpsimd
            def _(pool):
                def emit(p):
                    if p.has(0):
                        s = p.slot(0)
                        p.wait_lot("ld", 0, 48)
                        p.wait("g", -2, NG, 8)
                        pool.sem_inc(S["passed"], 1)
                        for j in range(CH):
                            half = "ga" if j < CH // 2 else "gb"
                            nc.gpsimd.indirect_dma_start(out=rec[s][:, j, :], out_offset=None, in_=rec_dram,
                                                         in_offset=bass.IndirectOffsetOnAxis(ap=idx[s][:, j:j + 1], axis=0)).then_inc(S[f"{half}{s}"], 16)
                pool.wait_ge(S["set"], 2)
                nc.gpsimd.indirect_dma_start(out=headr[:, :], out_offset=None, in_=rec_dram,
                                             in_offset=bass.IndirectOffsetOnAxis(ap=headi[:, 0:1], axis=0)).then_inc(S["head_in"], 16)
                trips(pool, S, CHUNKS, 2, 0, 0, emit)
                pool.wait_ge(S["end"], 14)
                nc.gpsimd.indirect_dma_start(out=carry_dram, out_offset=bass.IndirectOffsetOnAxis(ap=headi[:, 1:2], axis=0),
                                             in_=carry[:, :], in_offset=None, bounds_check=M - 1, oob_is_err=False).then_inc(S["carried"], 16)
                pool.wait_ge(S["carried"], 16)

            @block.tensor
            def _(pe):
                pe.wait_ge(S["consts_in"], 16 * 9)

                def emit(p):
                    if p.has(0):
                        s = p.slot(0)
                        p.wait_slot("tin", 0)
                        for n in range(16):
                            h, m = n // 8, n % 8
                            if n < 4:
                                p.wait("hT", -1, 16, 13 + n)
                            else:
                                p.wait("hT", 0, 16, n - 3)
                            nt = (4 - h) * W
                            nc.tensor.matmul(p_h[n % 4][:, 0:nt], w1[:, P * m:P * (m + 1)], tT[s][:, 4 * W * h:4 * W * h + nt],
                                             start=True, stop=True).then_inc(S["hp"], 1)
                        for r in range(SROWS):
                            h = r // 4
                            bank = p_y[(s + r) % 2]
                            if r < 2:
                                p.wait("y", -1, SROWS, SROWS - 1 + r)
                            else:
                                p.wait("y", 0, SROWS, r - 1)
                            p.wait("hT", 0, 16, 8 * h + 8)
                            for x in range(EXPERTS):
                                for k in range(2):
                                    mm = nc.tensor.matmul(bank[:, x, :], hT[h][:, 2 * x + k, W * (r - 4 * h):W * (r - 4 * h + 1)], w2[:, 2 * x + k, :],
                                                          start=k == 0, stop=k == 1)
                            mm.then_inc(S["yp"], 1)
                trips(pe, S, CHUNKS, 2, 0, 0, emit)
                pe.wait_ge(S["end"], 2)
                for k in range(3):
                    mm = nc.tensor.transpose(p_e[:, k, :], ends[:, k, :], ident[:, :])
                mm.then_inc(S["endp"], 1)
                pe.wait_ge(S["end"], 12)
                for k, tile in enumerate((cm, cs)):
                    mm = nc.tensor.transpose(p_c[:, k, :], tile[:, 0:P], ident[0:20, 0:20])
                mm.then_inc(S["endp"], 1)

            @block.scalar
            def _(act):
                act.wait_ge(S["consts_in"], 16 * 9)

                def emit(p):
                    if p.has(-1):
                        s = p.slot(-1)
                        nc.scalar.preload_act_table_set("natural_log_exp_and_others")
                        p.wait("g", -1, NG, 7)
                        p.wait_slot("ro", -3)
                        nc.scalar.activation(ee[:, :, :, :], dd[:, :, :, :], ACT.Exp).then_inc(S["ee"], 1)
                        nc.scalar.activation(out[s][:, :, 0:GH], ms[s][:, :, 1:CH + 1].rearrange("p h j -> p j h"), ACT.Copy).then_inc(S["ee"], 1)
                    if p.has(0):
                        nc.scalar.preload_act_table(ACT.Gelu)
                        for n in range(16):
                            h, m = n // 8, n % 8
                            nt = (4 - h) * W
                            p.wait("hp", 0, 16, n + 1)
                            if m == 0:
                                p.wait("yp", -1, SROWS, 4 + 3 * h)
                            nc.scalar.activation(hT[h][:, m, :], p_h[n % 4][:, 0:nt], ACT.Gelu, bias=b1[:, m:m + 1]).then_inc(S["hT"], 1)
                trips(act, S, CHUNKS, 2, 0, 1, emit, peel=2)
                nc.scalar.preload_act_table_set("natural_log_exp_and_others")
                act.wait_ge(S["end"], 10)
                nc.scalar.activation(cd[:, :, :], cd[:, :, :], ACT.Exp).then_inc(S["cexp"], 1)

            @block.vector
            def _(v):
                nc.vector.memset(prior[:, :], -1.0)
                nc.vector.memset(after[:, :], -1.0).then_inc(S["set"], 1)
                v.wait_ge(S["consts_in"], 16 * 9)
                nc.vector.tensor_copy(headi[:, 0:1], heads[:, 0:1]).then_inc(S["set"], 1)
                nc.vector.tensor_tensor(flag[:, 0:1], heads[:, 0:1], prior[:, CH - 1:CH], ALU.is_equal)
                nc.vector.tensor_tensor(flag[:, 1:2], heads[:, 0:1], tails[:, CH - 1:CH], ALU.is_equal)
                nc.vector.tensor_tensor(flag[:, 2:3], tails[:, CH - 1:CH], after[:, 0:1], ALU.is_equal)
                nc.vector.tensor_scalar(flag[:, 4:5], heads[:, 0:1], float(IMG), None, ALU.is_ge)
                nc.vector.tensor_scalar(flag[:, 5:6], heads[:, 0:1], float(2 * IMG), None, ALU.is_ge)
                nc.vector.tensor_scalar(flag[:, 6:7], heads[:, 0:1], float(3 * IMG), None, ALU.is_ge).then_inc(S["set"], 1)
                v.wait_ge(S["set"], 3)
                nc.vector.tensor_tensor(flag[:, 3:4], flag[:, 0:1], flag[:, 1:2], ALU.mult)
                nc.vector.tensor_tensor(flag[:, 7:8], flag[:, 4:5], flag[:, 5:6], ALU.add).then_inc(S["set"], 1)
                v.wait_ge(S["set"], 4)
                nc.vector.tensor_tensor(flag[:, 4:5], flag[:, 7:8], flag[:, 6:7], ALU.add)
                nc.vector.tensor_tensor(flag[:, 5:6], flag[:, 2:3], flag[:, 1:2], ALU.mult).then_inc(S["set"], 1)
                v.wait_ge(S["set"], 5)
                nc.vector.scalar_tensor_tensor(flag[:, 6:7], flag[:, 5:6], 1.0, flag[:, 0:1], ALU.subtract, ALU.mult)
                nc.vector.scalar_tensor_tensor(flag[:, 7:8], flag[:, 4:5], float(-IMG), heads[:, 0:1], ALU.mult, ALU.add).then_inc(S["set"], 1)
                v.wait_ge(S["set"], 6)
                nc.vector.tensor_scalar(flag[:, 4:5], flag[:, 7:8], float(ROLL), float(IMG), ALU.is_lt, ALU.mult)
                nc.vector.tensor_scalar(flag[:, 5:6], flag[:, 6:7], NONE, NONE - ROLL, ALU.mult, ALU.add).then_inc(S["set"], 1)
                v.wait_ge(S["set"], 7)
                nc.vector.tensor_tensor(flag[:, 6:7], flag[:, 4:5], flag[:, 5:6], ALU.add).then_inc(S["set"], 1)
                v.wait_ge(S["set"], 8)
                nc.vector.tensor_tensor(headi[:, 1:2], flag[:, 6:7], heads[:, 0:1], ALU.add).then_inc(S["set"], 1)
                v.wait_ge(S["head_in"], 16)

                def emit(p):
                    if p.has(-1):
                        s = p.slot(-1)
                        o = 1 - s
                        first = isinstance(p.t, int) and p.t == 1

                        def so_far(k):
                            p.wait("g", -1, NG, k)

                        def before(tile):
                            return 0.0 if first else tile
                        p.wait_lot("ld", -1, 48)
                        p.wait_lot("ga", -1, CH // 2 * 16)
                        p.wait_lot("gb", -1, CH // 2 * 16)
                        if first:
                            nc.vector.memset(ms[o][:, :, CH], 0.0)
                            nc.vector.tensor_copy(start[s][:, 0, :], headr[:, FEAT + GH:REC])
                        nc.vector.tensor_scalar(pen[:, :], same[s][:, :], -LOW, LOW, ALU.mult, ALU.add).then_inc(S["g"], 1)
                        so_far(1)
                        for h in range(GH):
                            ins = nc.vector.tensor_tensor_scan(ad[s][:, h, :], same[s][:, :], start[s][:, :, h], before(ad[o][:, h, CH - 1:CH]), ALU.mult, ALU.add)
                        ins.then_inc(S["g"], 1)
                        so_far(2)
                        nc.vector.tensor_tensor(e[s][:, :, :], rec[s][:, :, FEAT:FEAT + GH].rearrange("p j h -> p h j"), ad[s][:, :, :], ALU.add).then_inc(S["g"], 1)
                        so_far(3)
                        nc.vector.scalar_tensor_tensor(e[s][:, :, :], e[s][:, :, :], 0.2, e[s][:, :, :], ALU.mult, ALU.max).then_inc(S["g"], 1)
                        so_far(4)
                        p.wait("ee", -3, 2)
                        nc.vector.tensor_copy(ms[s][:, :, 0], ms[o][:, :, CH])
                        for h in range(GH):
                            ins = nc.vector.tensor_tensor_scan(ms[s][:, h, 1:CH + 1], pen[:, :], e[s][:, h, :], before(ms[o][:, h, CH:CH + 1]), ALU.add, ALU.max)
                        ins.then_inc(S["g"], 1)
                        so_far(5)
                        nc.vector.tensor_tensor(dd[:, 0, :, :], ms[s][:, :, 0:CH], ms[s][:, :, 1:CH + 1], ALU.subtract)
                        nc.vector.tensor_tensor(dd[:, 1, :, :], e[s][:, :, :], ms[s][:, :, 1:CH + 1], ALU.subtract).then_inc(S["g"], 1)
                        so_far(6)
                        nc.vector.tensor_tensor(dd[:, 0, :, :], dd[:, 0, :, :], pen[:, :].rearrange("p (o j) -> p o j", o=1).to_broadcast([P, GH, CH]), ALU.add).then_inc(S["g"], 1)
                        p.wait("ee", -1, 2)
                        nc.vector.tensor_tensor(wt[:, :, :].rearrange("p (h x) j -> p h x j", h=GH),
                                                rec[s][:, :, 0:FEAT].rearrange("p j (h x) -> p h x j", h=GH),
                                                ee[:, 1, :, :].rearrange("p h (o j) -> p h o j", o=1).to_broadcast([P, GH, EXPERTS, CH]), ALU.mult).then_inc(S["g"], 1)
                        so_far(8)
                        p.wait_slot("ro", -3)
                        for h in range(GH):
                            ins = nc.vector.tensor_tensor_scan(out[s][:, :, GH + h], ee[:, 0, h, :], ee[:, 1, h, :], before(out[o][:, CH - 1, GH + h:GH + h + 1]), ALU.mult, ALU.add)
                        ins.then_inc(S["g"], 1)
                        for f in range(FEAT):
                            c = 2 * GH + f
                            ins = nc.vector.tensor_tensor_scan(out[s][:, :, c], ee[:, 0, f // EXPERTS, :], wt[:, f, :], before(out[o][:, CH - 1, c:c + 1]), ALU.mult, ALU.add)
                        ins.then_inc(S["g"], 1)
                        so_far(10)
                    if p.has(0):
                        s = p.slot(0)
                        p.wait_slot("yo", -2)
                        for r in range(SROWS):
                            p.wait("yp", 0, SROWS, r + 1)
                            nc.vector.tensor_tensor(y[s][:, r, :], p_y[(s + r) % 2][:, :, :].rearrange("p x c -> p (x c)"), b2[0:W, :], ALU.add).then_inc(S["y"], 1)
                trips(v, S, CHUNKS, 2, 0, 1, emit, peel=2)
                end = Steps(S["end"])

                def do(ins):
                    v.wait_ge(end.sem, end.done_by(ins))
                m = ms[1][:, :, CH:CH + 1]
                nc.vector.tensor_copy(ends[:, 0, 0:GH], ms[1][:, :, CH])
                nc.vector.tensor_copy(ends[:, 0, GH:20].rearrange("p (h x) -> p h x", h=GH), m.to_broadcast([P, GH, EXPERTS]))
                do(nc.vector.tensor_copy(ends[:, 1, :], out[1][:, CH - 1, GH:REC]))
                do(nc.vector.tensor_copy(ends[:, 2, :], flag[:, 3:4].to_broadcast([P, 20])))
                v.wait_ge(S["endp"], 1)
                do(nc.vector.tensor_copy(endT[:, :, :], p_e[:, :, :]))
                do(nc.vector.tensor_scalar(endT[:, 2, :], endT[:, 2, :], -LOW, LOW, ALU.mult, ALU.add))
                do(nc.vector.memset(cm[:, 0:1], LOW))
                do(nc.vector.memset(cs[:, 0:1], 0.0))
                do(nc.vector.tensor_tensor_scan(cm[:, 1:P + 1], endT[:, 2, :], endT[:, 0, :], 0.0, ALU.add, ALU.max))
                do(nc.vector.tensor_tensor(cd[:, 0, :], cm[:, 0:P], cm[:, 1:P + 1], ALU.subtract))
                do(nc.vector.tensor_tensor(cd[:, 1, :], endT[:, 0, :], cm[:, 1:P + 1], ALU.subtract))
                do(nc.vector.tensor_tensor(cd[:, 0, :], cd[:, 0, :], endT[:, 2, :], ALU.add))
                v.wait_ge(S["cexp"], 1)
                do(nc.vector.tensor_tensor(endT[:, 1, :], endT[:, 1, :], cd[:, 1, :], ALU.mult))
                do(nc.vector.tensor_tensor_scan(cs[:, 1:P + 1], cd[:, 0, :], endT[:, 1, :], 0.0, ALU.mult, ALU.add))
                v.wait_ge(S["endp"], 2)
                do(nc.vector.tensor_copy(carry[:, 0:GH], p_c[:, 0, 0:GH]))
                do(nc.vector.tensor_copy(carry[:, GH:REC], p_c[:, 1, :]))
        clear(nc, own.values())


FB = 14
FBLOCKS = NPP // FB
NF = 36


def combine(nc, d, end_dram, scan_dram, carry_dram, recs_dram, x3_dram, y_dram, out_dram):
    with ExitStack() as ctx:
        def sb(name, shape, dt=F32):
            return ctx.enter_context(nc.sbuf_tensor("cb_" + name, shape, dt))

        def two(name, shape, dt=F32):
            return [sb(f"{name}{i}", shape, dt) for i in range(2)]

        end = sb("end", [P, NPP], I32)
        low = sb("low", [P, FB, REC])
        cst = sb("cst", [P, 3, FEAT])
        order = sb("order", [P, 2, 4, 4])
        eps = sb("eps", [P, 1])
        x, y = two("x", [P, FB, C]), two("y", [P, FB, EXPERTS * C])
        a, b, r = (two(n, [P, FB, REC]) for n in ("a", "b", "r"))
        es = sb("es", [P, FB, GH])
        top = sb("top", [P, FB, GH])
        df = sb("df", [P, 3, FB, GH])
        ex = sb("ex", [P, 3, FB, GH])
        s0, s1 = (sb(n, [P, FB, GH]) for n in ("s0", "s1"))
        v0, v1, v2 = (sb(n, [P, FB, FEAT]) for n in ("v0", "v1", "v2"))
        mu, var, lnv, rstd, best, tot, rtot = (sb(n, [P, FB]) for n in ("mu", "var", "lnv", "rstd", "best", "tot", "rtot"))
        sc, rank, q, pq = (sb(n, [P, FB, EXPERTS]) for n in ("sc", "rank", "q", "pq"))
        c0, c1 = (sb(n, [P, FB, 16]) for n in ("c0", "c1"))
        prod = sb("prod", [P, 2, FB, C])
        gate = two("gate", [P, FB, EXPERTS])
        S = {n: ctx.enter_context(nc.semaphore("cb_" + n)) for n in (
            "consts_in", "set", "in0", "in1", "xy0", "xy1", "pre", "f", "sq", "act", "sum", "prod", "out0", "out1", "passed", "passed_sp")}
        S.update(zip(("ga0", "ga1"), d["soft"][11:13]))

        with nc.Block() as block:
            @block.sync
            def _(sp):
                for dst, src in ((end[:, :], end_dram), (cst[:, :, :], d["g_ln"]), (order[:, :, :, :], d["order"])):
                    sp.dma_start(dst, src).then_inc(S["consts_in"], 16)

                def emit(p):
                    if p.has(2):
                        s = p.slot(2)
                        p.wait("f", 0, NF)
                        cols = bass.ds((p.t + 2) * FB, FB)
                        for dst, src in ((b[s], carry_dram), (r[s], recs_dram)):
                            sp.dma_start(dst[:, :, :], src.rearrange("(p i) c -> p i c", p=P)[:, cols, :]).then_inc(S[f"in{s}"], 16)
                    if p.has(1):
                        s = p.slot(1)
                        p.wait("sum", -1, EXPERTS)
                        sp.sem_inc(S["passed_sp"], 1)
                        p.wait_slot("out", -1)
                        cols = bass.ds((p.t + 1) * FB, FB)
                        for dst, src in ((x[s], x3_dram), (y[s], y_dram)):
                            sp.dma_start(dst[:, :, :], src.rearrange("(p i) c -> p i c", p=P)[:, cols, :]).then_inc(S[f"xy{s}"], 16)
                    if p.has(0):
                        s = p.slot(0)
                        p.wait("sum", 0, EXPERTS)
                        sp.sem_inc(S["passed_sp"], 1)
                        sp.dma_start(out_dram.rearrange("(p i) c -> p i c", p=P)[:, bass.ds(p.t * FB, FB), :], x[s][:, :, :]).then_inc(S[f"out{s}"], 16)
                trips(sp, S, FBLOCKS, 2, 2, 0, emit)
                for s in range(2):
                    sp.wait_ge(S[f"out{s}"], 16 * (FBLOCKS // 2))

            @block.gpsimd
            def _(pool):
                idx = [sb(f"idx{i}", [P, FB], I32) for i in range(2)]
                copied = ctx.enter_context(nc.semaphore("cb_copied"))
                pool.wait_ge(S["consts_in"], 48)
                pool.wait_ge(S["set"], 1)

                def emit(p):
                    if p.has(0):
                        s = p.slot(0)
                        p.wait("f", -2, NF)
                        p.wait_lot("ga", -2, FB * 16)
                        pool.sem_inc(S["passed"], 1)
                        nc.gpsimd.tensor_copy(a[s][:, :, :], low[:, :, :])
                        nc.gpsimd.tensor_copy(idx[s][:, :], end[:, bass.ds(p.t * FB, FB)]).then_inc(copied, 1)
                        pool.wait_ge(copied, p.t + 1)
                        pool.sem_inc(S["passed"], 1)
                        for j in range(FB):
                            nc.gpsimd.indirect_dma_start(out=a[s][:, j, :], out_offset=None, in_=scan_dram,
                                                         in_offset=bass.IndirectOffsetOnAxis(ap=idx[s][:, j:j + 1], axis=0),
                                                         bounds_check=E - 1, oob_is_err=False).then_inc(S[f"ga{s}"], 16)
                trips(pool, S, FBLOCKS, 2, 0, 0, emit)

            @block.scalar
            def _(act):
                nc.scalar.preload_act_table_set("natural_log_exp_and_others")
                act.wait_ge(S["set"], 1)

                def product(p, k):
                    s, n = p.slot(0), EXPERTS - 2 + k
                    p.wait("f", 0, NF)
                    p.wait_lot("xy", 0, 32)
                    p.wait("sum", -1, EXPERTS, n + 1)
                    for j in range(FB):
                        ins = nc.scalar.activation(prod[:, k, j, :], y[s][:, j, C * n:C * (n + 1)], ACT.Copy, scale=gate[s][:, j, n:n + 1])
                    ins.then_inc(S["prod"], 1)

                def emit(p):
                    if p.u == 0:
                        nc.scalar.preload_act_table_set("natural_log_exp_and_others")
                    if p.has(1):
                        p.wait("f", 1, NF, 5)
                        nc.scalar.activation(ex[:, :, :, :], df[:, :, :, :], ACT.Exp).then_inc(S["act"], 1)
                    if p.has(0):
                        product(p, 0)
                    if p.has(1):
                        p.wait("f", 1, NF, 19)
                        nc.scalar.activation(lnv[:, :], var[:, :], ACT.Ln, bias=eps[:, 0:1], scale=1.0 / FEAT).then_inc(S["act"], 1)
                        p.wait("act", 1, 4, 2)
                        nc.scalar.activation(rstd[:, :], lnv[:, :], ACT.Exp, scale=-0.5).then_inc(S["act"], 1)
                    if p.has(0):
                        product(p, 1)
                    if p.has(1):
                        p.wait("f", 1, NF, 32)
                        nc.scalar.activation(q[:, :, :], q[:, :, :], ACT.Exp).then_inc(S["act"], 1)
                trips(act, S, FBLOCKS, 2, 1, 0, emit)

            @block.vector
            def _(v):
                nc.vector.memset(eps[:, :], 1e-5)
                nc.vector.memset(low[:, :, 0:GH], LOW)
                nc.vector.memset(low[:, :, GH:REC], 0.0).then_inc(S["set"], 1)
                v.wait_ge(S["consts_in"], 48)

                def wide(t, n):
                    return t.rearrange("p i (h o) -> p i h o", o=1).to_broadcast([P, FB, GH, n])

                def parts(t):
                    return t.rearrange("p i (h x) -> p i h x", h=GH)

                def row(k):
                    return cst[:, k:k + 1, :].to_broadcast([P, FB, FEAT])

                def per(t, n):
                    return t[:, :].rearrange("p (i o) -> p i o", o=1).to_broadcast([P, FB, n])

                def small(p):
                    s = p.slot(0)
                    k = [0]
                    A, Bc, R = a[s], b[s], r[s]
                    tt = nc.vector.tensor_tensor

                    def did(ins):
                        ins.then_inc(S["f"], 1)
                        k[0] += 1

                    def ready():
                        p.wait("f", 0, NF, k[0])
                    p.wait_lot("in", 0, 32)
                    p.wait_lot("ga", 0, FB * 16)
                    did(tt(es[:, :, :], R[:, :, FEAT:FEAT + GH], R[:, :, FEAT + GH:REC], ALU.add)); ready()
                    did(nc.vector.scalar_tensor_tensor(es[:, :, :], es[:, :, :], 0.2, es[:, :, :], ALU.mult, ALU.max))
                    did(tt(top[:, :, :], A[:, :, 0:GH], Bc[:, :, 0:GH], ALU.max)); ready()
                    did(tt(top[:, :, :], top[:, :, :], es[:, :, :], ALU.max)); ready()
                    tt(df[:, 0, :, :], A[:, :, 0:GH], top[:, :, :], ALU.subtract)
                    tt(df[:, 1, :, :], Bc[:, :, 0:GH], top[:, :, :], ALU.subtract)
                    did(tt(df[:, 2, :, :], es[:, :, :], top[:, :, :], ALU.subtract))
                    yield
                    p.wait("act", 0, 4, 1)
                    did(tt(s0[:, :, :], A[:, :, GH:2 * GH], ex[:, 0, :, :], ALU.mult))
                    did(tt(s1[:, :, :], Bc[:, :, GH:2 * GH], ex[:, 1, :, :], ALU.mult))
                    did(tt(parts(v0[:, :, :]), parts(A[:, :, 2 * GH:REC]), wide(ex[:, 0, :, :], 4), ALU.mult))
                    did(tt(parts(v1[:, :, :]), parts(Bc[:, :, 2 * GH:REC]), wide(ex[:, 1, :, :], 4), ALU.mult))
                    did(tt(parts(v2[:, :, :]), parts(R[:, :, 0:FEAT]), wide(ex[:, 2, :, :], 4), ALU.mult)); ready()
                    did(tt(s0[:, :, :], s0[:, :, :], s1[:, :, :], ALU.add))
                    did(tt(v0[:, :, :], v0[:, :, :], v1[:, :, :], ALU.add)); ready()
                    did(nc.vector.scalar_tensor_tensor(s1[:, :, :], s0[:, :, :], 1e-16, ex[:, 2, :, :], ALU.add, ALU.add))
                    did(tt(v1[:, :, :], v0[:, :, :], v2[:, :, :], ALU.add)); ready()
                    did(nc.vector.reciprocal(s0[:, :, :], s1[:, :, :])); ready()
                    did(tt(parts(v2[:, :, :]), parts(v1[:, :, :]), wide(s0[:, :, :], 4), ALU.mult)); ready()
                    did(tt(v0[:, :, :], v2[:, :, :], row(0), ALU.add)); ready()
                    yield
                    nc.vector.tensor_reduce(mu[:, :], v0[:, :, :], AX_X, ALU.add).then_inc(S["f"], 1)
                    k[0] += 1
                    ready()
                    nc.vector.scalar_tensor_tensor(v1[:, :, :], per(mu, FEAT), -1.0 / FEAT, v0[:, :, :], ALU.mult, ALU.add).then_inc(S["sq"], 1)
                    p.wait("sq", 0, 2, 1)
                    nc.vector.tensor_tensor(v2[:, :, :], v1[:, :, :], v1[:, :, :], ALU.mult).then_inc(S["sq"], 1)
                    p.wait("sq", 0, 2, 2)
                    did(nc.vector.tensor_reduce(var[:, :], v2[:, :, :], AX_X, ALU.add))
                    yield
                    p.wait("act", 0, 4, 3)
                    did(tt(v0[:, :, :], v1[:, :, :], per(rstd, FEAT), ALU.mult)); ready()
                    did(tt(v1[:, :, :], v0[:, :, :], row(1), ALU.mult)); ready()
                    did(tt(v2[:, :, :], v1[:, :, :], row(2), ALU.add)); ready()
                    did(nc.vector.tensor_reduce(pq[:, :, :], v2[:, :, :].rearrange("p i (h x) -> p i x h", h=GH), AX_X, ALU.add)); ready()
                    did(nc.vector.tensor_scalar(sc[:, :, :], pq[:, :, :], 1.0 / GH, None, ALU.mult)); ready()
                    mine = sc[:, :, :].rearrange("p i (e o) -> p i e o", o=1).to_broadcast([P, FB, 4, 4])
                    theirs = sc[:, :, :].rearrange("p i (o f) -> p i o f", o=1).to_broadcast([P, FB, 4, 4])

                    def mask(n):
                        return order[:, n, :, :].rearrange("p (o e) f -> p o (e f)", o=1).to_broadcast([P, FB, 16])
                    did(tt(parts(c0[:, :, :]), theirs, mine, ALU.is_ge))
                    did(tt(parts(c1[:, :, :]), theirs, mine, ALU.is_gt))
                    did(nc.vector.tensor_reduce(best[:, :], sc[:, :, :], AX_X, ALU.max)); ready()
                    did(tt(c0[:, :, :], c0[:, :, :], mask(0), ALU.mult))
                    did(tt(c1[:, :, :], c1[:, :, :], mask(1), ALU.mult))
                    did(tt(q[:, :, :], sc[:, :, :], per(best, EXPERTS), ALU.subtract)); ready()
                    did(tt(c0[:, :, :], c0[:, :, :], c1[:, :, :], ALU.add)); ready()
                    did(nc.vector.tensor_reduce(rank[:, :, :], parts(c0[:, :, :]), AX_X, ALU.add)); ready()
                    yield
                    p.wait("act", 0, 4, 4)
                    did(nc.vector.scalar_tensor_tensor(pq[:, :, :], rank[:, :, :], 1.5, q[:, :, :], ALU.is_le, ALU.mult)); ready()
                    did(nc.vector.tensor_reduce(tot[:, :], pq[:, :, :], AX_X, ALU.add)); ready()
                    did(nc.vector.reciprocal(rtot[:, :], tot[:, :])); ready()
                    did(tt(gate[s][:, :, :], pq[:, :, :], per(rtot, EXPERTS), ALU.mult)); ready()
                    assert k[0] == NF, k[0]

                def emit(p):
                    nxt = iter(())
                    if p.has(1):
                        nxt = small(p.next())
                    next(nxt, None)
                    for n in range(EXPERTS):
                        if p.has(0):
                            s = p.slot(0)
                            if n:
                                p.wait("sum", 0, EXPERTS, n)
                            else:
                                p.wait_lot("xy", 0, 32)
                            if n >= EXPERTS - 2:
                                k = n - (EXPERTS - 2)
                                p.wait("prod", 0, 2, k + 1)
                                ins = nc.vector.tensor_tensor(x[s][:, :, :], x[s][:, :, :], prod[:, k, :, :], ALU.add)
                            for j in range(FB if n < EXPERTS - 2 else 0):
                                ins = nc.vector.scalar_tensor_tensor(x[s][:, j, :], y[s][:, j, C * n:C * (n + 1)], gate[s][:, j, n:n + 1], x[s][:, j, :], ALU.mult, ALU.add)
                            ins.then_inc(S["sum"], 1)
                        next(nxt, None)
                    assert next(nxt, None) is None
                trips(v, S, FBLOCKS, 2, 1, 0, emit)
def shape_tables():
    coords = np.arange(1 - WIN, WIN, dtype=np.float32)
    tab = np.stack(np.meshgrid(coords, coords, indexing="ij"), axis=-1) * np.float32(8.0 / 7.0)
    tab = (np.sign(tab) * np.log1p(np.abs(tab)) / np.log(8.0)).reshape(-1, 2).astype(np.float32)
    head = np.arange(P) // HD
    region = np.repeat([1, 2], WIN - SHIFT)
    masks = np.zeros((P, 4, WIN * WIN), np.float32)
    for row in range(2):
        for col in range(2):
            for w in range(2):
                rr = region if row else np.zeros(WIN, int)
                cc = region if col and w else np.zeros(WIN, int)
                reg = (rr[:, None] * 3 + cc[None, :]).reshape(-1)
                masks[64 * w:64 * w + 64, row * 2 + col] = np.where(reg[:, None] == reg[None, :], 0.0, -100.0)
    return {
        "ident": np.eye(P, dtype=np.float32),
        "rel_tab": np.ascontiguousarray(tab[::-1].T),
        "masks": masks,
        "same_head": (head[:, None] == head[None, :]).astype(np.float32),
        "row_signs": row_signs(),
        "head_parity": np.stack([head % 2 == 0, head % 2 == 1], 1).astype(np.float32),
    }


def windows(x):
    x = np.roll(x, (-SHIFT, -SHIFT), axis=(1, 2))
    x = x.reshape(B, SPI, WIN, PPS, 2, WIN, C).transpose(0, 1, 4, 2, 5, 3, 6)
    return np.ascontiguousarray(x.reshape(STRIPS, P, PPS, C))


def expert_order():
    e = np.arange(EXPERTS)
    return np.ascontiguousarray(np.broadcast_to(np.stack([e[None, :] < e[:, None], e[None, :] > e[:, None]]), (P, 2, 4, 4))).astype(np.float32)


def metaformer(nc, d, out_dram):
    def dram(name, shape, dt=F32):
        return nc.dram_tensor(name, shape, dt, kind="Internal").ap()

    src, dst, same, first = dram("src", (E,), I32), dram("dst", (E,)), dram("same", (E,)), dram("first", (P, EP // BLK))
    rowptr, rowptrs = dram("rowptr", (M + 1,)), dram("rowptrs", (2, M))
    start, end = dram("start", (P, NPP), I32), dram("end", (P, NPP), I32)
    adst, carry, scan = dram("adst", (E, GH)), dram("carry", (M, REC)), dram("scan", (E, REC))
    tables = {"bt": dram("bt", (HEADS, (2 * WIN - 1) ** 2)), "bias": dram("bias", (WIN * WIN, 512)), "bm": dram("bm", (4, P, 512))}
    x1, x2, x3 = dram("x1", (STRIPS, P, PPS, C)), dram("x2", (STRIPS, W, WIN, C)), dram("x3", (M, C))
    tT, rec, recs, y = dram("tT", (P, M)), dram("rec", (M, REC)), dram("recs", (M, REC)), dram("y", (M, EXPERTS * C))

    d = {**d, "soft": [nc.alloc_semaphore(f"soft{k}") for k in range(15)]}
    with ExitStack() as ctx:
        sort_edges(nc, d["edges"], d["row_signs"], d["ident"], src, dst, same, first, Bias(nc, ctx, d, tables))
    with ExitStack() as ctx:
        score = ctx.enter_context(nc.sbuf_tensor("score", [P, PAIRS], F32))
        gate = ctx.enter_context(nc.sbuf_tensor("gate", [P, PAIRS], F32))
        stats = ctx.enter_context(nc.sbuf_tensor("stats", [P, PAIRS, 2], F32))
        with ExitStack() as inner:
            search = Search(nc, inner, d, dst, first)
            search.load()
            attention(nc, d, tables, x1, score, stats, search)
            select_tokens(nc, d, score, gate, Spans(nc, inner, search.rp, rowptr, rowptrs, start, end, adst, carry))
        pixels = ctx.enter_context(nc.sbuf_tensor("pixels", [P, B * PADW, PADW], BF16))
        routed_ffn(nc, d, x1, x2, stats, gate, pixels)
        convolve(nc, d, pixels, x2, x3, tT, rec, recs, start, adst)
    graph_and_experts(nc, d, src, dst, same, first, rec, adst, tT, scan, carry, y)
    combine(nc, d, end, scan, carry, recs, x3, y, out_dram)


def kernel(**inputs):
    import concourse.bacc as bacc
    from concourse.bass_utils import run_bass_kernel_spmd

    i = {name: np.asarray(a) for name, a in inputs.items()}

    def spread(a):
        return np.ascontiguousarray(np.broadcast_to(a, (P, *a.shape)))

    def hidden(a, n):
        return np.ascontiguousarray(a.reshape(n, P).T)

    raster = np.broadcast_to(np.arange(H * W, dtype=np.float32).reshape(1, H, W, 1), (B, H, W, C))
    shapes = shape_tables()
    consts = np.zeros((P, 8), np.float32)
    consts[:, 0] = i["L0_conv_q_bias"]
    consts[:, 1] = np.repeat(i["L0_conv_scale"].reshape(-1), HD)
    consts[:, 2:4] = shapes["head_parity"]
    consts[:, 4] = i["L0_ffn_br"][0]
    consts[:, 5] = i["L0_conv_v_bias"]
    arrays = {
        **{name: shapes[name] for name in ("ident", "rel_tab", "masks", "same_head", "row_signs")},
        "node_ids": node_ids(),
        "order": expert_order(),
        "raster": np.ascontiguousarray(windows(raster)[..., 0].transpose(1, 0, 2).reshape(P, PAIRS)),
        "x_win": windows(i["x"]),
        "consts": consts,
        "w_qkv": i["L0_conv_w_qkv"],
        "w_proj": i["L0_conv_w_proj"],
        "b_proj": i["L0_conv_b_proj"][None],
        "cpb_w1": i["L0_conv_cpb_w1"],
        "cpb_b1": hidden(i["L0_conv_cpb_b1"], 2),
        "cpb_w2": i["L0_conv_cpb_w2"].reshape(2, P, HEADS).transpose(1, 0, 2),
        "wr": spread(i["L0_ffn_wr"][:, 0]),
        "f_w1": i["L0_ffn_w1"],
        "f_w2": i["L0_ffn_w2"].reshape(4, P, C).transpose(1, 0, 2),
        "f_b1": hidden(i["L0_ffn_b1"], 4),
        "f_b2": i["L0_ffn_b2"][None],
        "c_w": i["L1_conv_w"].reshape(TAPS, C, C),
        "g_wgat": i["L1_ffn_W_gat"],
        "g_att": spread(np.stack([i["L1_ffn_att_src"].reshape(-1), i["L1_ffn_att_dst"].reshape(-1)])),
        "g_w1": i["L1_ffn_W1"].transpose(1, 0, 2).reshape(C, EXPERTS * EH),
        "g_w2": i["L1_ffn_W2"].reshape(2 * EXPERTS, P, C).transpose(1, 0, 2),
        "g_b1": hidden(i["L1_ffn_b1"], 2 * EXPERTS),
        "g_b2": spread(i["L1_ffn_b2"].reshape(-1)),
        "g_ln": spread(np.stack([i["L1_ffn_b_gat"], i["L1_ffn_ln_gamma"], i["L1_ffn_ln_beta"]])),
        "edges": i["L1_ffn_edge_index"],
    }
    arrays = {f"in_{name}": np.ascontiguousarray(a) for name, a in arrays.items()}
    nc = bacc.Bacc("TRN2", target_bir_lowering=False, num_devices=1)
    d = {name[3:]: nc.dram_tensor(name, a.shape, mybir.dt.from_np(a.dtype), kind="ExternalInput").ap()
         for name, a in arrays.items()}
    out = nc.dram_tensor("out", (M, C), F32, kind="ExternalOutput").ap()
    metaformer(nc, d, out)
    r = run_bass_kernel_spmd(nc, [arrays], core_ids=[0])
    return np.roll(r.results[0]["out"].reshape(B, H, W, C), SHIFT, axis=1)
```
